# Optimizing a Trainium2 kernel written in Bass

```python
import numpy as np
import jax
import jax.numpy as jnp

def _softmax(x, axis=-1):
    return jax.nn.softmax(x, axis=axis)

def _gelu(x):
    return jax.nn.gelu(x, approximate=True)

def _silu(x):
    return jax.nn.silu(x)

def _sigmoid(x):
    return jax.nn.sigmoid(x)

def _layernorm(x, axis=-1, eps=1e-05):
    m = jnp.mean(x, axis=axis, keepdims=True)
    v = jnp.var(x, axis=axis, keepdims=True)
    return (x - m) / jnp.sqrt(v + eps)

def _scatter_add(tgt, idx, src, axis=0):
    return tgt.at[idx].add(src)

def _segment_sum(src, seg, n):
    return jax.ops.segment_sum(src, seg, n)
kernel_name = 'mk_gnn_resnorm_d4_gnn_r64_a272b0'

def setup_inputs(seed: int=0):
    np.random.seed(seed)
    _w = jnp.asarray

    def _rec_inputs():
        import jax
        import jax.numpy as jnp
        _gk = jax.random.key(seed)
        x = -0.0001006 + 1 * jax.random.normal(jax.random.fold_in(_gk, 1), (100000, 48), jnp.float32)
        src = jax.random.randint(jax.random.fold_in(_gk, 2), (50000,), 0, 100000, jnp.int32)
        dst = jax.random.randint(jax.random.fold_in(_gk, 3), (50000,), 0, 100000, jnp.int32)
        _o = jnp.argsort(dst, stable=True)
        src = src[_o]
        dst = dst[_o]
        edge_attr_48 = -4.21973e-05 + 0.999841 * jax.random.normal(jax.random.fold_in(_gk, 12), (50000, 48), jnp.float32)
        edge_type_8 = jax.random.randint(jax.random.fold_in(_gk, 13), (50000,), 0, 8, jnp.int32)
        edge_weight = jax.random.uniform(jax.random.fold_in(_gk, 14), (50000,), jnp.float32, 0.0, 1)
        edge_weight1 = jax.random.uniform(jax.random.fold_in(_gk, 15), (50000, 1), jnp.float32, 0.0, 1)
        return (x, src, dst, edge_attr_48, edge_type_8, edge_weight, edge_weight1)
    x, src, dst, edge_attr_48, edge_type_8, edge_weight, edge_weight1 = _rec_inputs()

    def _L0_gnn_setup():
        import jax, jax.numpy as jnp
        import numpy as np
        N_NODES = 100000
        N_EDGES = 25000
        D_FEAT = 48
        key = jax.random.key(seed)
        k1, k2, k3, k4 = jax.random.split(key, 4)
        node_feat = jax.random.normal(k1, (N_NODES, D_FEAT), dtype=jnp.float32)
        edge_feat = jax.random.normal(k2, (N_EDGES, D_FEAT), dtype=jnp.float32)
        src = jax.random.randint(k3, (N_EDGES,), 0, N_NODES, dtype=jnp.int32)
        dst = jax.random.randint(k4, (N_EDGES,), 0, N_NODES, dtype=jnp.int32)
        eps = jnp.zeros((1,), dtype=jnp.float32)
        return {'node_feat': node_feat, 'edge_feat': edge_feat, 'src': src, 'dst': dst, 'eps': eps}
    _L0_gnn_all = _L0_gnn_setup()
    _L0_gnn_in = {k: v for k, v in _L0_gnn_all.items() if k in ('eps',)}
    del _L0_gnn_all

    def _L1_gnn_setup():
        import jax, jax.numpy as jnp
        import numpy as np
        K = 10
        ALPHA = 0.1
        N_NODES = 100000
        N_EDGES = 25000
        D_FEAT = 48
        key = jax.random.key(seed)
        k1, k2, k3, k4 = jax.random.split(key, 4)
        feat = jax.random.normal(k1, (N_NODES, D_FEAT), dtype=jnp.float32)
        edge_weight = jax.random.uniform(k2, (N_EDGES,), dtype=jnp.float32)
        src = jax.random.randint(k3, (N_EDGES,), 0, N_NODES, dtype=jnp.int32)
        dst = jax.random.randint(k4, (N_EDGES,), 0, N_NODES, dtype=jnp.int32)
        return {'feat': feat, 'edge_weight': edge_weight, 'src': src, 'dst': dst}
    _L1_gnn_all = _L1_gnn_setup()
    _L1_gnn_in = {k: v for k, v in _L1_gnn_all.items() if k in ()}
    del _L1_gnn_all

    def _L2_gnn_setup():
        import jax, jax.numpy as jnp
        import numpy as np
        N_NODES = 50000
        N_EDGES = 25000
        IN_FEAT = 48
        OUT_FEAT = 48
        NUM_RELS = 8
        key = jax.random.key(seed)
        ks = jax.random.split(key, 9)
        s1 = float(np.sqrt(2.0) * np.sqrt(6.0 / (IN_FEAT + IN_FEAT)))
        s2 = float(np.sqrt(2.0) * np.sqrt(6.0 / (IN_FEAT + OUT_FEAT)))
        return {'inputs': jax.random.normal(ks[0], (N_NODES, IN_FEAT), dtype=jnp.float32), 'norm': jax.random.uniform(ks[1], (N_EDGES, 1), dtype=jnp.float32), 'weight1': jax.random.uniform(ks[2], (NUM_RELS, IN_FEAT, IN_FEAT), jnp.float32, -s1, s1), 'weight2': jax.random.uniform(ks[3], (NUM_RELS, IN_FEAT, OUT_FEAT), jnp.float32, -s2, s2), 'bias1': jax.random.normal(ks[4], (IN_FEAT,), dtype=jnp.float32) * 0.1, 'bias2': jax.random.normal(ks[5], (OUT_FEAT,), dtype=jnp.float32) * 0.1, 'src': jax.random.randint(ks[6], (N_EDGES,), 0, N_NODES, dtype=jnp.int64) if jax.config.jax_enable_x64 else jax.random.randint(ks[6], (N_EDGES,), 0, N_NODES).astype(jnp.int32), 'dst': jax.random.randint(ks[7], (N_EDGES,), 0, N_NODES).astype(jnp.int32), 'rel_type': jax.random.randint(ks[8], (N_EDGES,), 0, NUM_RELS).astype(jnp.int32)}
    _L2_gnn_all = _L2_gnn_setup()
    _L2_gnn_in = {k: v for k, v in _L2_gnn_all.items() if k in ('weight1', 'weight2', 'bias1', 'bias2')}
    del _L2_gnn_all

    def _L3_gnn_setup():
        import jax, jax.numpy as jnp
        import numpy as np
        N_NODES = 100000
        N_EDGES = 25000
        IN_FEAT = 48
        OUT_FEAT = 48
        key = jax.random.key(seed)
        k_h, k_src, k_dst, k_tw, k_tb, k_pw, k_pb = jax.random.split(key, 7)
        lim = 1.0 / np.sqrt(IN_FEAT)
        return {'h': jax.random.normal(k_h, (N_NODES, IN_FEAT), dtype=jnp.float32), 'theta_w': jax.random.uniform(k_tw, (OUT_FEAT, IN_FEAT), jnp.float32, -lim, lim), 'theta_b': jax.random.uniform(k_tb, (OUT_FEAT,), jnp.float32, -lim, lim), 'phi_w': jax.random.uniform(k_pw, (OUT_FEAT, IN_FEAT), jnp.float32, -lim, lim), 'phi_b': jax.random.uniform(k_pb, (OUT_FEAT,), jnp.float32, -lim, lim), 'src': jax.random.randint(k_src, (N_EDGES,), 0, N_NODES, dtype=jnp.int64), 'dst': jax.random.randint(k_dst, (N_EDGES,), 0, N_NODES, dtype=jnp.int64)}
    _L3_gnn_all = _L3_gnn_setup()
    _L3_gnn_in = {k: v for k, v in _L3_gnn_all.items() if k in ('theta_w', 'theta_b', 'phi_w', 'phi_b')}
    del _L3_gnn_all
    return {'x': x, 'src': src, 'dst': dst, 'edge_attr_48': edge_attr_48, 'edge_type_8': edge_type_8, 'edge_weight': edge_weight, 'edge_weight1': edge_weight1, 'L0_gnn_eps': _L0_gnn_in['eps'], 'L2_gnn_weight1': _L2_gnn_in['weight1'], 'L2_gnn_weight2': _L2_gnn_in['weight2'], 'L2_gnn_bias1': _L2_gnn_in['bias1'], 'L2_gnn_bias2': _L2_gnn_in['bias2'], 'L3_gnn_theta_w': _L3_gnn_in['theta_w'], 'L3_gnn_theta_b': _L3_gnn_in['theta_b'], 'L3_gnn_phi_w': _L3_gnn_in['phi_w'], 'L3_gnn_phi_b': _L3_gnn_in['phi_b']}

def reference(x, src, dst, edge_attr_48, edge_type_8, edge_weight, edge_weight1, L0_gnn_eps, L2_gnn_weight1, L2_gnn_weight2, L2_gnn_bias1, L2_gnn_bias2, L3_gnn_theta_w, L3_gnn_theta_b, L3_gnn_phi_w, L3_gnn_phi_b):
    import jax
    import jax.numpy as jnp

    def _L0_gnn_ref(node_feat, edge_feat, src, dst, eps):
        import jax, jax.numpy as jnp
        import numpy as np
        N_NODES = 100000
        N_EDGES = 25000
        D_FEAT = 48
        m = jax.nn.relu(node_feat[src] + edge_feat)
        neigh = jax.ops.segment_sum(m, dst, num_segments=N_NODES)
        return (1.0 + eps[0]) * node_feat + neigh

    def _L1_gnn_ref(feat, edge_weight, src, dst):
        import jax, jax.numpy as jnp
        import numpy as np
        K = 10
        ALPHA = 0.1
        N_NODES = 100000
        N_EDGES = 25000
        D_FEAT = 48
        n = feat.shape[0]
        feat_0 = feat

        def step(f, _):
            msg = f[src] * edge_weight[:, None]
            agg = jax.ops.segment_sum(msg, dst, num_segments=n)
            f = (1.0 - ALPHA) * agg + ALPHA * feat_0
            return (f, None)
        out, _ = jax.lax.scan(step, feat, None, length=K)
        return out

    def _L2_gnn_ref(inputs, norm, weight1, weight2, bias1, bias2, src, dst, rel_type):
        import jax, jax.numpy as jnp
        import numpy as np
        N_NODES = 50000
        N_EDGES = 25000
        IN_FEAT = 48
        OUT_FEAT = 48
        NUM_RELS = 8
        h1 = jax.nn.relu(jnp.einsum('ni,rij->nrj', inputs, weight1) + bias1)
        h2 = jnp.einsum('nrj,rjo->nro', h1, weight2)
        msg = h2[src, rel_type] * norm
        agg = jax.ops.segment_sum(msg, dst, num_segments=inputs.shape[0])
        return jax.nn.relu(agg + bias2)

    def _L3_gnn_ref(h, theta_w, theta_b, phi_w, phi_b, src, dst):
        import jax, jax.numpy as jnp
        import numpy as np
        N_NODES = 100000
        N_EDGES = 25000
        IN_FEAT = 48
        OUT_FEAT = 48
        phi_all = h @ phi_w.T + phi_b
        diff = h[dst] - h[src]
        e = diff @ theta_w.T + theta_b + phi_all[src]
        out = jax.ops.segment_max(e, dst, num_segments=N_NODES)
        out = jnp.where(jnp.isneginf(out), 0.0, out)
        return out
    x = _layernorm(x + _L0_gnn_ref(x, edge_attr_48, src, dst, L0_gnn_eps), axis=-1)
    x = _layernorm(x + _L1_gnn_ref(x, edge_weight, src, dst), axis=-1)
    x = _layernorm(x + _L2_gnn_ref(x, edge_weight1, L2_gnn_weight1, L2_gnn_weight2, L2_gnn_bias1, L2_gnn_bias2, src, dst, edge_type_8), axis=-1)
    x = _layernorm(x + _L3_gnn_ref(x, L3_gnn_theta_w, L3_gnn_theta_b, L3_gnn_phi_w, L3_gnn_phi_b, src, dst), axis=-1)
    return x

_drawn_inputs = setup_inputs


def setup_inputs(seed=0):
    import zlib

    import numpy as np

    out = dict(_drawn_inputs(seed))
    spreads = {}
    factors = {'edge_weight': 3.487, 'L2_gnn_bias1': 2.819}
    for name, (base, spread) in spreads.items():
        noise = np.random.default_rng([zlib.crc32(name.encode()), seed]).standard_normal(out[name].shape)
        drawn = base * np.exp(spread * noise) if base else spread * noise
        out[name] = jnp.asarray(drawn.astype(out[name].dtype))
    for name, factor in factors.items():
        out[name] = (out[name] * factor).astype(out[name].dtype)
    return out
```

```python
import concourse.bass as bass
from concourse import mybir
from contextlib import ExitStack

F32, I32 = mybir.dt.float32, mybir.dt.int32
ALU, ACT, AX = mybir.AluOpType, mybir.ActivationFunctionType, mybir.AxisListType

N, E, F, R = 100000, 50000, 48, 8
P, T = 128, 4
GE = P * T
NG = -(-E // GE)
EP = NG * GE
NC = (NG + 1) * T
NI = NG // 2
RC = R * F // P
XW = F + 1
ROWS, CHUNKS = 39, 20
REST = N - P * ROWS * CHUNKS
RP, RR = 32, REST // 32
LN_EPS, ALPHA, STEPS = 1e-5, 0.1, 10
FAR = float(1 << 23)
LOW = 3.0e38


def wait(eng, sem, value):
    if not isinstance(value, int) or value > 0:
        eng.wait_ge(sem, value)


class Chain:

    def __init__(self, eng, sem, per):
        self.eng, self.sem, self.per = eng, sem, per

    def turn(self, n):
        self.base, self.count = n * self.per, 0
        return self

    def then(self, ins):
        ins.then_inc(self.sem, 1)
        self.count += 1
        assert self.count <= self.per
        self.eng.wait_ge(self.sem, self.base + self.count)

    def last(self):
        assert self.count == self.per, (self.count, self.per)


def mid(ap, rows):
    return ap.unsqueeze(2).to_broadcast([ap.shape[0], rows, F])


def gnn(nc, a, out):
    ctx = ExitStack()
    with ctx:
        def sb(name, shape, dt=F32):
            return ctx.enter_context(nc.sbuf_tensor(name, shape, dt))

        def pair(name, shape, dt=F32):
            return [sb(f"{name}{b}", shape, dt) for b in range(2)]

        def sem(name):
            return ctx.enter_context(nc.semaphore(name))

        def sems(name):
            return [sem(f"{name}{b}") for b in range(2)]

        def dram(name, shape, dt=F32):
            return nc.dram_tensor(name, shape, dt, kind="Internal").ap()

        xpos = dram("xpos", (N, XW))
        layer = {k: dram(f"layer{k}", (2 * EP, F)) for k in (1, 2, 3)}
        krylov = [dram(f"krylov{b}", (EP + 1, F)) for b in range(2)]
        rows_dram = dram("rows_dram", (2, EP))

        ident = sb("ident", [P, P])
        rel = sb("rel", [P, RC])
        bias1 = sb("bias1", [P, RC])
        bias2 = sb("bias2", [P, F])
        bias2r = sb("bias2r", [P, F])
        bias3 = sb("bias3", [P, F])
        phb = sb("phb", [P, F])
        w1 = sb("w1", [F, R * F])
        w2 = sb("w2", [P, RC, F])
        theta = sb("theta", [F, F])
        phi = sb("phi", [F, F])
        pmt = sb("pmt", [F, F])
        eps0 = sb("eps0", [P, 1])
        c = sb("c", [P, 1])
        c2 = sb("c2", [P, 1])
        lneps = sb("lneps", [P, 1])
        neg1 = sb("neg1", [P, ROWS])
        zrow = sb("zrow", [1, F])
        src = sb("src", [P, NC], I32)
        dst = sb("dst", [P, NC], I32)
        nxt = sb("nxt", [P, NC], I32)
        dstc = sb("dstc", [P, NC], I32)
        posi = sb("posi", [P, NC], I32)
        outi = sb("outi", [P, NC], I32)
        idx2 = sb("idx2", [P, NC], I32)
        idxk = sb("idxk", [P, NC], I32)
        ei = sb("ei", [P, NC], I32)
        ef = sb("ef", [P, NC])
        posf = sb("posf", [P, NC])
        w9 = sb("w9", [P, NC])
        t1 = sb("t1", [P, NC])
        t2 = sb("t2", [P, NC])
        XD = sb("XD", [P, NG * T * F])

        def xd(g):
            return XD[:, bass.ds(g * (T * F), T * F)].rearrange("p (t f) -> p t f", f=F)

        def col(ap, g):
            return ap[:, bass.ds(g * T, T)]

        def rows(table, g, base=0):
            return table[bass.ds(g * GE + base, GE), :].rearrange("(p t) f -> p (t f)", t=T)

        def centre(dc, y, d, q, m, u, n):
            dc.then(nc.vector.tensor_reduce(m, y, AX.X, ALU.add))
            dc.then(nc.vector.tensor_scalar(m, m, 1.0 / F, None, ALU.mult))
            dc.then(nc.vector.tensor_tensor(d, y, mid(m, n), ALU.subtract))
            dc.then(nc.vector.tensor_tensor(q, d, d, ALU.mult))
            dc.then(nc.vector.tensor_reduce(u, q, AX.X, ALU.add))

        def lone_source(dve, dc, s_var, s_std, k, x, d, q, m, u, r, v, s, p, n, x1=None, x2=None):
            centre(dc, x, d, q, m, u, n)
            dc.then(nc.vector.tensor_scalar(u, u, c2[0:p, :], None, ALU.mult))
            nc.vector.tensor_copy(v, u).then_inc(s_var, 1)
            dve.wait_ge(s_std, k + 1)
            dc.then(nc.vector.reciprocal(r, s))
            dc.then(nc.vector.tensor_tensor(u, u, r, ALU.mult))
            dc.then(nc.vector.tensor_tensor(u, u, r, ALU.mult))
            nc.vector.tensor_scalar(v, u, (1 + ALPHA) ** 2, None, ALU.mult).then_inc(s_var, 1)
            dc.then(nc.vector.tensor_scalar(r, r, c[0:p, :], None, ALU.mult))
            if x1 is not None:
                nc.vector.tensor_tensor(x1, d, mid(r, n), ALU.mult)
            dve.wait_ge(s_std, k + 2)
            dc.then(nc.vector.reciprocal(u, s))
            dc.then(nc.vector.scalar_tensor_tensor(out=r, in0=u, scalar=1 + ALPHA, in1=r, op0=ALU.mult, op1=ALU.mult))
            x2 = d if x2 is None else x2
            dc.then(nc.vector.tensor_tensor(x2, d, mid(r, n), ALU.mult))
            dc.then(nc.vector.tensor_tensor(q, x2, bias2r[0:p, :].unsqueeze(1).to_broadcast([p, n, F]), ALU.add))
            dc.then(nc.vector.tensor_reduce(m, q, AX.X, ALU.add))
            dc.then(nc.vector.tensor_scalar(m, m, 1.0 / F, None, ALU.mult))
            dc.then(nc.vector.tensor_tensor(d, q, mid(m, n), ALU.subtract))
            dc.then(nc.vector.tensor_tensor(q, d, d, ALU.mult))
            dc.then(nc.vector.tensor_reduce(u, q, AX.X, ALU.add))
            nc.vector.tensor_scalar(v, u, 1.0 / F, None, ALU.mult).then_inc(s_var, 1)
            dve.wait_ge(s_std, k + 3)
            dc.then(nc.vector.reciprocal(r, s))

        with ExitStack() as scope:
            xin = [scope.enter_context(nc.sbuf_tensor(f"xin{b}", [P, ROWS, XW], F32)) for b in range(2)]
            dr = scope.enter_context(nc.sbuf_tensor("dr", [NG, GE], I32))
            dp = scope.enter_context(nc.sbuf_tensor("dp", [NG, GE], I32))
            keepr = scope.enter_context(nc.sbuf_tensor("keepr", [NG, GE], F32))
            penr = scope.enter_context(nc.sbuf_tensor("penr", [NG, GE], F32))
            s_const, s_col, s_chain, s_ei, s_keep = (sem(n) for n in ("s_const", "s_col", "s_chain", "s_ei", "s_keep"))
            s_neg, s_rows, s_zero, s_relu = sem("s_neg"), sem("s_rows"), sem("s_zero"), sem("s_relu")
            s_xin, s_xout = sems("s_xin"), sems("s_xout")
            xv = a["x"][0:P * ROWS * CHUNKS, :].rearrange("(p c r) f -> p c r f", p=P, c=CHUNKS)
            pv = xpos[0:P * ROWS * CHUNKS, :].rearrange("(p c r) f -> p c (r f)", p=P, c=CHUNKS)
            consts = [(ident, "ident"), (rel, "rel"), (bias1, "bias1"), (w1, "w1"), (w2, "w2"),
                      (theta, "thetaT"), (phi, "phiT")]
            wide = [(bias2, "bias2"), (bias3, "theta_b"), (phb, "phi_b"), (eps0, "eps")]
            cols = [(src, "src"), (dst, "dst"), (nxt, "nxt"), (w9, "ew")]
            with nc.Block() as block:
                @block.sync
                def _(sp):
                    for t, n in cols:
                        sp.dma_start(t[:, :], a[n]).then_inc(s_col, 16)
                    sp.dma_start(dr[:, :], a["dst_row"][1:EP + 1].rearrange("(g e) -> g e", e=GE)).then_inc(s_col, 16)
                    sp.dma_start(dp[:, :], a["dst_row"][0:EP].rearrange("(g e) -> g e", e=GE)).then_inc(s_col, 16)
                    for t, n in consts:
                        sp.dma_start(t[:], a[n]).then_inc(s_const, 16)
                    for t, n in wide:
                        sp.dma_start(t[:, :], a[n].partition_broadcast(P)).then_inc(s_const, 16)

                    def load(i, b):
                        wait(sp, s_xout[b], i * 16)
                        sp.dma_start(xin[b][:, :, 0:F], xv[:, bass.ds(i * 2 + b, 1)].rearrange("p c r f -> p (c r) f")).then_inc(s_xin[b], 16)

                    for b in range(2):
                        load(0, b)
                    with sp.Fori(1, CHUNKS // 2) as i:
                        for b in range(2):
                            load(i, b)
                    sp.wait_ge(s_xout[0], 16 * CHUNKS // 2)
                    sp.dma_start(xin[0][0:RP, 0:RR, 0:F], a["x"][N - REST:N, :].rearrange("(p r) f -> p r f", p=RP)).then_inc(s_xin[0], 16)
                    sp.wait_ge(s_keep, 1)
                    sp.dma_start(rows_dram[0:1, :].rearrange("o (g e) -> (o g) e", e=GE), keepr[:, :]).then_inc(s_rows, 16)
                    sp.dma_start(rows_dram[1:2, :].rearrange("o (g e) -> (o g) e", e=GE), penr[:, :]).then_inc(s_rows, 16)
                    sp.wait_ge(s_zero, 1)
                    for k in krylov:
                        sp.dma_start(k[EP:EP + 1, :], zrow[:, :]).then_inc(s_rows, 16)
                    sp.wait_ge(s_rows, 64)
                    sp.wait_ge(s_const, 16 * (len(consts) + len(wide)))

                @block.scalar
                def _(act):
                    act.wait_ge(s_neg, 1)

                    def store(i, b):
                        act.wait_ge(s_xin[b], i * 16 + 16)
                        act.dma_start(pv[:, bass.ds(i * 2 + b, 1)].rearrange("p c w -> p (c w)"), xin[b][:, :, :].rearrange("p r w -> p (r w)")).then_inc(s_xout[b], 16)

                    with act.Fori(0, CHUNKS // 2) as i:
                        for b in range(2):
                            store(i, b)
                    act.wait_ge(s_xin[0], 16 * CHUNKS // 2 + 16)
                    act.dma_start(xpos[N - REST:N, :].rearrange("(p r) w -> p (r w)", p=RP), xin[0][0:RP, 0:RR, :].rearrange("p r w -> p (r w)")).then_inc(s_xout[0], 16)
                    act.wait_ge(s_xout[0], 16 * CHUNKS // 2 + 16)
                    act.wait_ge(s_xout[1], 16 * CHUNKS // 2)

                @block.gpsimd
                def _(pool):
                    nc.gpsimd.iota(ei[:, :], pattern=[[GE, NG + 1], [1, T]], base=0, channel_multiplier=T).then_inc(s_ei, 1)

                @block.vector
                def _(dve):
                    dc = Chain(dve, s_chain, 10).turn(0)
                    for b in range(2):
                        ins = nc.vector.memset(xin[b][:, :, F:XW], -1.0)
                    ins.then_inc(s_neg, 1)
                    nc.vector.memset(lneps[:, :], LN_EPS)
                    nc.vector.memset(zrow[:, :], 0.0).then_inc(s_zero, 1)
                    dve.wait_ge(s_ei, 1)
                    nc.vector.tensor_copy(ef[:, :], ei[:, :])
                    dve.wait_ge(s_col, 16 * 6)
                    nc.vector.tensor_scalar(w9[:, :], w9[:, :], 1.0 - ALPHA, None, ALU.mult)
                    nc.vector.tensor_scalar(dstc[:, :], dst[:, :], N - 1, None, ALU.min)
                    dc.then(nc.vector.tensor_tensor(t1[:, :], dst[:, :], nxt[:, :], ALU.is_equal))
                    dc.then(nc.vector.tensor_scalar(t1[:, :], t1[:, :], FAR, None, ALU.mult))
                    dc.then(nc.vector.tensor_tensor(outi[:, :], t1[:, :], dst[:, :], ALU.add))
                    dc.then(nc.vector.tensor_scalar(t2[:, :], dst[:, :], float(XW), float(F), ALU.mult, ALU.add))
                    dc.then(nc.vector.tensor_tensor(posi[:, :], t1[:, :], t2[:, :], ALU.add))
                    dc.then(nc.vector.tensor_tensor(keepr[:, :], dr[:, :], dp[:, :], ALU.is_equal))
                    nc.vector.tensor_scalar(penr[:, :], keepr[:, :], 1.0, LOW, ALU.subtract, ALU.mult).then_inc(s_keep, 1)
                    dve.wait_ge(s_const, 16 * (len(consts) + len(wide)))
                    dc.then(nc.vector.tensor_scalar(c[:, :], eps0[:, :], 2.0, None, ALU.add))
                    dc.then(nc.vector.tensor_tensor(c2[:, :], c[:, :], c[:, :], ALU.mult))
                    dc.then(nc.vector.tensor_scalar(c2[:, :], c2[:, :], 1.0 / F, None, ALU.mult))
                    nc.vector.tensor_scalar(bias2r[:, :], bias2[:, :], 0.0, None, ALU.max)
                    nc.vector.tensor_tensor(bias3[:, :], bias3[:, :], phb[:, :], ALU.add)
                    dc.then(nc.vector.tensor_tensor(pmt[:, :], phi[:, :], theta[:, :], ALU.subtract))
                    dc.last()

        with ExitStack() as scope:
            def sc(name, shape, dt=F32):
                return scope.enter_context(nc.sbuf_tensor(name, shape, dt))
            nx = [sc(f"nx{b}", [P, ROWS, F]) for b in range(2)]
            no = [sc(f"no{b}", [P, ROWS, F]) for b in range(2)]
            nd, nq = sc("nd", [P, ROWS, F]), sc("nq", [P, ROWS, F])
            nm, nv, ns, nr, nu = (sc(n, [P, ROWS]) for n in ("nm", "nv", "ns", "nr", "nu"))
            pidx = [sc(f"pidx{b}", [P, T], I32) for b in range(2)]
            pval = [sc(f"pval{b}", [P, T]) for b in range(2)]
            s_nx, s_st, s_pos = sems("s_nx"), sems("s_st"), sems("s_pos")
            s_nchain, s_out, s_nvar, s_nstd, s_pstage, s_turn = (sem(n) for n in ("s_nchain", "s_out", "s_nvar", "s_nstd", "s_pstage", "s_turn"))
            xv = a["x"][0:P * ROWS * CHUNKS, :].rearrange("(p c r) f -> p c (r f)", p=P, c=CHUNKS)
            ov = out[0:P * ROWS * CHUNKS, :].rearrange("(p c r) f -> p c (r f)", p=P, c=CHUNKS)
            xpos_cells = xpos.rearrange("n (w o) -> (n w) o", o=1)
            with nc.Block() as block:
                @block.sync
                def _(sp):
                    def load(i, b):
                        wait(sp, s_out, i * 2 + b - 1)
                        sp.dma_start(nx[b][:, :, :].rearrange("p r f -> p (r f)"), xv[:, bass.ds(i * 2 + b, 1)].rearrange("p c w -> p (c w)")).then_inc(s_nx[b], 16)

                    def store(i, b):
                        wait(sp, s_out, i * 2 + b + 1)
                        sp.dma_start(ov[:, bass.ds(i * 2 + b, 1)].rearrange("p c w -> p (c w)"), no[b][:, :, :].rearrange("p r f -> p (r f)")).then_inc(s_st[b], 16)

                    for b in range(2):
                        load(0, b)
                    with sp.Fori(1, CHUNKS // 2) as i:
                        for b in range(2):
                            store(i - 1, b)
                            load(i, b)
                    store(CHUNKS // 2 - 1, 0)
                    sp.dma_start(nx[0][0:RP, 0:RR, :], a["x"][N - REST:N, :].rearrange("(p r) f -> p r f", p=RP)).then_inc(s_nx[0], 16)
                    store(CHUNKS // 2 - 1, 1)
                    sp.wait_ge(s_out, CHUNKS + 1)
                    sp.dma_start(out[N - REST:N, :].rearrange("(p r) f -> p r f", p=RP), no[0][0:RP, 0:RR, :]).then_inc(s_st[0], 16)
                    sp.wait_ge(s_st[0], 16 * (CHUNKS // 2 + 1))
                    sp.wait_ge(s_st[1], 16 * (CHUNKS // 2))

                @block.scalar
                def _(act):
                    def roots(n, p, r):
                        for k in range(4):
                            act.wait_ge(s_nvar, n * 4 + k + 1)
                            nc.scalar.activation(ns[0:p, 0:r], nv[0:p, 0:r], ACT.Sqrt, bias=lneps[0:p, :]).then_inc(s_nstd, 1)

                    def stage(i, b):
                        wait(act, s_pos[b], i * 16 * T)
                        nc.scalar.copy(pidx[b][:, :], col(posi, i * 2 + b)).then_inc(s_pstage, 1)
                        nc.scalar.copy(pval[b][:, :], col(ef, i * 2 + b)).then_inc(s_pstage, 1)

                    for b in range(2):
                        stage(0, b)
                    with act.Fori(0, CHUNKS) as i:
                        for k in range(2):
                            for b in range(2):
                                stage(i * 2 + (1 + k), b)
                        roots(i, P, ROWS)
                    roots(CHUNKS, RP, RR)
                    with act.Fori(2 * CHUNKS + 1, NI) as i:
                        for b in range(2):
                            stage(i, b)

                @block.gpsimd
                def _(pool):
                    bound = pool.to_reg(N * XW - 1)
                    with pool.Fori(0, NI) as i:
                        for b in range(2):
                            pool.wait_ge(s_pstage, (i * 2 + b) * 2 + 2)
                            pool.sem_inc(s_turn, 1)
                            for t in range(T):
                                nc.gpsimd.indirect_dma_start(
                                    out=xpos_cells, out_offset=bass.IndirectOffsetOnAxis(ap=pidx[b][:, t:t + 1], axis=0),
                                    in_=pval[b][:, t:t + 1], in_offset=None, bounds_check=bound, oob_is_err=False).then_inc(s_pos[b], 16)
                    for b in range(2):
                        pool.wait_ge(s_pos[b], NI * 16 * T)

                @block.vector
                def _(dve):
                    dc = Chain(dve, s_nchain, 23)

                    def chunk(n, i, b, p, r):
                        dc.turn(n)
                        x, d, q, o = nx[b][0:p, 0:r, :], nd[0:p, 0:r, :], nq[0:p, 0:r, :], no[b][0:p, 0:r, :]
                        m, v, s, rr, u = (t[0:p, 0:r] for t in (nm, nv, ns, nr, nu))
                        dve.wait_ge(s_nx[b], i * 16 + 16)
                        lone_source(dve, dc, s_nvar, s_nstd, n * 4, x, d, q, m, u, rr, v, s, p, r)
                        dc.then(nc.vector.tensor_tensor(u, u, rr, ALU.mult))
                        nc.vector.scalar_tensor_tensor(out=v, in0=u, scalar=1.0 / F, in1=rr, op0=ALU.mult, op1=ALU.mult).then_inc(s_nvar, 1)
                        dve.wait_ge(s_nstd, n * 4 + 4)
                        dc.then(nc.vector.reciprocal(u, s))
                        dc.then(nc.vector.tensor_tensor(rr, rr, u, ALU.mult))
                        wait(dve, s_st[b], i * 16)
                        nc.vector.tensor_tensor(o, d, mid(rr, r), ALU.mult).then_inc(s_out, 1)
                        dc.last()

                    for b in range(2):
                        chunk(b, 0, b, P, ROWS)
                    with dve.Fori(1, CHUNKS // 2) as i:
                        for b in range(2):
                            chunk(i * 2 + b, i, b, P, ROWS)
                    chunk(CHUNKS, CHUNKS // 2, 0, RP, RR)

        pe_turn = sem("pe_turn")
        gb = pair("gb", [P, T, XW])
        ib = pair("ib", [P, 2 * T], I32)
        kb = pair("kb", [F, GE])
        msg = pair("msg", [P, T, F])
        scan = pair("scan", [F, GE])
        ey, ed, eq = (sb(n, [P, T, F]) for n in ("ey", "ed", "eq"))
        em, eu, er = (sb(n, [P, T]) for n in ("em", "eu", "er"))
        ev, es = sb("ev", [P, T]), sb("es", [P, T])
        psT = [ctx.enter_context(nc.psum_tensor(f"psT{b}", [F, GE], F32)) for b in range(2)]
        psR = [ctx.enter_context(nc.psum_tensor(f"psR{b}", [P, T, F], F32)) for b in range(2)]
        psH = [ctx.enter_context(nc.psum_tensor(f"psH{c}", [P, GE], F32)) for c in range(RC)]
        psM = ctx.enter_context(nc.psum_tensor("psM", [F, GE], F32))

        def slot(ap, t):
            return ap.rearrange("f (p t) -> f p t", t=T)[:, :, t]

        def keep_row(r, g):
            return rows_dram[r:r + 1, bass.ds(g * GE, GE)].to_broadcast([F, GE])

        def pairs(eng, body):
            for b in range(2):
                body(0, b)
            with eng.Fori(1, NI) as i:
                for b in range(2):
                    body(i, b)

        def to_columns(dst_ps, rows_sb):
            for t in range(T):
                last = nc.tensor.transpose(slot(dst_ps, t), rows_sb[:, t, 0:F], ident[:, :])
            return last

        def to_rows(dst_ps, cols_sb):
            for t in range(T):
                last = nc.tensor.transpose(dst_ps[:, t, :], slot(cols_sb, t), ident[0:F, 0:F])
            return last

        with ExitStack() as scope:
            def sp2(name):
                return [scope.enter_context(nc.sbuf_tensor(f"{name}{b}", [P, T, F], F32)) for b in range(2)]
            xdb, efb, act0, x1s, x2s, x3s = (sp2(n) for n in ("xdb", "efb", "act0_", "x1s", "x2s", "x3s"))
            s_g, s_ef, s_kb, s_s1, s_s2, s_s3 = (sems(n) for n in ("a_g", "a_ef", "a_kb", "a_s1", "a_s2", "a_s3"))
            s_x1 = sems("a_x1")
            (s_stage, s_turn, s_add, s_relu, s_cols, s_scan, s_rows, s_pre, s_epi, s_src, s_read, s_self, s_xd, s_var,
             s_std, s_sum) = (sem(f"a_{n}") for n in ("stage", "turn", "add", "relu", "cols", "scan", "rows", "pre", "epi",
                             "src", "read", "self", "xd", "var", "std", "sum"))
            with nc.Block() as block:
                @block.sync
                def _(sp):
                    def load(i, b):
                        g = i * 2 + b
                        wait(sp, s_add, g - 1)
                        sp.dma_start(efb[b][:, :, :].rearrange("p t f -> p (t f)"), a["edge"][:, bass.ds(g * T * F, T * F)]).then_inc(s_ef[b], 16)
                        wait(sp, s_scan, g - 1)
                        sp.dma_start(kb[b][:, :], keep_row(0, g)).then_inc(s_kb[b], 16)

                    def store(i, b):
                        g = i * 2 + b
                        sp.wait_ge(s_src, g + 1)
                        for buf, k, s in ((x1s, 1, s_s1), (x2s, 2, s_s2), (x3s, 3, s_s3)):
                            sp.dma_start(rows(layer[k], g, EP), buf[b][:, :, :].rearrange("p t f -> p (t f)")).then_inc(s[b], 16)

                    def store_x1(i, b):
                        g = i * 2 + b
                        sp.wait_ge(s_xd, g + 1)
                        sp.dma_start(rows(layer[1], g), XD[:, bass.ds(g * T * F, T * F)]).then_inc(s_x1[b], 16)

                    load(0, 0)
                    load(0, 1)
                    store(0, 0)
                    with sp.Fori(1, NI) as i:
                        load(i, 0)
                        store(i - 1, 1)
                        store_x1(i - 1, 0)
                        load(i, 1)
                        store(i, 0)
                        store_x1(i - 1, 1)
                    store(NI - 1, 1)
                    store_x1(NI - 1, 0)
                    store_x1(NI - 1, 1)
                    for b in range(2):
                        for s in (s_s1, s_s2, s_s3, s_x1):
                            sp.wait_ge(s[b], 16 * NI)

                @block.scalar
                def _(act):
                    def stage(i, b):
                        g = i * 2 + b
                        wait(act, s_g[b], i * 32 * T)
                        nc.scalar.copy(ib[b][:, 0:T], col(src, g)).then_inc(s_stage, 1)
                        nc.scalar.copy(ib[b][:, T:2 * T], col(dstc, g)).then_inc(s_stage, 1)

                    def root(n):
                        act.wait_ge(s_var, n + 1)
                        nc.scalar.activation(es[:, :], ev[:, :], ACT.Sqrt, bias=lneps[:, :]).then_inc(s_std, 1)

                    def body(i, b):
                        g = i * 2 + b
                        stage(i + b, 1 - b)
                        act.wait_ge(s_add, g + 1)
                        wait(act, s_cols, g - 1)
                        nc.scalar.activation(act0[b][:, :, :], msg[b][:, :, :], ACT.Relu).then_inc(s_relu, 1)
                        nc.scalar.copy(col(posf, g), gb[b][:, :, F]).then_inc(s_read, 1)
                        first = isinstance(g, int) and g == 0
                        at = 0 if first else g * 4 - 1
                        for k in range(3 if first else 4):
                            root(at + k)

                    stage(0, 0)
                    pairs(act, body)
                    root(4 * NG - 1)

                @block.gpsimd
                def _(pool):
                    def body(i, b):
                        g = i * 2 + b
                        wait(pool, s_read, g - 1)
                        wait(pool, s_src, g - 1)
                        wait(pool, s_self, g - 1)
                        pool.wait_ge(s_stage, (g + 1) * 2)
                        pool.sem_inc(s_turn, 1)
                        for t in range(T):
                            nc.gpsimd.indirect_dma_start(
                                out=gb[b][:, t, :], out_offset=None, in_=xpos,
                                in_offset=bass.IndirectOffsetOnAxis(ap=ib[b][:, t:t + 1], axis=0)).then_inc(s_g[b], 16)
                        for t in range(T):
                            nc.gpsimd.indirect_dma_start(
                                out=xdb[b][:, t, :], out_offset=None, in_=a["x"],
                                in_offset=bass.IndirectOffsetOnAxis(ap=ib[b][:, T + t:T + t + 1], axis=0)).then_inc(s_g[b], 16)

                    pairs(pool, body)

                @block.tensor
                def _(pe):
                    def body(i, b):
                        g = i * 2 + b
                        pe.wait_ge(s_relu, g + 1)
                        wait(pe, s_scan, g - 1)
                        pe.sem_inc(pe_turn, 1)
                        to_columns(psT[b], act0[b]).then_inc(s_cols, 1)
                        pe.wait_ge(s_scan, g + 1)
                        wait(pe, s_sum, g - 1)
                        pe.sem_inc(pe_turn, 1)
                        to_rows(psR[b], scan[b]).then_inc(s_rows, 1)

                    pairs(pe, body)

                @block.vector
                def _(dve):
                    pre, epi = Chain(dve, s_pre, 20), Chain(dve, s_epi, 6)

                    def epilogue(i, b, k):
                        g = i * 2 + b
                        epi.turn(g)
                        dve.wait_ge(s_rows, g + 1)
                        nc.vector.tensor_tensor(ey[:, :, :], psR[b][:, :, :], xd(g), ALU.add).then_inc(s_sum, 1)
                        dve.wait_ge(s_sum, g + 1)
                        centre(epi, ey[:, :, :], ed[:, :, :], eq[:, :, :], em[:, :], eu[:, :], T)
                        nc.vector.tensor_scalar(ev[:, :], eu[:, :], 1.0 / F, None, ALU.mult).then_inc(s_var, 1)
                        dve.wait_ge(s_std, k + 1)
                        epi.then(nc.vector.reciprocal(er[:, :], es[:, :]))
                        nc.vector.tensor_tensor(xd(g), ed[:, :, :], mid(er[:, :], T), ALU.mult).then_inc(s_xd, 1)
                        epi.last()

                    def body(i, b):
                        g = i * 2 + b
                        first = isinstance(g, int) and g == 0
                        pre.turn(g)
                        dve.wait_ge(s_g[b], (i + 1) * 32 * T)
                        dve.wait_ge(s_ef[b], (i + 1) * 16)
                        wait(dve, s_relu, g - 1)
                        nc.vector.tensor_tensor(msg[b][:, :, :], gb[b][:, :, 0:F], efb[b][:, :, :], ALU.add).then_inc(s_add, 1)
                        nc.vector.tensor_scalar(xd(g), xdb[b][:, :, :], c[:, :], None, ALU.mult).then_inc(s_self, 1)
                        wait(dve, s_s1[b], i * 16)
                        wait(dve, s_s2[b], i * 16)
                        wait(dve, s_s3[b], i * 16)
                        lone_source(dve, pre, s_var, s_std, 0 if first else g * 4 - 1, gb[b][:, :, 0:F], ed[:, :, :], eq[:, :, :],
                                    em[:, :], eu[:, :], er[:, :], ev[:, :], es[:, :], P, T, x1s[b][:, :, :], x2s[b][:, :, :])
                        nc.vector.tensor_tensor(x3s[b][:, :, :], ed[:, :, :], mid(er[:, :], T), ALU.mult).then_inc(s_src, 1)
                        if not first:
                            epilogue(i - 1 + b, 1 - b, g * 4 + 2)
                        dve.wait_ge(s_cols, g + 1)
                        dve.wait_ge(s_kb[b], (i + 1) * 16)
                        wait(dve, s_rows, g - 1)
                        wait(dve, s_scan, g)
                        start = 0.0 if first else scan[1 - b][:, GE - 1:GE]
                        nc.vector.tensor_tensor_scan(scan[b][:, :], kb[b][:, :], psT[b][:, :], start, ALU.mult, ALU.add).then_inc(s_scan, 1)
                        pre.last()

                    pairs(dve, body)
                    epilogue(NI - 1, 1, 4 * NG - 1)

        with ExitStack() as scope:
            s_idx = sem("s_idx")
            with nc.Block() as block:
                @block.vector
                def _(dve):
                    dc = Chain(dve, s_idx, 7).turn(0)
                    W = NG * T
                    own, end, has, far = ef[:, 0:W], posf[:, 0:W], t1[:, 0:W], t2[:, 0:W]
                    dc.then(nc.vector.tensor_scalar(has, end, 0.0, None, ALU.is_ge))
                    dc.then(nc.vector.tensor_scalar(own, own, float(EP), None, ALU.add))
                    dc.then(nc.vector.tensor_tensor(far, end, own, ALU.subtract))
                    dc.then(nc.vector.tensor_tensor(far, far, has, ALU.mult))
                    dc.then(nc.vector.tensor_tensor(idx2[:, 0:W], far, own, ALU.add))
                    dc.then(nc.vector.scalar_tensor_tensor(out=far, in0=end, scalar=float(EP), in1=has, op0=ALU.subtract, op1=ALU.mult))
                    nc.vector.tensor_scalar(idxk[:, 0:W], far, float(EP), None, ALU.add)
                    nc.vector.memset(idx2[:, W:NC], 0)
                    dc.then(nc.vector.memset(idxk[:, W:NC], 0))
                    dc.last()

        with ExitStack() as scope:
            rb = [scope.enter_context(nc.sbuf_tensor(f"rb{b}", [P, T, F], F32)) for b in range(2)]
            s_g, s_kb, s_rst, s_x2 = (sems(n) for n in ("b_g", "b_kb", "b_rst", "b_x2"))
            (s_stage, s_turn, s_msg, s_cols, s_scan, s_rows, s_rb, s_acc, s_epi, s_xd, s_var, s_std, s_two) = (
                sem(f"b_{n}") for n in ("stage", "turn", "msg", "cols", "scan", "rows", "rb", "acc", "epi", "xd", "var", "std", "two"))
            LAST = STEPS - 1

            def passes(eng, one):
                one(0, layer[1], krylov[0])
                with eng.Fori(0, (STEPS - 2) // 2) as j:
                    for h in range(2):
                        one(j * 2 + (1 + h), krylov[h], krylov[1 - h])
                one(LAST, krylov[0], None)

            with nc.Block() as block:
                @block.sync
                def _(sp):
                    def one(k, _, target):
                        def load(i, b):
                            n = k * NG + i * 2 + b
                            wait(sp, s_scan, n - 1)
                            sp.dma_start(kb[b][:, :], keep_row(0, i * 2 + b)).then_inc(s_kb[b], 16)

                        def store(i, b):
                            n = k * NG + i * 2 + b
                            if target is None:
                                sp.wait_ge(s_xd, i * 2 + b + 1)
                                sp.dma_start(rows(layer[2], i * 2 + b), XD[:, bass.ds((i * 2 + b) * T * F, T * F)]).then_inc(s_x2[b], 16)
                            else:
                                sp.wait_ge(s_rb, n + 1)
                                sp.dma_start(rows(target, i * 2 + b), rb[b][:, :, :].rearrange("p t f -> p (t f)")).then_inc(s_rst[b], 16)

                        load(0, 0)
                        load(0, 1)
                        with sp.Fori(1, NI) as i:
                            load(i, 0)
                            store(i - 1, 0)
                            load(i, 1)
                            store(i - 1, 1)
                        store(NI - 1, 0)
                        store(NI - 1, 1)

                    passes(sp, one)
                    for b in range(2):
                        sp.wait_ge(s_rst[b], 16 * NI * LAST)
                        sp.wait_ge(s_x2[b], 16 * NI)

                @block.scalar
                def _(act):
                    def one(k, _, target):
                        first_pass = isinstance(k, int) and k == 0
                        idx = idx2 if first_pass else idxk

                        def stage(i, b):
                            wait(act, s_g[b], (k * NI + i) * 16 * T)
                            nc.scalar.copy(ib[b][:, 0:T], col(idx, i * 2 + b)).then_inc(s_stage, 1)

                        def body(i, b):
                            n = k * NG + i * 2 + b
                            stage(i + b, 1 - b)
                            act.wait_ge(s_rows, n + 1)
                            if target is not None:
                                wait(act, s_rst[b], (k * NI + i) * 16)
                                wait(act, s_acc, n - 1)
                                nc.scalar.copy(rb[b][:, :, :], psR[b][:, :, :]).then_inc(s_rb, 1)
                            else:
                                act.wait_ge(s_var, i * 2 + b + 1)
                                nc.scalar.activation(es[:, :], ev[:, :], ACT.Sqrt, bias=lneps[:, :]).then_inc(s_std, 1)

                        wait(act, s_stage, k * (NG + 1))
                        stage(0, 0)
                        pairs(act, body)

                    passes(act, one)

                @block.gpsimd
                def _(pool):
                    def one(k, source, _):
                        def body(i, b):
                            g = i * 2 + b
                            wait(pool, s_msg, k * NG + g - 1)
                            pool.wait_ge(s_stage, k * (NG + 1) + g + 1)
                            pool.sem_inc(s_turn, 1)
                            for t in range(T):
                                nc.gpsimd.indirect_dma_start(
                                    out=gb[b][:, t, 0:F], out_offset=None, in_=source,
                                    in_offset=bass.IndirectOffsetOnAxis(ap=ib[b][:, t:t + 1], axis=0)).then_inc(s_g[b], 16)

                        for b in range(2):
                            wait(pool, s_rst[b], k * NI * 16)
                        pairs(pool, body)

                    passes(pool, one)

                @block.tensor
                def _(pe):
                    def one(k, _, target):
                        def body(i, b):
                            n = k * NG + i * 2 + b
                            pe.wait_ge(s_msg, n + 1)
                            wait(pe, s_scan, n - 1)
                            pe.sem_inc(pe_turn, 1)
                            to_columns(psT[b], msg[b]).then_inc(s_cols, 1)
                            pe.wait_ge(s_scan, n + 1)
                            if target is not None:
                                wait(pe, s_rb, n - 1)
                            else:
                                wait(pe, s_rb, LAST * NG)
                                wait(pe, s_acc, n - 1)
                            pe.sem_inc(pe_turn, 1)
                            to_rows(psR[b], scan[b]).then_inc(s_rows, 1)

                        pairs(pe, body)

                    passes(pe, one)

                @block.vector
                def _(dve):
                    epi = Chain(dve, s_epi, 6)

                    def one(k, _, target):
                        first_pass = isinstance(k, int) and k == 0

                        def epilogue(i, b):
                            g = i * 2 + b
                            if target is not None:
                                if first_pass:
                                    dve.wait_ge(s_two, g + 1)
                                dve.wait_ge(s_rb, k * NG + g + 1)
                                nc.vector.scalar_tensor_tensor(out=xd(g), in0=rb[b][:, :, :], scalar=ALPHA, in1=xd(g), op0=ALU.mult, op1=ALU.add).then_inc(s_acc, 1)
                                return
                            dve.wait_ge(s_rows, k * NG + g + 1)
                            nc.vector.tensor_tensor(ey[:, :, :], psR[b][:, :, :], xd(g), ALU.add).then_inc(s_acc, 1)
                            dve.wait_ge(s_acc, k * NG + g + 1)
                            epi.turn(g)
                            centre(epi, ey[:, :, :], ed[:, :, :], eq[:, :, :], em[:, :], eu[:, :], T)
                            nc.vector.tensor_scalar(ev[:, :], eu[:, :], 1.0 / F, None, ALU.mult).then_inc(s_var, 1)
                            dve.wait_ge(s_std, g + 1)
                            epi.then(nc.vector.reciprocal(er[:, :], es[:, :]))
                            nc.vector.tensor_tensor(xd(g), ed[:, :, :], mid(er[:, :], T), ALU.mult).then_inc(s_xd, 1)
                            epi.last()

                        def body(i, b):
                            g = i * 2 + b
                            n = k * NG + g
                            first = isinstance(i, int) and i == 0 and b == 0
                            dve.wait_ge(s_g[b], (k * NI + i + 1) * 16 * T)
                            wait(dve, s_cols, n - 1)
                            nc.vector.tensor_tensor(msg[b][:, :, :], gb[b][:, :, 0:F], mid(col(w9, g), T), ALU.mult).then_inc(s_msg, 1)
                            if first_pass:
                                nc.vector.tensor_scalar(xd(g), xd(g), 1 + ALPHA, None, ALU.mult).then_inc(s_two, 1)
                            if not first:
                                epilogue(i - 1 + b, 1 - b)
                            dve.wait_ge(s_cols, n + 1)
                            dve.wait_ge(s_kb[b], (k * NI + i + 1) * 16)
                            wait(dve, s_rows, n - 1)
                            wait(dve, s_scan, n)
                            start = 0.0 if first else scan[1 - b][:, GE - 1:GE]
                            nc.vector.tensor_tensor_scan(scan[b][:, :], kb[b][:, :], psT[b][:, :], start, ALU.mult, ALU.add).then_inc(s_scan, 1)

                        pairs(dve, body)
                        epilogue(NI - 1, 1)

                    passes(dve, one)

        with ExitStack() as scope:
            tb = [scope.enter_context(nc.sbuf_tensor(f"tb{b}", [P, GE], I32)) for b in range(2)]
            nb = [scope.enter_context(nc.sbuf_tensor(f"nb{b}", [F, GE], F32)) for b in range(2)]
            xT = scope.enter_context(nc.sbuf_tensor("xT", [F, GE], F32))
            h1 = [scope.enter_context(nc.sbuf_tensor(f"h1{q}", [P, GE], F32)) for q in range(RC)]
            hm = [scope.enter_context(nc.sbuf_tensor(f"hm{q}", [P, GE], F32)) for q in range(RC)]
            mw = scope.enter_context(nc.sbuf_tensor("mw", [F, GE], F32))
            s_g, s_kb, s_tb, s_nb, s_x3 = (sems(n) for n in ("c_g", "c_kb", "c_tb", "c_nb", "c_x3"))
            (s_stage, s_turn, s_cols, s_xT, s_h, s_h1, s_hm, s_m, s_mw, s_scan, s_rows, s_sum, s_epi, s_xd, s_var, s_std) = (
                sem(f"c_{n}") for n in ("stage", "turn", "cols", "xT", "h", "h1", "hm", "m", "mw", "scan", "rows", "sum", "epi",
                                        "xd", "var", "std"))
            with nc.Block() as block:
                @block.sync
                def _(sp):
                    def load(i, b):
                        g = i * 2 + b
                        wait(sp, s_hm, RC * (g - 1))
                        sp.dma_start(tb[b][:, :], a["type_row"][bass.ds(g * GE, GE)].partition_broadcast(P)).then_inc(s_tb[b], 16)
                        wait(sp, s_mw, g - 1)
                        sp.dma_start(nb[b][:, :], a["norm_row"][bass.ds(g * GE, GE)].partition_broadcast(F)).then_inc(s_nb[b], 16)
                        wait(sp, s_scan, g - 1)
                        sp.dma_start(kb[b][:, :], keep_row(0, g)).then_inc(s_kb[b], 16)

                    def store(i, b):
                        g = i * 2 + b
                        sp.wait_ge(s_xd, g + 1)
                        sp.dma_start(rows(layer[3], g), XD[:, bass.ds(g * T * F, T * F)]).then_inc(s_x3[b], 16)

                    load(0, 0)
                    load(0, 1)
                    with sp.Fori(1, NI) as i:
                        load(i, 0)
                        store(i - 1, 0)
                        load(i, 1)
                        store(i - 1, 1)
                    store(NI - 1, 0)
                    store(NI - 1, 1)
                    for b in range(2):
                        sp.wait_ge(s_x3[b], 16 * NI)

                @block.scalar
                def _(act):
                    def stage(i, b):
                        wait(act, s_g[b], i * 16 * T)
                        nc.scalar.copy(ib[b][:, 0:T], col(idx2, i * 2 + b)).then_inc(s_stage, 1)

                    def root(g):
                        act.wait_ge(s_var, g + 1)
                        nc.scalar.activation(es[:, :], ev[:, :], ACT.Sqrt, bias=lneps[:, :]).then_inc(s_std, 1)

                    def body(i, b):
                        g = i * 2 + b
                        first = isinstance(g, int) and g == 0
                        stage(i + b, 1 - b)
                        act.wait_ge(s_cols, g + 1)
                        wait(act, s_h, RC * g)
                        nc.scalar.copy(xT[:, :], psT[b][:, :]).then_inc(s_xT, 1)
                        for q in range(RC):
                            act.wait_ge(s_h, RC * g + q + 1)
                            wait(act, s_hm, RC * (g - 1) + q + 1)
                            nc.scalar.activation(h1[q][:, :], psH[q][:, :], ACT.Relu, bias=bias1[:, q:q + 1]).then_inc(s_h1, 1)
                        if not first:
                            root(g - 1)

                    stage(0, 0)
                    pairs(act, body)
                    root(NG - 1)

                @block.gpsimd
                def _(pool):
                    def body(i, b):
                        g = i * 2 + b
                        wait(pool, s_cols, g - 1)
                        pool.wait_ge(s_stage, g + 1)
                        pool.sem_inc(s_turn, 1)
                        for t in range(T):
                            nc.gpsimd.indirect_dma_start(
                                out=gb[b][:, t, 0:F], out_offset=None, in_=layer[2],
                                in_offset=bass.IndirectOffsetOnAxis(ap=ib[b][:, t:t + 1], axis=0)).then_inc(s_g[b], 16)

                    pairs(pool, body)

                @block.tensor
                def _(pe):
                    def body(i, b):
                        g = i * 2 + b
                        pe.wait_ge(s_g[b], (i + 1) * 16 * T)
                        wait(pe, s_xT, g - 1)
                        pe.sem_inc(pe_turn, 1)
                        to_columns(psT[b], gb[b]).then_inc(s_cols, 1)
                        pe.wait_ge(s_xT, g + 1)
                        for q in range(RC):
                            wait(pe, s_h1, RC * (g - 1) + q + 1)
                            nc.tensor.matmul(psH[q][:, :], w1[:, q * P:(q + 1) * P], xT[:, :], start=True, stop=True).then_inc(s_h, 1)
                        wait(pe, s_mw, g)
                        for q in range(RC):
                            pe.wait_ge(s_hm, RC * g + q + 1)
                            last = nc.tensor.matmul(psM[:, :], w2[:, q, :], hm[q][:, :], start=q == 0, stop=q == RC - 1)
                        last.then_inc(s_m, 1)
                        pe.wait_ge(s_scan, g + 1)
                        wait(pe, s_sum, g - 1)
                        pe.sem_inc(pe_turn, 1)
                        to_rows(psR[b], scan[b]).then_inc(s_rows, 1)

                    pairs(pe, body)

                @block.vector
                def _(dve):
                    epi = Chain(dve, s_epi, 7)

                    def epilogue(i, b):
                        g = i * 2 + b
                        epi.turn(g)
                        dve.wait_ge(s_rows, g + 1)
                        nc.vector.tensor_tensor(ey[:, :, :], psR[b][:, :, :], bias2[:, :].unsqueeze(1).to_broadcast([P, T, F]), ALU.add).then_inc(s_sum, 1)
                        dve.wait_ge(s_sum, g + 1)
                        epi.then(nc.vector.scalar_tensor_tensor(out=ey[:, :, :], in0=ey[:, :, :], scalar=0.0, in1=xd(g), op0=ALU.max, op1=ALU.add))
                        centre(epi, ey[:, :, :], ed[:, :, :], eq[:, :, :], em[:, :], eu[:, :], T)
                        nc.vector.tensor_scalar(ev[:, :], eu[:, :], 1.0 / F, None, ALU.mult).then_inc(s_var, 1)
                        dve.wait_ge(s_std, g + 1)
                        epi.then(nc.vector.reciprocal(er[:, :], es[:, :]))
                        nc.vector.tensor_tensor(xd(g), ed[:, :, :], mid(er[:, :], T), ALU.mult).then_inc(s_xd, 1)
                        epi.last()

                    def body(i, b):
                        g = i * 2 + b
                        first = isinstance(g, int) and g == 0
                        dve.wait_ge(s_tb[b], (i + 1) * 16)
                        for q in range(RC):
                            dve.wait_ge(s_h1, RC * g + q + 1)
                            wait(dve, s_m, g)
                            nc.vector.scalar_tensor_tensor(out=hm[q][:, :], in0=tb[b][:, :], scalar=rel[:, q:q + 1], in1=h1[q][:, :], op0=ALU.is_equal, op1=ALU.mult).then_inc(s_hm, 1)
                        if not first:
                            epilogue(i - 1 + b, 1 - b)
                        dve.wait_ge(s_m, g + 1)
                        dve.wait_ge(s_nb[b], (i + 1) * 16)
                        nc.vector.tensor_tensor(mw[:, :], psM[:, :], nb[b][:, :], ALU.mult).then_inc(s_mw, 1)
                        dve.wait_ge(s_mw, g + 1)
                        dve.wait_ge(s_kb[b], (i + 1) * 16)
                        wait(dve, s_rows, g - 1)
                        wait(dve, s_scan, g)
                        start = 0.0 if first else scan[1 - b][:, GE - 1:GE]
                        nc.vector.tensor_tensor_scan(scan[b][:, :], kb[b][:, :], mw[:, :], start, ALU.mult, ALU.add).then_inc(s_scan, 1)

                    pairs(dve, body)
                    epilogue(NI - 1, 1)

        with ExitStack() as scope:
            dT = scope.enter_context(nc.sbuf_tensor("dT", [F, GE], F32))
            xT = scope.enter_context(nc.sbuf_tensor("xT3", [F, GE], F32))
            xdb, xo = ([scope.enter_context(nc.sbuf_tensor(f"{n}{b}", [P, T, F], F32)) for b in range(2)] for n in ("xdb3", "xo"))
            ob = [scope.enter_context(nc.sbuf_tensor(f"ob{b}", [P, T], I32)) for b in range(2)]
            psD = psH[0][0:F, :]
            s_g, s_kb, s_o = (sems(n) for n in ("d_g", "d_kb", "d_o"))
            (s_stage, s_turn, s_own, s_cols, s_dcols, s_xT, s_dT, s_e, s_scan, s_rows, s_sum, s_epi, s_xo, s_var, s_std,
             s_obs) = (sem(f"d_{n}") for n in ("stage", "turn", "own", "cols", "dcols", "xT", "dT", "e", "scan", "rows", "sum",
                                               "epi", "xo", "var", "std", "obs"))
            with nc.Block() as block:
                @block.sync
                def _(sp):
                    def load(i, b):
                        wait(sp, s_scan, i * 2 + b - 1)
                        sp.dma_start(kb[b][:, :], keep_row(1, i * 2 + b)).then_inc(s_kb[b], 16)

                    pairs(sp, load)

                @block.scalar
                def _(act):
                    def stage(i, b):
                        wait(act, s_g[b], i * 16 * T)
                        nc.scalar.copy(ib[b][:, 0:T], col(idx2, i * 2 + b)).then_inc(s_stage, 1)

                    def root(g):
                        act.wait_ge(s_var, g + 1)
                        nc.scalar.activation(es[:, :], ev[:, :], ACT.Sqrt, bias=lneps[:, :]).then_inc(s_std, 1)

                    def body(i, b):
                        g = i * 2 + b
                        first = isinstance(g, int) and g == 0
                        stage(i + b, 1 - b)
                        wait(act, s_dcols, g - 1)
                        wait(act, s_sum, g - 1)
                        nc.scalar.copy(xdb[b][:, :, :], xd(g)).then_inc(s_own, 1)
                        act.wait_ge(s_cols, g + 1)
                        wait(act, s_e, g)
                        nc.scalar.copy(xT[:, :], psT[b][:, :]).then_inc(s_xT, 1)
                        act.wait_ge(s_dcols, g + 1)
                        wait(act, s_rows, g)
                        nc.scalar.copy(dT[:, :], psD).then_inc(s_dT, 1)
                        wait(act, s_o[b], i * 16 * T)
                        nc.scalar.copy(ob[b][:, :], col(outi, g)).then_inc(s_obs, 1)
                        if not first:
                            root(g - 1)

                    stage(0, 0)
                    pairs(act, body)
                    root(NG - 1)

                @block.gpsimd
                def _(pool):
                    bound = pool.to_reg(N - 1)

                    def gather(i, b):
                        g = i * 2 + b
                        wait(pool, s_cols, g - 1)
                        pool.wait_ge(s_stage, g + 1)
                        pool.sem_inc(s_turn, 1)
                        for t in range(T):
                            nc.gpsimd.indirect_dma_start(
                                out=gb[b][:, t, 0:F], out_offset=None, in_=layer[3],
                                in_offset=bass.IndirectOffsetOnAxis(ap=ib[b][:, t:t + 1], axis=0)).then_inc(s_g[b], 16)

                    def scatter(i, b):
                        g = i * 2 + b
                        pool.wait_ge(s_xo, g + 1)
                        pool.wait_ge(s_obs, g + 1)
                        pool.sem_inc(s_turn, 1)
                        for t in range(T):
                            nc.gpsimd.indirect_dma_start(
                                out=out, out_offset=bass.IndirectOffsetOnAxis(ap=ob[b][:, t:t + 1], axis=0),
                                in_=xo[b][:, t, :], in_offset=None, bounds_check=bound, oob_is_err=False).then_inc(s_o[b], 16)

                    for b in range(2):
                        gather(0, b)
                    with pool.Fori(1, NI) as i:
                        for b in range(2):
                            gather(i, b)
                            scatter(i - 1, b)
                    for b in range(2):
                        scatter(NI - 1, b)
                    for b in range(2):
                        pool.wait_ge(s_o[b], NI * 16 * T)

                @block.tensor
                def _(pe):
                    def body(i, b):
                        g = i * 2 + b
                        pe.wait_ge(s_own, g + 1)
                        wait(pe, s_dT, g)
                        pe.sem_inc(pe_turn, 1)
                        to_columns(psD, xdb[b]).then_inc(s_dcols, 1)
                        pe.wait_ge(s_g[b], (i + 1) * 16 * T)
                        wait(pe, s_xT, g - 1)
                        pe.sem_inc(pe_turn, 1)
                        to_columns(psT[b], gb[b]).then_inc(s_cols, 1)
                        pe.wait_ge(s_xT, g + 1)
                        wait(pe, s_scan, g)
                        pe.sem_inc(pe_turn, 1)
                        nc.tensor.matmul(psM[:, :], pmt[:, :], xT[:, :], start=True, stop=True).then_inc(s_e, 1)
                        pe.wait_ge(s_dT, g + 1)
                        pe.wait_ge(s_scan, g + 1)
                        wait(pe, s_sum, g - 1)
                        pe.sem_inc(pe_turn, 1)
                        for t in range(T):
                            nc.tensor.matmul(psR[b][:, t, :], slot(scan[b], t), ident[0:F, 0:F], start=True, stop=False)
                            last = nc.tensor.matmul(psR[b][:, t, :], slot(dT, t), theta[:, :], start=False, stop=True)
                        last.then_inc(s_rows, 1)

                    pairs(pe, body)

                @block.vector
                def _(dve):
                    epi = Chain(dve, s_epi, 7)

                    def epilogue(i, b):
                        g = i * 2 + b
                        epi.turn(g)
                        dve.wait_ge(s_rows, g + 1)
                        epi.then(nc.vector.tensor_tensor(ey[:, :, :], psR[b][:, :, :], bias3[:, :].unsqueeze(1).to_broadcast([P, T, F]), ALU.add))
                        nc.vector.tensor_tensor(ey[:, :, :], ey[:, :, :], xdb[b][:, :, :], ALU.add).then_inc(s_sum, 1)
                        dve.wait_ge(s_sum, g + 1)
                        centre(epi, ey[:, :, :], ed[:, :, :], eq[:, :, :], em[:, :], eu[:, :], T)
                        nc.vector.tensor_scalar(ev[:, :], eu[:, :], 1.0 / F, None, ALU.mult).then_inc(s_var, 1)
                        dve.wait_ge(s_std, g + 1)
                        epi.then(nc.vector.reciprocal(er[:, :], es[:, :]))
                        wait(dve, s_o[b], i * 16 * T)
                        nc.vector.tensor_tensor(xo[b][:, :, :], ed[:, :, :], mid(er[:, :], T), ALU.mult).then_inc(s_xo, 1)
                        epi.last()

                    def body(i, b):
                        g = i * 2 + b
                        first = isinstance(g, int) and g == 0
                        dve.wait_ge(s_e, g + 1)
                        dve.wait_ge(s_kb[b], (i + 1) * 16)
                        wait(dve, s_rows, g - 1)
                        wait(dve, s_scan, g)
                        start = 0.0 if first else scan[1 - b][:, GE - 1:GE]
                        nc.vector.tensor_tensor_scan(scan[b][:, :], kb[b][:, :], psM[:, :], start, ALU.add, ALU.max).then_inc(s_scan, 1)
                        if not first:
                            epilogue(i - 1 + b, 1 - b)

                    pairs(dve, body)
                    epilogue(NI - 1, 1)


def kernel(**inputs):
    import numpy as np
    import concourse.bacc as bacc
    from concourse.bass_utils import run_bass_kernel_spmd

    given = {k: np.ascontiguousarray(np.asarray(v)) for k, v in inputs.items()}

    def padded(v, n, fill):
        return np.concatenate([v, np.full((n - v.shape[0],) + v.shape[1:], fill, v.dtype)])

    def columns(v, fill):
        return np.ascontiguousarray(padded(v, NC * P, fill).reshape(NG + 1, P, T).transpose(1, 0, 2).reshape(P, NC))

    dst = given["dst"]
    arrays = {
        "x": given["x"],
        "src": columns(given["src"], 0),
        "dst": columns(dst, N),
        "nxt": columns(padded(dst[1:], E, N), N),
        "dst_row": np.concatenate([np.full(1, -1, dst.dtype), padded(dst, EP, N)]),
        "ew": columns(given["edge_weight"], 0),
        "edge": np.ascontiguousarray(padded(given["edge_attr_48"], EP, 0).reshape(NG, P, T * F).transpose(1, 0, 2).reshape(P, NG * T * F)),
        "type_row": padded(given["edge_type_8"], EP, 0),
        "norm_row": padded(given["edge_weight1"].reshape(E), EP, 0),
        "eps": given["L0_gnn_eps"],
        "w1": np.ascontiguousarray(given["L2_gnn_weight1"].transpose(1, 0, 2).reshape(F, R * F)),
        "w2": np.ascontiguousarray(given["L2_gnn_weight2"].reshape(RC, P, F).transpose(1, 0, 2)),
        "bias1": np.ascontiguousarray(np.tile(given["L2_gnn_bias1"], R).reshape(RC, P).T),
        "bias2": given["L2_gnn_bias2"],
        "thetaT": np.ascontiguousarray(given["L3_gnn_theta_w"].T),
        "phiT": np.ascontiguousarray(given["L3_gnn_phi_w"].T),
        "theta_b": given["L3_gnn_theta_b"],
        "phi_b": given["L3_gnn_phi_b"],
        "ident": np.eye(P, dtype=np.float32),
        "rel": np.ascontiguousarray((np.arange(R * F) // F).astype(np.float32).reshape(RC, P).T),
    }
    nc = bacc.Bacc("TRN2", target_bir_lowering=False, num_devices=1)
    aps = {k: nc.dram_tensor(f"in_{k}", v.shape, mybir.dt.from_np(v.dtype), kind="ExternalInput").ap() for k, v in arrays.items()}
    out = nc.dram_tensor("out", (N, F), F32, kind="ExternalOutput").ap()
    gnn(nc, aps, out)
    r = run_bass_kernel_spmd(nc, [{f"in_{k}": v for k, v in arrays.items()}], core_ids=[0])
    return r.results[0]["out"]
```

```python
import concourse.bass as bass
from concourse import mybir
from contextlib import ExitStack

F32, I32 = mybir.dt.float32, mybir.dt.int32
ALU, ACT, AX = mybir.AluOpType, mybir.ActivationFunctionType, mybir.AxisListType

N, E, F, R = 100000, 50000, 48, 8
P, T = 128, 4
GE = P * T
U = 4
NG = -(-E // (GE * U)) * U
NT = NG // U
EP = NG * GE
NC = (NG + 2) * T
RC = R * F // P
XW = F + 1
ROWS, CHUNKS = 39, 20
PG = NG // CHUNKS
assert PG * CHUNKS == NG and CHUNKS % 2 == 0
REST = N - P * ROWS * CHUNKS
RP, RR = 32, REST // 32
LN_EPS, ALPHA, STEPS = 1e-5, 0.1, 10
FAR = float(1 << 23)
LOW = 3.0e38


def wait(eng, sem, value):
    if not isinstance(value, int) or value > 0:
        eng.wait_ge(sem, value)


class Chain:

    def __init__(self, eng, sem, per):
        self.eng, self.sem, self.per = eng, sem, per

    def turn(self, n):
        self.base, self.count = n * self.per, 0
        return self

    def then(self, ins):
        ins.then_inc(self.sem, 1)
        self.count += 1
        assert self.count <= self.per
        self.eng.wait_ge(self.sem, self.base + self.count)

    def last(self):
        assert self.count == self.per, (self.count, self.per)


def mid(ap, rows):
    return ap.unsqueeze(2).to_broadcast([ap.shape[0], rows, F])


def gnn(nc, a, out):
    ctx = ExitStack()
    with ctx:
        def sb(name, shape, dt=F32):
            return ctx.enter_context(nc.sbuf_tensor(name, shape, dt))

        def pair(name, shape, dt=F32):
            return [sb(f"{name}{b}", shape, dt) for b in range(2)]

        def sem(name):
            return ctx.enter_context(nc.semaphore(name))

        def sems(name):
            return [sem(f"{name}{b}") for b in range(2)]

        def dram(name, shape, dt=F32):
            return nc.dram_tensor(name, shape, dt, kind="Internal").ap()

        xpos = dram("xpos", (N, XW))
        layer = {k: dram(f"layer{k}", (2 * EP, F)) for k in (1, 2, 3)}
        krylov = [dram(f"krylov{b}", (EP + 1, F)) for b in range(2)]
        rows_dram = dram("rows_dram", (2, EP))

        ident = sb("ident", [P, P])
        rel = sb("rel", [P, RC])
        bias1 = sb("bias1", [P, RC])
        bias2 = sb("bias2", [P, F])
        bias2c = sb("bias2c", [P, F])
        bias3 = sb("bias3", [P, F])
        phb = sb("phb", [P, F])
        w1 = sb("w1", [F, R * F])
        w2 = sb("w2", [P, RC, F])
        theta = sb("theta", [F, F])
        phi = sb("phi", [F, F])
        pmt = sb("pmt", [F, F])
        eps0 = sb("eps0", [P, 1])
        c = sb("c", [P, 1])
        c2 = sb("c2", [P, 1])
        bm = sb("bm", [P, 1])
        lneps = sb("lneps", [P, 1])
        neg1 = sb("neg1", [P, ROWS])
        zrow = sb("zrow", [1, F])
        src = sb("src", [P, NC], I32)
        dst = sb("dst", [P, NC], I32)
        nxt = sb("nxt", [P, NC], I32)
        dstc = sb("dstc", [P, NC], I32)
        posi = sb("posi", [P, NC], I32)
        outi = sb("outi", [P, NC], I32)
        idx2 = sb("idx2", [P, NC], I32)
        idxk = sb("idxk", [P, NC], I32)
        ei = sb("ei", [P, NC], I32)
        ef = sb("ef", [P, NC])
        posf = sb("posf", [P, NC])
        w9 = sb("w9", [P, NC])
        t1 = sb("t1", [P, NC])
        t2 = sb("t2", [P, NC])
        XD = sb("XD", [P, NG * T * F])

        def xd(g):
            return XD[:, bass.ds(g * (T * F), T * F)].rearrange("p (t f) -> p t f", f=F)

        def col(ap, g):
            return ap[:, bass.ds(g * T, T)]

        def rows(table, g, base=0):
            return table[bass.ds(g * GE + base, GE), :].rearrange("(p t) f -> p (t f)", t=T)

        def spread(dc, y, d, q, m, n):
            dc.then(nc.vector.tensor_reduce(m, y, AX.X, ALU.add))
            dc.then(nc.vector.scalar_tensor_tensor(out=d, in0=mid(m, n), scalar=-1.0 / F, in1=y, op0=ALU.mult, op1=ALU.add))
            dc.then(nc.vector.tensor_tensor(q, d, d, ALU.mult))


        with ExitStack() as scope:
            xin = [scope.enter_context(nc.sbuf_tensor(f"xin{b}", [P, ROWS, XW], F32)) for b in range(2)]
            dr = scope.enter_context(nc.sbuf_tensor("dr", [NG, GE], I32))
            dp = scope.enter_context(nc.sbuf_tensor("dp", [NG, GE], I32))
            keepr = scope.enter_context(nc.sbuf_tensor("keepr", [NG, GE], F32))
            penr = scope.enter_context(nc.sbuf_tensor("penr", [NG, GE], F32))
            s_const, s_col, s_chain, s_ei, s_keep = (sem(n) for n in ("s_const", "s_col", "s_chain", "s_ei", "s_keep"))
            s_neg, s_rows, s_zero, s_relu = sem("s_neg"), sem("s_rows"), sem("s_zero"), sem("s_relu")
            s_xin, s_xout = sems("s_xin"), sems("s_xout")
            xv = a["x"][0:P * ROWS * CHUNKS, :].rearrange("(p c r) f -> p c r f", p=P, c=CHUNKS)
            pv = xpos[0:P * ROWS * CHUNKS, :].rearrange("(p c r) f -> p c (r f)", p=P, c=CHUNKS)
            consts = [(ident, "ident"), (rel, "rel"), (bias1, "bias1"), (w1, "w1"), (w2, "w2"),
                      (theta, "thetaT"), (phi, "phiT")]
            wide = [(bias2, "bias2"), (bias3, "theta_b"), (phb, "phi_b"), (eps0, "eps")]
            cols = [(src, "src"), (dst, "dst"), (nxt, "nxt"), (w9, "ew")]
            with nc.Block() as block:
                @block.sync
                def _(sp):
                    for t, n in cols:
                        sp.dma_start(t[:, :], a[n]).then_inc(s_col, 16)
                    sp.dma_start(dr[:, :], a["dst_row"][1:EP + 1].rearrange("(g e) -> g e", e=GE)).then_inc(s_col, 16)
                    sp.dma_start(dp[:, :], a["dst_row"][0:EP].rearrange("(g e) -> g e", e=GE)).then_inc(s_col, 16)
                    for t, n in consts:
                        sp.dma_start(t[:], a[n]).then_inc(s_const, 16)
                    for t, n in wide:
                        sp.dma_start(t[:, :], a[n].partition_broadcast(P)).then_inc(s_const, 16)

                    def load(i, b):
                        wait(sp, s_xout[b], i * 16)
                        sp.dma_start(xin[b][:, :, 0:F], xv[:, bass.ds(i * 2 + b, 1)].rearrange("p c r f -> p (c r) f")).then_inc(s_xin[b], 16)

                    for b in range(2):
                        load(0, b)
                    with sp.Fori(1, CHUNKS // 2) as i:
                        for b in range(2):
                            load(i, b)
                    sp.wait_ge(s_xout[0], 16 * CHUNKS // 2)
                    sp.dma_start(xin[0][0:RP, 0:RR, 0:F], a["x"][N - REST:N, :].rearrange("(p r) f -> p r f", p=RP)).then_inc(s_xin[0], 16)
                    sp.wait_ge(s_keep, 1)
                    sp.dma_start(rows_dram[0:1, :].rearrange("o (g e) -> (o g) e", e=GE), keepr[:, :]).then_inc(s_rows, 16)
                    sp.dma_start(rows_dram[1:2, :].rearrange("o (g e) -> (o g) e", e=GE), penr[:, :]).then_inc(s_rows, 16)
                    sp.wait_ge(s_zero, 1)
                    for k in krylov:
                        sp.dma_start(k[EP:EP + 1, :], zrow[:, :]).then_inc(s_rows, 16)
                    sp.wait_ge(s_rows, 64)
                    sp.wait_ge(s_const, 16 * (len(consts) + len(wide)))

                @block.scalar
                def _(act):
                    act.wait_ge(s_neg, 1)

                    def store(i, b):
                        act.wait_ge(s_xin[b], i * 16 + 16)
                        act.dma_start(pv[:, bass.ds(i * 2 + b, 1)].rearrange("p c w -> p (c w)"), xin[b][:, :, :].rearrange("p r w -> p (r w)")).then_inc(s_xout[b], 16)

                    with act.Fori(0, CHUNKS // 2) as i:
                        for b in range(2):
                            store(i, b)
                    act.wait_ge(s_xin[0], 16 * CHUNKS // 2 + 16)
                    act.dma_start(xpos[N - REST:N, :].rearrange("(p r) w -> p (r w)", p=RP), xin[0][0:RP, 0:RR, :].rearrange("p r w -> p (r w)")).then_inc(s_xout[0], 16)
                    act.wait_ge(s_xout[0], 16 * CHUNKS // 2 + 16)
                    act.wait_ge(s_xout[1], 16 * CHUNKS // 2)

                @block.gpsimd
                def _(pool):
                    nc.gpsimd.iota(ei[:, :], pattern=[[GE, NG + 2], [1, T]], base=0, channel_multiplier=T).then_inc(s_ei, 1)

                @block.vector
                def _(dve):
                    dc = Chain(dve, s_chain, 14).turn(0)
                    for b in range(2):
                        ins = nc.vector.memset(xin[b][:, :, F:XW], -1.0)
                    ins.then_inc(s_neg, 1)
                    nc.vector.memset(lneps[:, :], LN_EPS)
                    nc.vector.memset(zrow[:, :], 0.0).then_inc(s_zero, 1)
                    dve.wait_ge(s_ei, 1)
                    nc.vector.tensor_copy(ef[:, :], ei[:, :])
                    dve.wait_ge(s_col, 16 * 6)
                    nc.vector.tensor_scalar(w9[:, :], w9[:, :], 1.0 - ALPHA, None, ALU.mult)
                    nc.vector.tensor_scalar(dstc[:, :], dst[:, :], N - 1, None, ALU.min)
                    dc.then(nc.vector.tensor_tensor(t1[:, :], dst[:, :], nxt[:, :], ALU.is_equal))
                    dc.then(nc.vector.tensor_scalar(t1[:, :], t1[:, :], FAR, None, ALU.mult))
                    dc.then(nc.vector.tensor_tensor(outi[:, :], t1[:, :], dst[:, :], ALU.add))
                    dc.then(nc.vector.tensor_scalar(t2[:, :], dst[:, :], float(XW), float(F), ALU.mult, ALU.add))
                    dc.then(nc.vector.tensor_tensor(posi[:, :], t1[:, :], t2[:, :], ALU.add))
                    dc.then(nc.vector.tensor_tensor(keepr[:, :], dr[:, :], dp[:, :], ALU.is_equal))
                    nc.vector.tensor_scalar(penr[:, :], keepr[:, :], 1.0, LOW, ALU.subtract, ALU.mult).then_inc(s_keep, 1)
                    dve.wait_ge(s_const, 16 * (len(consts) + len(wide)))
                    dc.then(nc.vector.tensor_scalar(c[:, :], eps0[:, :], 2.0, None, ALU.add))
                    dc.then(nc.vector.tensor_tensor(c2[:, :], c[:, :], c[:, :], ALU.mult))
                    dc.then(nc.vector.tensor_scalar(c2[:, :], c2[:, :], 1.0 / F, None, ALU.mult))
                    dc.then(nc.vector.tensor_scalar(bias2c[:, :], bias2[:, :], 0.0, None, ALU.max))
                    dc.then(nc.vector.tensor_reduce(bm[:, :], bias2c[:, :], AX.X, ALU.add))
                    dc.then(nc.vector.tensor_scalar(bm[:, :], bm[:, :], 1.0 / F, None, ALU.mult))
                    dc.then(nc.vector.tensor_scalar(bias2c[:, :], bias2c[:, :], bm[:, :], None, ALU.subtract))
                    nc.vector.tensor_tensor(bias3[:, :], bias3[:, :], phb[:, :], ALU.add)
                    dc.then(nc.vector.tensor_tensor(pmt[:, :], phi[:, :], theta[:, :], ALU.subtract))
                    dc.last()

        with ExitStack() as scope:
            def sc(name, shape, dt=F32):
                return scope.enter_context(nc.sbuf_tensor(name, shape, dt))
            nx = [sc(f"nx{b}", [P, ROWS, F]) for b in range(2)]
            no = [sc(f"no{b}", [P, ROWS, F]) for b in range(2)]
            nd, nq = sc("nd", [P, ROWS, F]), sc("nq", [P, ROWS, F])
            nm, nv, ns, nr, nu = (sc(n, [P, ROWS]) for n in ("nm", "nv", "ns", "nr", "nu"))
            pidx = [sc(f"pidx{b}", [P, PG * T], I32) for b in range(2)]
            pval = [sc(f"pval{b}", [P, PG * T]) for b in range(2)]
            s_nx, s_st, s_pos = sems("s_nx"), sems("s_st"), sems("s_pos")
            s_nchain, s_out, s_nvar, s_nstd, s_nd, s_nq, s_pstage, s_turn = (
                sem(n) for n in ("s_nchain", "s_out", "s_nvar", "s_nstd", "s_nd", "s_nq", "s_pstage", "s_turn"))
            xv = a["x"][0:P * ROWS * CHUNKS, :].rearrange("(p c r) f -> p c (r f)", p=P, c=CHUNKS)
            ov = out[0:P * ROWS * CHUNKS, :].rearrange("(p c r) f -> p c (r f)", p=P, c=CHUNKS)
            xpos_cells = xpos.rearrange("n (w o) -> (n w) o", o=1)
            with nc.Block() as block:
                @block.sync
                def _(sp):
                    def load(i, b):
                        wait(sp, s_out, i * 2 + b - 1)
                        sp.dma_start(nx[b][:, :, :].rearrange("p r f -> p (r f)"), xv[:, bass.ds(i * 2 + b, 1)].rearrange("p c w -> p (c w)")).then_inc(s_nx[b], 16)

                    def store(i, b):
                        wait(sp, s_out, i * 2 + b + 1)
                        sp.dma_start(ov[:, bass.ds(i * 2 + b, 1)].rearrange("p c w -> p (c w)"), no[b][:, :, :].rearrange("p r f -> p (r f)")).then_inc(s_st[b], 16)

                    for b in range(2):
                        load(0, b)
                    with sp.Fori(1, CHUNKS // 2) as i:
                        for b in range(2):
                            store(i - 1, b)
                            load(i, b)
                    store(CHUNKS // 2 - 1, 0)
                    sp.dma_start(nx[0][0:RP, 0:RR, :], a["x"][N - REST:N, :].rearrange("(p r) f -> p r f", p=RP)).then_inc(s_nx[0], 16)
                    store(CHUNKS // 2 - 1, 1)
                    sp.wait_ge(s_out, CHUNKS + 1)
                    sp.dma_start(out[N - REST:N, :].rearrange("(p r) f -> p r f", p=RP), no[0][0:RP, 0:RR, :]).then_inc(s_st[0], 16)
                    sp.wait_ge(s_st[0], 16 * (CHUNKS // 2 + 1))
                    sp.wait_ge(s_st[1], 16 * (CHUNKS // 2))

                @block.scalar
                def _(act):
                    def root(n, p, r, src_t, scale):
                        act.wait_ge(s_nvar, n + 1)
                        nc.scalar.activation(ns[0:p, 0:r], src_t[0:p, 0:r], ACT.Sqrt, bias=lneps[0:p, :], scale=scale).then_inc(s_nstd, 1)

                    def square(n, p, r):
                        act.wait_ge(s_nd, n + 1)
                        nc.scalar.activation(nq[0:p, 0:r, :], nd[0:p, 0:r, :], ACT.Square).then_inc(s_nq, 1)

                    def work(n, p, r):
                        square(n * 2, p, r)
                        root(n * 4, p, r, nu, c2[0:p, :])
                        root(n * 4 + 1, p, r, nv, (1 + ALPHA) ** 2)
                        square(n * 2 + 1, p, r)
                        root(n * 4 + 2, p, r, nu, 1.0 / F)
                        root(n * 4 + 3, p, r, nv, 1.0 / F)

                    def stage(i, b):
                        w = PG * T
                        wait(act, s_pos[b], i * 16 * w)
                        nc.scalar.copy(pidx[b][:, :], posi[:, bass.ds((i * 2 + b) * w, w)]).then_inc(s_pstage, 1)
                        nc.scalar.copy(pval[b][:, :], ef[:, bass.ds((i * 2 + b) * w, w)]).then_inc(s_pstage, 1)

                    stage(0, 0)
                    stage(0, 1)
                    work(0, P, ROWS)
                    with act.Fori(1, CHUNKS // 2) as i:
                        stage(i, 0)
                        work(i * 2 - 1, P, ROWS)
                        stage(i, 1)
                        work(i * 2, P, ROWS)
                    work(CHUNKS - 1, P, ROWS)
                    work(CHUNKS, RP, RR)

                @block.gpsimd
                def _(pool):
                    bound = pool.to_reg(N * XW - 1)
                    with pool.Fori(0, CHUNKS // 2) as i:
                        for b in range(2):
                            pool.wait_ge(s_pstage, (i * 2 + b) * 2 + 2)
                            pool.sem_inc(s_turn, 1)
                            for t in range(PG * T):
                                nc.gpsimd.indirect_dma_start(
                                    out=xpos_cells, out_offset=bass.IndirectOffsetOnAxis(ap=pidx[b][:, t:t + 1], axis=0),
                                    in_=pval[b][:, t:t + 1], in_offset=None, bounds_check=bound, oob_is_err=False).then_inc(s_pos[b], 16)
                    for b in range(2):
                        pool.wait_ge(s_pos[b], CHUNKS // 2 * 16 * PG * T)

                @block.vector
                def _(dve):
                    dc = Chain(dve, s_nchain, 11)

                    def chunk(n, i, b, p, r):
                        dc.turn(n)
                        x, d, q, o = nx[b][0:p, 0:r, :], nd[0:p, 0:r, :], nq[0:p, 0:r, :], no[b][0:p, 0:r, :]
                        m, v, s, rr, u = (t[0:p, 0:r] for t in (nm, nv, ns, nr, nu))
                        dve.wait_ge(s_nx[b], i * 16 + 16)
                        dc.then(nc.vector.tensor_reduce(m, x, AX.X, ALU.add))
                        nc.vector.scalar_tensor_tensor(out=d, in0=mid(m, r), scalar=-1.0 / F, in1=x, op0=ALU.mult, op1=ALU.add).then_inc(s_nd, 1)
                        dve.wait_ge(s_nq, n * 2 + 1)
                        nc.vector.tensor_reduce(u, q, AX.X, ALU.add).then_inc(s_nvar, 1)
                        dve.wait_ge(s_nvar, n * 4 + 1)
                        dve.wait_ge(s_nstd, n * 4 + 1)
                        dc.then(nc.vector.reciprocal(rr, s))
                        dc.then(nc.vector.scalar_tensor_tensor(out=u, in0=u, scalar=c2[0:p, :], in1=rr, op0=ALU.mult, op1=ALU.mult))
                        nc.vector.tensor_tensor(v, u, rr, ALU.mult).then_inc(s_nvar, 1)
                        dve.wait_ge(s_nvar, n * 4 + 2)
                        dc.then(nc.vector.tensor_scalar(rr, rr, c[0:p, :], None, ALU.mult))
                        dve.wait_ge(s_nstd, n * 4 + 2)
                        dc.then(nc.vector.reciprocal(u, s))
                        dc.then(nc.vector.scalar_tensor_tensor(out=rr, in0=u, scalar=1 + ALPHA, in1=rr, op0=ALU.mult, op1=ALU.mult))
                        dc.then(nc.vector.tensor_tensor(d, d, mid(rr, r), ALU.mult))
                        nc.vector.tensor_tensor(d, d, bias2c[0:p, :].unsqueeze(1).to_broadcast([p, r, F]), ALU.add).then_inc(s_nd, 1)
                        dve.wait_ge(s_nd, n * 2 + 2)
                        dve.wait_ge(s_nq, n * 2 + 2)
                        nc.vector.tensor_reduce(u, q, AX.X, ALU.add).then_inc(s_nvar, 1)
                        dve.wait_ge(s_nvar, n * 4 + 3)
                        dve.wait_ge(s_nstd, n * 4 + 3)
                        dc.then(nc.vector.reciprocal(rr, s))
                        dc.then(nc.vector.tensor_tensor(u, u, rr, ALU.mult))
                        nc.vector.tensor_tensor(v, u, rr, ALU.mult).then_inc(s_nvar, 1)
                        dve.wait_ge(s_nvar, n * 4 + 4)
                        dve.wait_ge(s_nstd, n * 4 + 4)
                        dc.then(nc.vector.reciprocal(u, s))
                        dc.then(nc.vector.tensor_tensor(rr, rr, u, ALU.mult))
                        wait(dve, s_st[b], i * 16)
                        nc.vector.tensor_tensor(o, d, mid(rr, r), ALU.mult).then_inc(s_out, 1)
                        dve.wait_ge(s_out, n + 1)
                        dc.last()

                    for b in range(2):
                        chunk(b, 0, b, P, ROWS)
                    with dve.Fori(1, CHUNKS // 2) as i:
                        for b in range(2):
                            chunk(i * 2 + b, i, b, P, ROWS)
                    chunk(CHUNKS, CHUNKS // 2, 0, RP, RR)

        pe_turn, pool_turn = sem("pe_turn"), sem("pool_turn")

        def slots(name, shape, dt=F32, n=U, scope=ctx):
            return [scope.enter_context(nc.sbuf_tensor(f"{name}{s}", shape, dt)) for s in range(n)]

        gb = slots("gb", [P, T, XW])
        ib = slots("ib", [P, 2 * T], I32)
        kb = slots("kb", [F, GE])
        scan = slots("scan", [F, GE], n=2)
        ey, ed, eq = (sb(n, [P, T, F]) for n in ("ey", "ed", "eq"))
        em, eu, er, es = (sb(n, [P, T]) for n in ("em", "eu", "er", "es"))
        psT = [ctx.enter_context(nc.psum_tensor(f"psT{b}", [F, GE], F32)) for b in range(2)]
        psR = [ctx.enter_context(nc.psum_tensor(f"psR{b}", [P, T, F], F32)) for b in range(2)]
        psH = [ctx.enter_context(nc.psum_tensor(f"psH{q}", [P, GE], F32)) for q in range(RC)]
        psM = ctx.enter_context(nc.psum_tensor("psM", [F, GE], F32))

        def slot(ap, t):
            return ap.rearrange("f (p t) -> f p t", t=T)[:, :, t]

        def keep_row(r, g):
            return rows_dram[r:r + 1, bass.ds(g * GE, GE)].to_broadcast([F, GE])

        def turns(eng, body):
            for s in range(U):
                body(0, s)
            with eng.Fori(1, NT) as i:
                for s in range(U):
                    body(i, s)

        def back(i, s, n):
            return (i, s - n) if s >= n else (i - 1, s - n + U)

        def flat(rows_sb):
            return rows_sb[:, :, :].rearrange("p t f -> p (t f)")

        def to_columns(dst_ps, rows_sb):
            for t in range(T):
                last = nc.tensor.transpose(slot(dst_ps, t), rows_sb[:, t, 0:F], ident[:, :])
            return last

        def to_rows(dst_ps, cols_sb):
            for t in range(T):
                last = nc.tensor.transpose(dst_ps[:, t, :], slot(cols_sb, t), ident[0:F, 0:F])
            return last

        def last_norm(dve, epi, s_var, s_std, g):
            epi.then(nc.vector.tensor_reduce(em[:, :], ey[:, :, :], AX.X, ALU.add))
            epi.then(nc.vector.scalar_tensor_tensor(out=ed[:, :, :], in0=mid(em[:, :], T), scalar=-1.0 / F, in1=ey[:, :, :], op0=ALU.mult, op1=ALU.add))
            epi.then(nc.vector.tensor_tensor(eq[:, :, :], ed[:, :, :], ed[:, :, :], ALU.mult))
            nc.vector.tensor_reduce(eu[:, :], eq[:, :, :], AX.X, ALU.add).then_inc(s_var, 1)
            dve.wait_ge(s_std, g + 1)
            epi.then(nc.vector.reciprocal(er[:, :], es[:, :]))

        def gather(s, table, width, col0=0, dst=None):
            dst = gb if dst is None else dst
            for t in range(T):
                yield nc.gpsimd.indirect_dma_start(
                    out=dst[s][:, t, 0:width], out_offset=None, in_=table,
                    in_offset=bass.IndirectOffsetOnAxis(ap=ib[s][:, col0 + t:col0 + t + 1], axis=0))

        with ExitStack() as scope:
            def sp2(name, n=2):
                return slots(name, [P, T, F], n=n, scope=scope)
            xdb, efb = sp2("xdb", U), sp2("efb", U)
            msg, act0, x1s, x2s, x3s = (sp2(n) for n in ("msg0_", "act0_", "x1s", "x2s", "x3s"))
            ld, lq = (scope.enter_context(nc.sbuf_tensor(n, [P, T, F], F32)) for n in ("ld", "lq"))
            lm, lu, lv, lr, lw, ls = (scope.enter_context(nc.sbuf_tensor(n, [P, T], F32)) for n in ("lm", "lu", "lv", "lr", "lw", "ls"))
            s_g, s_ef, s_kb = ([sem(f"a_{n}{s}") for s in range(U)] for n in ("g", "ef", "kb"))
            s_s1, s_s2, s_s3, s_x1 = (sems(n) for n in ("a_s1", "a_s2", "a_s3", "a_x1"))
            (s_stage, s_add, s_relu, s_cols, s_scan, s_rows, s_lone, s_epi, s_src, s_posf, s_self, s_xd, s_sum, s_lvar, s_lstd,
             s_evar, s_estd, s_x1s) = (sem(f"a_{n}") for n in (
                 "stage", "add", "relu", "cols", "scan", "rows", "lone", "epi", "src", "posf", "self", "xd", "sum",
                 "lvar", "lstd", "evar", "estd", "x1s"))
            with nc.Block() as block:
                @block.sync
                def _(sp):
                    def load(i, s):
                        g = i * U + s
                        wait(sp, s_add, g - U + 1)
                        sp.dma_start(flat(efb[s]), a["edge"][:, bass.ds(g * T * F, T * F)]).then_inc(s_ef[s], 16)
                        wait(sp, s_scan, g - U + 1)
                        sp.dma_start(kb[s][:, :], keep_row(0, g)).then_inc(s_kb[s], 16)

                    def store(i, s):
                        g, b = i * U + s, s % 2
                        sp.wait_ge(s_src, g + 1)
                        for buf, k, done in ((x1s, 1, s_s1), (x2s, 2, s_s2), (x3s, 3, s_s3)):
                            sp.dma_start(rows(layer[k], g, EP), flat(buf[b])).then_inc(done[b], 16)

                    def store_x1(i, s):
                        g = i * U + s
                        sp.wait_ge(s_xd, g + 1)
                        sp.dma_start(rows(layer[1], g), XD[:, bass.ds(g * T * F, T * F)]).then_inc(s_x1[s % 2], 16)

                    def body(i, s):
                        load(i, s)
                        if not (isinstance(i, int) and s < 1):
                            store(*back(i, s, 1))
                        if not (isinstance(i, int) and s < 3):
                            store_x1(*back(i, s, 3))

                    turns(sp, body)
                    store(NT - 1, U - 1)
                    for s in range(1, U):
                        store_x1(NT - 1, s)
                    for b in range(2):
                        for done in (s_s1, s_s2, s_s3, s_x1):
                            sp.wait_ge(done[b], 16 * NG // 2)

                @block.scalar
                def _(act):
                    def stage(i, s):
                        g = i * U + s
                        wait(act, s_g[s], i * 32 * T)
                        nc.scalar.copy(ib[s][:, 0:T], col(src, g)).then_inc(s_stage, 1)
                        nc.scalar.copy(ib[s][:, T:2 * T], col(dstc, g)).then_inc(s_stage, 1)

                    def root(s_in, n, s_done, to, of, scale):
                        act.wait_ge(s_in, n + 1)
                        nc.scalar.activation(to[:, :], of[:, :], ACT.Sqrt, bias=lneps[:, :], scale=scale).then_inc(s_done, 1)

                    def body(i, s):
                        g, b = i * U + s, s % 2
                        stage(i + (s + 2) // U, (s + 2) % U)
                        act.wait_ge(s_add, g + 1)
                        wait(act, s_cols, g - 1)
                        nc.scalar.activation(act0[b][:, :, :], msg[b][:, :, :], ACT.Relu).then_inc(s_relu, 1)
                        nc.scalar.copy(col(posf, g), gb[s][:, :, F]).then_inc(s_posf, 1)
                        root(s_lvar, g * 3, s_lstd, ls, lu, c2[:, :])
                        if not (isinstance(i, int) and s < 1):
                            root(s_evar, g - 1, s_estd, es, eu, 1.0 / F)
                        root(s_lvar, g * 3 + 1, s_lstd, ls, lv, (1 + ALPHA) ** 2)
                        root(s_lvar, g * 3 + 2, s_lstd, ls, lu, 1.0 / F)

                    stage(0, 0)
                    stage(0, 1)
                    turns(act, body)
                    root(s_evar, NG - 1, s_estd, es, eu, 1.0 / F)

                @block.gpsimd
                def _(pool):
                    def body(i, s):
                        g = i * U + s
                        wait(pool, s_posf, g - U + 1)
                        wait(pool, s_lvar, 3 * (g - U) + 1)
                        wait(pool, s_self, g - U + 1)
                        pool.wait_ge(s_stage, (g + 1) * 2)
                        pool.sem_inc(pool_turn, 1)
                        for ins in gather(s, xpos, XW):
                            ins.then_inc(s_g[s], 16)
                        for ins in gather(s, a["x"], F, T, xdb):
                            ins.then_inc(s_g[s], 16)

                    turns(pool, body)

                @block.tensor
                def _(pe):
                    def body(i, s):
                        g, b = i * U + s, s % 2
                        pe.wait_ge(s_relu, g + 1)
                        wait(pe, s_scan, g - 1)
                        pe.sem_inc(pe_turn, 1)
                        to_columns(psT[b], act0[b]).then_inc(s_cols, 1)
                        pe.wait_ge(s_scan, g + 1)
                        wait(pe, s_sum, g - 1)
                        pe.sem_inc(pe_turn, 1)
                        to_rows(psR[b], scan[b]).then_inc(s_rows, 1)

                    turns(pe, body)

                @block.vector
                def _(dve):
                    lone, epi = Chain(dve, s_lone, 12), Chain(dve, s_epi, 4)

                    def run_end(i, s):
                        g = i * U + s
                        epi.turn(g)
                        dve.wait_ge(s_rows, g + 1)
                        nc.vector.tensor_tensor(ey[:, :, :], psR[s % 2][:, :, :], xd(g), ALU.add).then_inc(s_sum, 1)
                        dve.wait_ge(s_sum, g + 1)
                        spread(epi, ey[:, :, :], ed[:, :, :], eq[:, :, :], em[:, :], T)
                        nc.vector.tensor_reduce(eu[:, :], eq[:, :, :], AX.X, ALU.add).then_inc(s_evar, 1)

                    def run_end_x1(i, s):
                        g = i * U + s
                        dve.wait_ge(s_estd, g + 1)
                        epi.then(nc.vector.reciprocal(er[:, :], es[:, :]))
                        nc.vector.tensor_tensor(xd(g), ed[:, :, :], mid(er[:, :], T), ALU.mult).then_inc(s_xd, 1)
                        epi.last()

                    def body(i, s):
                        g, b = i * U + s, s % 2
                        first = isinstance(i, int) and s < 1
                        lone.turn(g)
                        dve.wait_ge(s_g[s], (i + 1) * 32 * T)
                        dve.wait_ge(s_ef[s], (i + 1) * 16)
                        wait(dve, s_relu, g - 1)
                        nc.vector.tensor_tensor(msg[b][:, :, :], gb[s][:, :, 0:F], efb[s][:, :, :], ALU.add).then_inc(s_add, 1)
                        nc.vector.tensor_scalar(xd(g), xdb[s][:, :, :], c[:, :], None, ALU.mult).then_inc(s_self, 1)
                        spread(lone, gb[s][:, :, 0:F], ld[:, :, :], lq[:, :, :], lm[:, :], T)
                        nc.vector.tensor_reduce(lu[:, :], lq[:, :, :], AX.X, ALU.add).then_inc(s_lvar, 1)
                        if not first:
                            run_end(*back(i, s, 1))
                        dve.wait_ge(s_lvar, g * 3 + 1)
                        dve.wait_ge(s_lstd, g * 3 + 1)
                        lone.then(nc.vector.reciprocal(lr[:, :], ls[:, :]))
                        lone.then(nc.vector.scalar_tensor_tensor(out=lu[:, :], in0=lu[:, :], scalar=c2[:, :], in1=lr[:, :], op0=ALU.mult, op1=ALU.mult))
                        nc.vector.tensor_tensor(lv[:, :], lu[:, :], lr[:, :], ALU.mult).then_inc(s_lvar, 1)
                        dve.wait_ge(s_lvar, g * 3 + 2)
                        lone.then(nc.vector.tensor_scalar(lr[:, :], lr[:, :], c[:, :], None, ALU.mult))
                        for done in (s_s1, s_s2, s_s3):
                            wait(dve, done[b], 16 * (i * 2 + s // 2))
                        nc.vector.tensor_tensor(x1s[b][:, :, :], ld[:, :, :], mid(lr[:, :], T), ALU.mult).then_inc(s_x1s, 1)
                        if not first:
                            run_end_x1(*back(i, s, 1))
                        dve.wait_ge(s_lstd, g * 3 + 2)
                        dve.wait_ge(s_x1s, g + 1)
                        lone.then(nc.vector.reciprocal(lw[:, :], ls[:, :]))
                        lone.then(nc.vector.scalar_tensor_tensor(out=lr[:, :], in0=lw[:, :], scalar=1 + ALPHA, in1=lr[:, :], op0=ALU.mult, op1=ALU.mult))
                        lone.then(nc.vector.tensor_tensor(x2s[b][:, :, :], ld[:, :, :], mid(lr[:, :], T), ALU.mult))
                        lone.then(nc.vector.tensor_tensor(ld[:, :, :], x2s[b][:, :, :], bias2c[:, :].unsqueeze(1).to_broadcast([P, T, F]), ALU.add))
                        lone.then(nc.vector.tensor_tensor(lq[:, :, :], ld[:, :, :], ld[:, :, :], ALU.mult))
                        nc.vector.tensor_reduce(lu[:, :], lq[:, :, :], AX.X, ALU.add).then_inc(s_lvar, 1)
                        dve.wait_ge(s_cols, g + 1)
                        dve.wait_ge(s_kb[s], (i + 1) * 16)
                        wait(dve, s_rows, g - 1)
                        wait(dve, s_scan, g)
                        start = 0.0 if first else scan[1 - b][:, GE - 1:GE]
                        nc.vector.tensor_tensor_scan(scan[b][:, :], kb[s][:, :], psT[b][:, :], start, ALU.mult, ALU.add).then_inc(s_scan, 1)
                        dve.wait_ge(s_lvar, g * 3 + 3)
                        dve.wait_ge(s_lstd, g * 3 + 3)
                        lone.then(nc.vector.reciprocal(lr[:, :], ls[:, :]))
                        nc.vector.tensor_tensor(x3s[b][:, :, :], ld[:, :, :], mid(lr[:, :], T), ALU.mult).then_inc(s_src, 1)
                        dve.wait_ge(s_src, g + 1)
                        lone.last()

                    turns(dve, body)
                    run_end(NT - 1, U - 1)
                    run_end_x1(NT - 1, U - 1)

        with ExitStack() as scope:
            s_idx = sem("s_idx")
            with nc.Block() as block:
                @block.vector
                def _(dve):
                    dc = Chain(dve, s_idx, 7).turn(0)
                    W = NG * T
                    own, end, has, far = ef[:, 0:W], posf[:, 0:W], t1[:, 0:W], t2[:, 0:W]
                    dc.then(nc.vector.tensor_scalar(has, end, 0.0, None, ALU.is_ge))
                    dc.then(nc.vector.tensor_scalar(own, own, float(EP), None, ALU.add))
                    dc.then(nc.vector.tensor_tensor(far, end, own, ALU.subtract))
                    dc.then(nc.vector.tensor_tensor(far, far, has, ALU.mult))
                    dc.then(nc.vector.tensor_tensor(idx2[:, 0:W], far, own, ALU.add))
                    dc.then(nc.vector.scalar_tensor_tensor(out=far, in0=end, scalar=float(EP), in1=has, op0=ALU.subtract, op1=ALU.mult))
                    nc.vector.tensor_scalar(idxk[:, 0:W], far, float(EP), None, ALU.add)
                    nc.vector.memset(idx2[:, W:NC], 0)
                    dc.then(nc.vector.memset(idxk[:, W:NC], 0))
                    dc.last()

        with ExitStack() as scope:
            rb, msg = (slots(n, [P, T, F], n=2, scope=scope) for n in ("rb", "msg"))
            s_g, s_kb = ([sem(f"b_{n}{s}") for s in range(U)] for n in ("g", "kb"))
            s_rst, s_x2 = sems("b_rst"), sems("b_x2")
            (s_stage, s_msg, s_cols, s_scan, s_rows, s_rb, s_acc, s_epi, s_xd, s_var, s_std, s_two) = (
                sem(f"b_{n}") for n in ("stage", "msg", "cols", "scan", "rows", "rb", "acc", "epi", "xd", "var", "std", "two"))
            LAST = STEPS - 1

            def passes(eng, one):
                one(0, layer[1], krylov[0])
                with eng.Fori(0, (STEPS - 2) // 2) as j:
                    for h in range(2):
                        one(j * 2 + (1 + h), krylov[h], krylov[1 - h])
                one(LAST, krylov[0], None)

            with nc.Block() as block:
                @block.sync
                def _(sp):
                    def one(k, _, target):
                        def load(i, s):
                            wait(sp, s_scan, k * NG + i * U + s - U + 1)
                            sp.dma_start(kb[s][:, :], keep_row(0, i * U + s)).then_inc(s_kb[s], 16)

                        def store(i, s):
                            g, b = i * U + s, s % 2
                            if target is None:
                                sp.wait_ge(s_xd, g + 1)
                                sp.dma_start(rows(layer[2], g), XD[:, bass.ds(g * T * F, T * F)]).then_inc(s_x2[b], 16)
                            else:
                                sp.wait_ge(s_rb, k * NG + g + 1)
                                sp.dma_start(rows(target, g), flat(rb[b])).then_inc(s_rst[b], 16)

                        def body(i, s):
                            load(i, s)
                            if not (isinstance(i, int) and s < 2):
                                store(*back(i, s, 2))

                        turns(sp, body)
                        store(NT - 1, U - 2)
                        store(NT - 1, U - 1)

                    passes(sp, one)
                    for b in range(2):
                        sp.wait_ge(s_rst[b], 16 * NG // 2 * LAST)
                        sp.wait_ge(s_x2[b], 16 * NG // 2)

                @block.scalar
                def _(act):
                    def one(k, _, target):
                        idx = idx2 if isinstance(k, int) and k == 0 else idxk

                        def stage(i, s):
                            wait(act, s_g[s], (k * NT + i) * 16 * T)
                            nc.scalar.copy(ib[s][:, 0:T], col(idx, i * U + s)).then_inc(s_stage, 1)

                        def body(i, s):
                            b = s % 2
                            n = k * NG + i * U + s
                            stage(i + (s + 2) // U, (s + 2) % U)
                            act.wait_ge(s_rows, n + 1)
                            if target is not None:
                                wait(act, s_rst[b], (k * (NG // 2) + i * 2 + s // 2) * 16)
                                wait(act, s_acc, n - 1)
                                nc.scalar.copy(rb[b][:, :, :], psR[b][:, :, :]).then_inc(s_rb, 1)
                            else:
                                act.wait_ge(s_var, i * U + s + 1)
                                nc.scalar.activation(es[:, :], eu[:, :], ACT.Sqrt, bias=lneps[:, :], scale=1.0 / F).then_inc(s_std, 1)

                        wait(act, s_stage, k * (NG + 2))
                        stage(0, 0)
                        stage(0, 1)
                        turns(act, body)

                    passes(act, one)

                @block.gpsimd
                def _(pool):
                    def one(k, source, _):
                        def body(i, s):
                            g = i * U + s
                            wait(pool, s_msg, k * NG + g - U + 1)
                            pool.wait_ge(s_stage, k * (NG + 2) + g + 1)
                            pool.sem_inc(pool_turn, 1)
                            for ins in gather(s, source, F):
                                ins.then_inc(s_g[s], 16)

                        for b in range(2):
                            wait(pool, s_rst[b], k * (NG // 2) * 16)
                        turns(pool, body)

                    passes(pool, one)

                @block.tensor
                def _(pe):
                    def one(k, _, target):
                        def body(i, s):
                            b = s % 2
                            n = k * NG + i * U + s
                            pe.wait_ge(s_msg, n + 1)
                            wait(pe, s_scan, n - 1)
                            pe.sem_inc(pe_turn, 1)
                            to_columns(psT[b], msg[b]).then_inc(s_cols, 1)
                            pe.wait_ge(s_scan, n + 1)
                            if target is not None:
                                wait(pe, s_rb, n - 1)
                            else:
                                wait(pe, s_rb, LAST * NG)
                                wait(pe, s_acc, n - 1)
                            pe.sem_inc(pe_turn, 1)
                            to_rows(psR[b], scan[b]).then_inc(s_rows, 1)

                        turns(pe, body)

                    passes(pe, one)

                @block.vector
                def _(dve):
                    epi = Chain(dve, s_epi, 4)

                    def one(k, _, target):
                        first_pass = isinstance(k, int) and k == 0

                        def epilogue(i, s):
                            g, b = i * U + s, s % 2
                            if target is not None:
                                if first_pass:
                                    dve.wait_ge(s_two, g + 1)
                                dve.wait_ge(s_rb, k * NG + g + 1)
                                nc.vector.scalar_tensor_tensor(out=xd(g), in0=rb[b][:, :, :], scalar=ALPHA, in1=xd(g), op0=ALU.mult, op1=ALU.add).then_inc(s_acc, 1)
                                return
                            dve.wait_ge(s_rows, k * NG + g + 1)
                            nc.vector.tensor_tensor(ey[:, :, :], psR[b][:, :, :], xd(g), ALU.add).then_inc(s_acc, 1)
                            dve.wait_ge(s_acc, k * NG + g + 1)
                            epi.turn(g)
                            last_norm(dve, epi, s_var, s_std, g)
                            nc.vector.tensor_tensor(xd(g), ed[:, :, :], mid(er[:, :], T), ALU.mult).then_inc(s_xd, 1)
                            epi.last()

                        def body(i, s):
                            g, b = i * U + s, s % 2
                            n = k * NG + g
                            first = isinstance(i, int) and s < 1
                            dve.wait_ge(s_g[s], (k * NT + i + 1) * 16 * T)
                            wait(dve, s_cols, n - 1)
                            nc.vector.tensor_tensor(msg[b][:, :, :], gb[s][:, :, 0:F], mid(col(w9, g), T), ALU.mult).then_inc(s_msg, 1)
                            if first_pass:
                                nc.vector.tensor_scalar(xd(g), xd(g), 1 + ALPHA, None, ALU.mult).then_inc(s_two, 1)
                            if not first:
                                epilogue(*back(i, s, 1))
                            dve.wait_ge(s_cols, n + 1)
                            dve.wait_ge(s_kb[s], (k * NT + i + 1) * 16)
                            wait(dve, s_rows, n - 1)
                            wait(dve, s_scan, n)
                            start = 0.0 if first else scan[1 - b][:, GE - 1:GE]
                            nc.vector.tensor_tensor_scan(scan[b][:, :], kb[s][:, :], psT[b][:, :], start, ALU.mult, ALU.add).then_inc(s_scan, 1)

                        turns(dve, body)
                        epilogue(NT - 1, U - 1)

                    passes(dve, one)

        with ExitStack() as scope:
            tb, nb = slots("tb", [P, GE], I32, scope=scope), slots("nb", [F, GE], scope=scope)
            xT = slots("xT", [F, GE], n=2, scope=scope)
            h1 = slots("h1", [P, GE], n=RC, scope=scope)
            hm = [slots(f"hm{b}", [P, GE], n=RC, scope=scope) for b in range(2)]
            mw = scope.enter_context(nc.sbuf_tensor("mw", [F, GE], F32))
            s_g, s_kb, s_tb, s_nb = ([sem(f"c_{n}{s}") for s in range(U)] for n in ("g", "kb", "tb", "nb"))
            s_x3 = sems("c_x3")
            (s_stage, s_cols, s_xT, s_h, s_h1, s_hm, s_m, s_mw, s_scan, s_rows, s_sum, s_epi, s_xd, s_var, s_std) = (
                sem(f"c_{n}") for n in ("stage", "cols", "xT", "h", "h1", "hm", "m", "mw", "scan", "rows", "sum", "epi",
                                        "xd", "var", "std"))
            with nc.Block() as block:
                @block.sync
                def _(sp):
                    def load(i, s):
                        g = i * U + s
                        wait(sp, s_hm, RC * (g - U + 1))
                        sp.dma_start(tb[s][:, :], a["type_row"][bass.ds(g * GE, GE)].partition_broadcast(P)).then_inc(s_tb[s], 16)
                        wait(sp, s_mw, g - U + 1)
                        sp.dma_start(nb[s][:, :], a["norm_row"][bass.ds(g * GE, GE)].partition_broadcast(F)).then_inc(s_nb[s], 16)
                        wait(sp, s_scan, g - U + 1)
                        sp.dma_start(kb[s][:, :], keep_row(0, g)).then_inc(s_kb[s], 16)

                    def store(i, s):
                        g = i * U + s
                        sp.wait_ge(s_xd, g + 1)
                        sp.dma_start(rows(layer[3], g), XD[:, bass.ds(g * T * F, T * F)]).then_inc(s_x3[s % 2], 16)

                    def body(i, s):
                        load(i, s)
                        if not isinstance(i, int):
                            store(i - 1, s)

                    turns(sp, body)
                    for s in range(U):
                        store(NT - 1, s)
                    for b in range(2):
                        sp.wait_ge(s_x3[b], 16 * NG // 2)

                @block.scalar
                def _(act):
                    def stage(i, s):
                        wait(act, s_g[s], i * 16 * T)
                        nc.scalar.copy(ib[s][:, 0:T], col(idx2, i * U + s)).then_inc(s_stage, 1)

                    def root(g):
                        act.wait_ge(s_var, g + 1)
                        nc.scalar.activation(es[:, :], eu[:, :], ACT.Sqrt, bias=lneps[:, :], scale=1.0 / F).then_inc(s_std, 1)

                    def body(i, s):
                        g, b = i * U + s, s % 2
                        stage(i + (s + 2) // U, (s + 2) % U)
                        act.wait_ge(s_cols, g + 1)
                        wait(act, s_h, RC * (g - 1))
                        nc.scalar.copy(xT[b][:, :], psT[b][:, :]).then_inc(s_xT, 1)
                        for q in range(RC):
                            act.wait_ge(s_h, RC * g + q + 1)
                            wait(act, s_hm, RC * (g - 1) + q + 1)
                            nc.scalar.activation(h1[q][:, :], psH[q][:, :], ACT.Relu, bias=bias1[:, q:q + 1]).then_inc(s_h1, 1)
                        if not (isinstance(i, int) and s < 2):
                            root(g - 2)

                    stage(0, 0)
                    stage(0, 1)
                    turns(act, body)
                    root(NG - 2)
                    root(NG - 1)

                @block.gpsimd
                def _(pool):
                    def body(i, s):
                        g = i * U + s
                        wait(pool, s_cols, g - U + 1)
                        pool.wait_ge(s_stage, g + 1)
                        pool.sem_inc(pool_turn, 1)
                        for ins in gather(s, layer[2], F):
                            ins.then_inc(s_g[s], 16)

                    turns(pool, body)

                @block.tensor
                def _(pe):
                    def second(i, s):
                        g = i * U + s
                        wait(pe, s_mw, g)
                        for q in range(RC):
                            pe.wait_ge(s_hm, RC * g + q + 1)
                            last = nc.tensor.matmul(psM[:, :], w2[:, q, :], hm[s % 2][q][:, :], start=q == 0, stop=q == RC - 1)
                        last.then_inc(s_m, 1)

                    def sums(i, s):
                        g = i * U + s
                        pe.wait_ge(s_scan, g + 1)
                        wait(pe, s_sum, g - 1)
                        pe.sem_inc(pe_turn, 1)
                        to_rows(psR[s % 2], scan[s % 2]).then_inc(s_rows, 1)

                    def body(i, s):
                        g, b = i * U + s, s % 2
                        pe.wait_ge(s_g[s], (i + 1) * 16 * T)
                        wait(pe, s_xT, g - 1)
                        pe.sem_inc(pe_turn, 1)
                        to_columns(psT[b], gb[s]).then_inc(s_cols, 1)
                        if not (isinstance(i, int) and s < 1):
                            second(*back(i, s, 1))
                        pe.wait_ge(s_xT, g + 1)
                        for q in range(RC):
                            wait(pe, s_h1, RC * (g - 1) + q + 1)
                            nc.tensor.matmul(psH[q][:, :], w1[:, q * P:(q + 1) * P], xT[b][:, :], start=True, stop=True).then_inc(s_h, 1)
                        if not (isinstance(i, int) and s < 1):
                            sums(*back(i, s, 1))

                    turns(pe, body)
                    second(NT - 1, U - 1)
                    sums(NT - 1, U - 1)

                @block.vector
                def _(dve):
                    epi = Chain(dve, s_epi, 5)

                    def epilogue(i, s):
                        g = i * U + s
                        epi.turn(g)
                        dve.wait_ge(s_rows, g + 1)
                        nc.vector.tensor_tensor(ey[:, :, :], psR[s % 2][:, :, :], bias2[:, :].unsqueeze(1).to_broadcast([P, T, F]), ALU.add).then_inc(s_sum, 1)
                        dve.wait_ge(s_sum, g + 1)
                        epi.then(nc.vector.scalar_tensor_tensor(out=ey[:, :, :], in0=ey[:, :, :], scalar=0.0, in1=xd(g), op0=ALU.max, op1=ALU.add))
                        last_norm(dve, epi, s_var, s_std, g)
                        nc.vector.tensor_tensor(xd(g), ed[:, :, :], mid(er[:, :], T), ALU.mult).then_inc(s_xd, 1)
                        epi.last()

                    def add_up(i, s):
                        g, b = i * U + s, s % 2
                        first = isinstance(i, int) and g == 0
                        dve.wait_ge(s_m, g + 1)
                        dve.wait_ge(s_nb[s], (i + 1) * 16)
                        wait(dve, s_scan, g)
                        nc.vector.tensor_tensor(mw[:, :], psM[:, :], nb[s][:, :], ALU.mult).then_inc(s_mw, 1)
                        dve.wait_ge(s_mw, g + 1)
                        dve.wait_ge(s_kb[s], (i + 1) * 16)
                        wait(dve, s_rows, g - 1)
                        start = 0.0 if first else scan[1 - b][:, GE - 1:GE]
                        nc.vector.tensor_tensor_scan(scan[b][:, :], kb[s][:, :], mw[:, :], start, ALU.mult, ALU.add).then_inc(s_scan, 1)

                    def body(i, s):
                        g, b = i * U + s, s % 2
                        if not (isinstance(i, int) and s < 1):
                            add_up(*back(i, s, 1))
                        dve.wait_ge(s_tb[s], (i + 1) * 16)
                        wait(dve, s_m, g - 1)
                        for q in range(RC):
                            dve.wait_ge(s_h1, RC * g + q + 1)
                            nc.vector.scalar_tensor_tensor(out=hm[b][q][:, :], in0=tb[s][:, :], scalar=rel[:, q:q + 1], in1=h1[q][:, :], op0=ALU.is_equal, op1=ALU.mult).then_inc(s_hm, 1)
                        if not (isinstance(i, int) and s < 2):
                            epilogue(*back(i, s, 2))

                    turns(dve, body)
                    add_up(NT - 1, U - 1)
                    epilogue(NT - 1, U - 2)
                    epilogue(NT - 1, U - 1)

        with ExitStack() as scope:
            dT, xT = slots("dT", [F, GE], n=2, scope=scope), slots("xT3", [F, GE], n=2, scope=scope)
            xdb, xo = (slots(n, [P, T, F], scope=scope) for n in ("xdb3", "xo"))
            ob = slots("ob", [P, T], I32, scope=scope)
            psD = psH[0][0:F, :]
            s_g, s_kb, s_o = ([sem(f"d_{n}{s}") for s in range(U)] for n in ("g", "kb", "o"))
            (s_stage, s_own, s_cols, s_dcols, s_xT, s_dT, s_e, s_scan, s_rows, s_sum, s_epi, s_xo, s_var, s_std,
             s_obs) = (sem(f"d_{n}") for n in ("stage", "own", "cols", "dcols", "xT", "dT", "e", "scan", "rows", "sum",
                                               "epi", "xo", "var", "std", "obs"))
            with nc.Block() as block:
                @block.sync
                def _(sp):
                    def load(i, s):
                        g = i * U + s
                        wait(sp, s_scan, g - U + 1)
                        sp.dma_start(kb[s][:, :], keep_row(1, g)).then_inc(s_kb[s], 16)

                    turns(sp, load)

                @block.scalar
                def _(act):
                    def stage(i, s):
                        wait(act, s_g[s], i * 16 * T)
                        nc.scalar.copy(ib[s][:, 0:T], col(idx2, i * U + s)).then_inc(s_stage, 1)

                    def root(g):
                        act.wait_ge(s_var, g + 1)
                        nc.scalar.activation(es[:, :], eu[:, :], ACT.Sqrt, bias=lneps[:, :], scale=1.0 / F).then_inc(s_std, 1)

                    def body(i, s):
                        g, b = i * U + s, s % 2
                        stage(i + (s + 2) // U, (s + 2) % U)
                        wait(act, s_dcols, g - U + 1)
                        wait(act, s_sum, g - U + 1)
                        nc.scalar.copy(xdb[s][:, :, :], xd(g)).then_inc(s_own, 1)
                        wait(act, s_o[s], i * 16 * T)
                        nc.scalar.copy(ob[s][:, :], col(outi, g)).then_inc(s_obs, 1)
                        act.wait_ge(s_cols, g + 1)
                        wait(act, s_e, g - 1)
                        nc.scalar.copy(xT[b][:, :], psT[b][:, :]).then_inc(s_xT, 1)
                        act.wait_ge(s_dcols, g + 1)
                        wait(act, s_rows, g - 1)
                        nc.scalar.copy(dT[b][:, :], psD).then_inc(s_dT, 1)
                        if not (isinstance(i, int) and s < 2):
                            root(g - 2)

                    stage(0, 0)
                    stage(0, 1)
                    turns(act, body)
                    root(NG - 2)
                    root(NG - 1)

                @block.gpsimd
                def _(pool):
                    bound = pool.to_reg(N - 1)

                    def fetch(i, s):
                        g = i * U + s
                        wait(pool, s_cols, g - U + 1)
                        pool.wait_ge(s_stage, g + 1)
                        pool.sem_inc(pool_turn, 1)
                        for ins in gather(s, layer[3], F):
                            ins.then_inc(s_g[s], 16)

                    def scatter(i, s):
                        g = i * U + s
                        pool.wait_ge(s_xo, g + 1)
                        pool.wait_ge(s_obs, g + 1)
                        pool.sem_inc(pool_turn, 1)
                        for t in range(T):
                            nc.gpsimd.indirect_dma_start(
                                out=out, out_offset=bass.IndirectOffsetOnAxis(ap=ob[s][:, t:t + 1], axis=0),
                                in_=xo[s][:, t, :], in_offset=None, bounds_check=bound, oob_is_err=False).then_inc(s_o[s], 16)

                    def body(i, s):
                        fetch(i, s)
                        if not (isinstance(i, int) and s < 3):
                            scatter(*back(i, s, 3))

                    turns(pool, body)
                    for s in range(1, U):
                        scatter(NT - 1, s)
                    for s in range(U):
                        pool.wait_ge(s_o[s], NT * 16 * T)

                @block.tensor
                def _(pe):
                    def total(i, s):
                        g, b = i * U + s, s % 2
                        pe.wait_ge(s_dT, g + 1)
                        pe.wait_ge(s_scan, g + 1)
                        wait(pe, s_sum, g - 1)
                        pe.sem_inc(pe_turn, 1)
                        for t in range(T):
                            nc.tensor.matmul(psR[b][:, t, :], slot(scan[b], t), ident[0:F, 0:F], start=True, stop=False)
                            last = nc.tensor.matmul(psR[b][:, t, :], slot(dT[b], t), theta[:, :], start=False, stop=True)
                        last.then_inc(s_rows, 1)

                    def body(i, s):
                        g, b = i * U + s, s % 2
                        pe.wait_ge(s_own, g + 1)
                        wait(pe, s_dT, g)
                        pe.sem_inc(pe_turn, 1)
                        to_columns(psD, xdb[s]).then_inc(s_dcols, 1)
                        pe.wait_ge(s_g[s], (i + 1) * 16 * T)
                        wait(pe, s_xT, g - 1)
                        pe.sem_inc(pe_turn, 1)
                        to_columns(psT[b], gb[s]).then_inc(s_cols, 1)
                        if not (isinstance(i, int) and s < 1):
                            total(*back(i, s, 1))
                        pe.wait_ge(s_xT, g + 1)
                        wait(pe, s_scan, g)
                        pe.sem_inc(pe_turn, 1)
                        nc.tensor.matmul(psM[:, :], pmt[:, :], xT[b][:, :], start=True, stop=True).then_inc(s_e, 1)

                    turns(pe, body)
                    total(NT - 1, U - 1)

                @block.vector
                def _(dve):
                    epi = Chain(dve, s_epi, 5)

                    def epilogue(i, s):
                        g = i * U + s
                        epi.turn(g)
                        dve.wait_ge(s_rows, g + 1)
                        epi.then(nc.vector.tensor_tensor(ey[:, :, :], psR[s % 2][:, :, :], bias3[:, :].unsqueeze(1).to_broadcast([P, T, F]), ALU.add))
                        nc.vector.tensor_tensor(ey[:, :, :], ey[:, :, :], xdb[s][:, :, :], ALU.add).then_inc(s_sum, 1)
                        dve.wait_ge(s_sum, g + 1)
                        last_norm(dve, epi, s_var, s_std, g)
                        wait(dve, s_o[s], i * 16 * T)
                        nc.vector.tensor_tensor(xo[s][:, :, :], ed[:, :, :], mid(er[:, :], T), ALU.mult).then_inc(s_xo, 1)
                        epi.last()

                    def body(i, s):
                        g, b = i * U + s, s % 2
                        first = isinstance(i, int) and s < 1
                        dve.wait_ge(s_e, g + 1)
                        dve.wait_ge(s_kb[s], (i + 1) * 16)
                        wait(dve, s_rows, g - 1)
                        wait(dve, s_scan, g)
                        start = 0.0 if first else scan[1 - b][:, GE - 1:GE]
                        nc.vector.tensor_tensor_scan(scan[b][:, :], kb[s][:, :], psM[:, :], start, ALU.add, ALU.max).then_inc(s_scan, 1)
                        if not (isinstance(i, int) and s < 2):
                            epilogue(*back(i, s, 2))

                    turns(dve, body)
                    epilogue(NT - 1, U - 2)
                    epilogue(NT - 1, U - 1)


def kernel(**inputs):
    import numpy as np
    import concourse.bacc as bacc
    from concourse.bass_utils import run_bass_kernel_spmd

    given = {k: np.ascontiguousarray(np.asarray(v)) for k, v in inputs.items()}

    def padded(v, n, fill):
        return np.concatenate([v, np.full((n - v.shape[0],) + v.shape[1:], fill, v.dtype)])

    def columns(v, fill):
        return np.ascontiguousarray(padded(v, NC * P, fill).reshape(NG + 2, P, T).transpose(1, 0, 2).reshape(P, NC))

    dst = given["dst"]
    arrays = {
        "x": given["x"],
        "src": columns(given["src"], 0),
        "dst": columns(dst, N),
        "nxt": columns(padded(dst[1:], E, N), N),
        "dst_row": np.concatenate([np.full(1, -1, dst.dtype), padded(dst, EP, N)]),
        "ew": columns(given["edge_weight"], 0),
        "edge": np.ascontiguousarray(padded(given["edge_attr_48"], EP, 0).reshape(NG, P, T * F).transpose(1, 0, 2).reshape(P, NG * T * F)),
        "type_row": padded(given["edge_type_8"], EP, 0),
        "norm_row": padded(given["edge_weight1"].reshape(E), EP, 0),
        "eps": given["L0_gnn_eps"],
        "w1": np.ascontiguousarray(given["L2_gnn_weight1"].transpose(1, 0, 2).reshape(F, R * F)),
        "w2": np.ascontiguousarray(given["L2_gnn_weight2"].reshape(RC, P, F).transpose(1, 0, 2)),
        "bias1": np.ascontiguousarray(np.tile(given["L2_gnn_bias1"], R).reshape(RC, P).T),
        "bias2": given["L2_gnn_bias2"],
        "thetaT": np.ascontiguousarray(given["L3_gnn_theta_w"].T),
        "phiT": np.ascontiguousarray(given["L3_gnn_phi_w"].T),
        "theta_b": given["L3_gnn_theta_b"],
        "phi_b": given["L3_gnn_phi_b"],
        "ident": np.eye(P, dtype=np.float32),
        "rel": np.ascontiguousarray((np.arange(R * F) // F).astype(np.float32).reshape(RC, P).T),
    }
    nc = bacc.Bacc("TRN2", target_bir_lowering=False, num_devices=1)
    aps = {k: nc.dram_tensor(f"in_{k}", v.shape, mybir.dt.from_np(v.dtype), kind="ExternalInput").ap() for k, v in arrays.items()}
    out = nc.dram_tensor("out", (N, F), F32, kind="ExternalOutput").ap()
    gnn(nc, aps, out)
    r = run_bass_kernel_spmd(nc, [{f"in_{k}": v for k, v in arrays.items()}], core_ids=[0])
    return r.results[0]["out"]
```

```python
import concourse.bass as bass
from concourse import mybir
from contextlib import ExitStack

F32, I32 = mybir.dt.float32, mybir.dt.int32
ALU, ACT, AX = mybir.AluOpType, mybir.ActivationFunctionType, mybir.AxisListType

N, E, F, R = 100000, 50000, 48, 8
P, T = 128, 4
GE = P * T
U = 4
NG = -(-E // (GE * U)) * U
NT = NG // U
EP = NG * GE
NC = (NG + 2) * T
RC = R * F // P
XW = F + 1
ROWS, CHUNKS = 39, 20
PG = NG // CHUNKS
assert PG * CHUNKS == NG and CHUNKS % 2 == 0
REST = N - P * ROWS * CHUNKS
RP, RR = 32, REST // 32
RS = 64
RK = RS + R
ZW = 1920
assert EP * F // P % ZW == 0
LN_EPS, ALPHA, STEPS = 1e-5, 0.1, 10
FAR = float(1 << 23)
APART = 1.0e30
LOW = 3.0e38


def wait(eng, sem, value):
    if not isinstance(value, int) or value > 0:
        eng.wait_ge(sem, value)


class Chain:

    def __init__(self, eng, sem, per):
        self.eng, self.sem, self.per = eng, sem, per

    def turn(self, n):
        self.base, self.count = n * self.per, 0
        return self

    def then(self, ins):
        ins.then_inc(self.sem, 1)
        self.count += 1
        assert self.count <= self.per
        self.eng.wait_ge(self.sem, self.base + self.count)

    def last(self):
        assert self.count == self.per, (self.count, self.per)


class Scope(ExitStack):

    def __init__(self, nc):
        super().__init__()
        self.nc, self.made = nc, []

    def sem(self, name):
        self.made.append(self.enter_context(self.nc.semaphore(name)))
        return self.made[-1]

    def __exit__(self, *failed):
        if failed[0] is None:
            with self.nc.Block() as block:
                @block.sync
                def _(sp):
                    for s in self.made:
                        sp.sem_clear(s)
        return super().__exit__(*failed)


def mid(ap, rows):
    return ap.unsqueeze(2).to_broadcast([ap.shape[0], rows, F])


def gnn(nc, a, out):
    ctx = ExitStack()
    with ctx:
        def sb(name, shape, dt=F32):
            return ctx.enter_context(nc.sbuf_tensor(name, shape, dt))

        def pair(name, shape, dt=F32):
            return [sb(f"{name}{b}", shape, dt) for b in range(2)]

        def sem(name):
            return ctx.enter_context(nc.semaphore(name))

        def sems(name):
            return [sem(f"{name}{b}") for b in range(2)]

        def dram(name, shape, dt=F32):
            return nc.dram_tensor(name, shape, dt, kind="Internal").ap()

        xpos = dram("xpos", (N, XW))
        layer = {k: dram(f"layer{k}", (2 * EP, F)) for k in (1, 2, 3)}
        other = dram("other", (EP + 1, F))
        onehot = dram("onehot", (R, EP))
        rows_dram = dram("rows_dram", (2, EP))

        ident = sb("ident", [P, P])
        bias1 = sb("bias1", [P, RC])
        bias2 = sb("bias2", [P, F])
        bias2c = sb("bias2c", [P, F])
        bias3 = sb("bias3", [P, F])
        phb = sb("phb", [P, F])
        w1 = sb("w1", [RK, R * F])
        w2 = sb("w2", [P, RC, F])
        theta = sb("theta", [F, F])
        phi = sb("phi", [F, F])
        pmt = sb("pmt", [F, F])
        eps0 = sb("eps0", [P, 1])
        c = sb("c", [P, 1])
        c2 = sb("c2", [P, 1])
        bm = sb("bm", [P, 1])
        lneps = sb("lneps", [P, 1])
        neg1 = sb("neg1", [P, ROWS])
        zrow = sb("zrow", [1, F])
        src = sb("src", [P, NC], I32)
        dst = sb("dst", [P, NC], I32)
        nxt = sb("nxt", [P, NC], I32)
        dstc = sb("dstc", [P, NC], I32)
        posi = sb("posi", [P, NC], I32)
        outi = sb("outi", [P, NC], I32)
        idx2 = sb("idx2", [P, NC], I32)
        idxk = sb("idxk", [P, NC], I32)
        ei = sb("ei", [P, NC], I32)
        ef = sb("ef", [P, NC])
        posf = sb("posf", [P, NC])
        w9 = sb("w9", [P, NC])
        t1 = sb("t1", [P, NC])
        t2 = sb("t2", [P, NC])
        XD = sb("XD", [P, NG * T * F])

        def xd(g):
            return XD[:, bass.ds(g * (T * F), T * F)].rearrange("p (t f) -> p t f", f=F)

        def col(ap, g):
            return ap[:, bass.ds(g * T, T)]

        def rows(table, g, base=0):
            return table[bass.ds(g * GE + base, GE), :].rearrange("(p t) f -> p (t f)", t=T)

        def spread(dc, y, d, q, m, n):
            dc.then(nc.vector.tensor_reduce(m, y, AX.X, ALU.add))
            dc.then(nc.vector.scalar_tensor_tensor(out=d, in0=mid(m, n), scalar=-1.0 / F, in1=y, op0=ALU.mult, op1=ALU.add))
            dc.then(nc.vector.tensor_tensor(q, d, d, ALU.mult))


        with ExitStack() as scope:
            xin = [scope.enter_context(nc.sbuf_tensor(f"xin{b}", [P, ROWS, XW], F32)) for b in range(2)]
            dr = scope.enter_context(nc.sbuf_tensor("dr", [NG, GE], I32))
            dp = scope.enter_context(nc.sbuf_tensor("dp", [NG, GE], I32))
            kind = scope.enter_context(nc.sbuf_tensor("kind", [NG, GE], I32))
            hot = [scope.enter_context(nc.sbuf_tensor(f"hot{r}", [NG, GE], F32)) for r in range(R)]
            s_kind, s_hot, s_w1 = sem("s_kind"), sem("s_hot"), sem("s_w1")
            keepr = scope.enter_context(nc.sbuf_tensor("keepr", [NG, GE], F32))
            penr = scope.enter_context(nc.sbuf_tensor("penr", [NG, GE], F32))
            s_const, s_col, s_chain, s_ei, s_keep = (sem(n) for n in ("s_const", "s_col", "s_chain", "s_ei", "s_keep"))
            s_neg, s_rows = sem("s_neg"), sem("s_rows")
            s_xin, s_xout = sems("s_xin"), sems("s_xout")
            xv = a["x"][0:P * ROWS * CHUNKS, :].rearrange("(p c r) f -> p c r f", p=P, c=CHUNKS)
            pv = xpos[0:P * ROWS * CHUNKS, :].rearrange("(p c r) f -> p c (r f)", p=P, c=CHUNKS)
            consts = [(ident, "ident"), (bias1, "bias1"), (w2, "w2"),
                      (theta, "thetaT"), (phi, "phiT")]
            wide = [(bias2, "bias2"), (bias3, "theta_b"), (phb, "phi_b"), (eps0, "eps")]
            cols = [(src, "src"), (dst, "dst"), (nxt, "nxt"), (w9, "ew")]
            with nc.Block() as block:
                @block.sync
                def _(sp):
                    for t, n in cols:
                        sp.dma_start(t[:, :], a[n]).then_inc(s_col, 16)
                    sp.dma_start(dr[:, :], a["dst_row"][1:EP + 1].rearrange("(g e) -> g e", e=GE)).then_inc(s_col, 16)
                    sp.dma_start(kind[:, :], a["type_row"].rearrange("(g e) -> g e", e=GE)).then_inc(s_kind, 16)
                    sp.dma_start(dp[:, :], a["dst_row"][0:EP].rearrange("(g e) -> g e", e=GE)).then_inc(s_col, 16)
                    for t, n in consts:
                        sp.dma_start(t[:], a[n]).then_inc(s_const, 16)
                    sp.wait_ge(s_w1, 1)
                    sp.dma_start(w1[0:F, :], a["w1"]).then_inc(s_const, 16)
                    sp.dma_start(w1[RS:RK, :], a["apart"]).then_inc(s_const, 16)
                    for t, n in wide:
                        sp.dma_start(t[:, :], a[n].partition_broadcast(P)).then_inc(s_const, 16)

                    def load(i, b):
                        wait(sp, s_xout[b], i * 16)
                        sp.dma_start(xin[b][:, :, 0:F], xv[:, bass.ds(i * 2 + b, 1)].rearrange("p c r f -> p (c r) f")).then_inc(s_xin[b], 16)

                    for b in range(2):
                        load(0, b)
                    with sp.Fori(1, CHUNKS // 2) as i:
                        for b in range(2):
                            load(i, b)
                    sp.wait_ge(s_xout[0], 16 * CHUNKS // 2)
                    sp.dma_start(xin[0][0:RP, 0:RR, 0:F], a["x"][N - REST:N, :].rearrange("(p r) f -> p r f", p=RP)).then_inc(s_xin[0], 16)
                    sp.wait_ge(s_keep, 1)
                    sp.dma_start(rows_dram[0:1, :].rearrange("o (g e) -> (o g) e", e=GE), keepr[:, :]).then_inc(s_rows, 16)
                    sp.dma_start(rows_dram[1:2, :].rearrange("o (g e) -> (o g) e", e=GE), penr[:, :]).then_inc(s_rows, 16)
                    sp.wait_ge(s_hot, 1)
                    for r in range(R):
                        sp.dma_start(onehot[r:r + 1, :].rearrange("o (g e) -> (o g) e", e=GE), hot[r][:, :]).then_inc(s_rows, 16)
                    sp.wait_ge(s_rows, 16 * (2 + R))
                    sp.wait_ge(s_const, 16 * (len(consts) + len(wide) + 2))

                @block.scalar
                def _(act):
                    act.wait_ge(s_neg, 1)

                    def store(i, b):
                        act.wait_ge(s_xin[b], i * 16 + 16)
                        act.dma_start(pv[:, bass.ds(i * 2 + b, 1)].rearrange("p c w -> p (c w)"), xin[b][:, :, :].rearrange("p r w -> p (r w)")).then_inc(s_xout[b], 16)

                    with act.Fori(0, CHUNKS // 2) as i:
                        for b in range(2):
                            store(i, b)
                    act.wait_ge(s_xin[0], 16 * CHUNKS // 2 + 16)
                    act.dma_start(xpos[N - REST:N, :].rearrange("(p r) w -> p (r w)", p=RP), xin[0][0:RP, 0:RR, :].rearrange("p r w -> p (r w)")).then_inc(s_xout[0], 16)
                    act.wait_ge(s_xout[0], 16 * CHUNKS // 2 + 16)
                    act.wait_ge(s_xout[1], 16 * CHUNKS // 2)

                @block.gpsimd
                def _(pool):
                    nc.gpsimd.iota(ei[:, :], pattern=[[GE, NG + 2], [1, T]], base=0, channel_multiplier=T).then_inc(s_ei, 1)

                @block.vector
                def _(dve):
                    dc = Chain(dve, s_chain, 14).turn(0)
                    for b in range(2):
                        ins = nc.vector.memset(xin[b][:, :, F:XW], -1.0)
                    ins.then_inc(s_neg, 1)
                    nc.vector.memset(w1[:, :], 0.0).then_inc(s_w1, 1)
                    nc.vector.memset(lneps[:, :], LN_EPS)
                    nc.vector.memset(zrow[:, :], 0.0)
                    dve.wait_ge(s_ei, 1)
                    nc.vector.tensor_copy(ef[:, :], ei[:, :])
                    dve.wait_ge(s_kind, 16)
                    for r in range(R):
                        ins = nc.vector.tensor_scalar(hot[r][:, :], kind[:, :], float(r), None, ALU.is_equal)
                    ins.then_inc(s_hot, 1)
                    dve.wait_ge(s_col, 16 * 6)
                    nc.vector.tensor_scalar(w9[:, :], w9[:, :], 1.0 - ALPHA, None, ALU.mult)
                    nc.vector.tensor_scalar(dstc[:, :], dst[:, :], N - 1, None, ALU.min)
                    dc.then(nc.vector.tensor_tensor(t1[:, :], dst[:, :], nxt[:, :], ALU.is_equal))
                    dc.then(nc.vector.tensor_scalar(t1[:, :], t1[:, :], FAR, None, ALU.mult))
                    dc.then(nc.vector.tensor_tensor(outi[:, :], t1[:, :], dst[:, :], ALU.add))
                    dc.then(nc.vector.tensor_scalar(t2[:, :], dst[:, :], float(XW), float(F), ALU.mult, ALU.add))
                    dc.then(nc.vector.tensor_tensor(posi[:, :], t1[:, :], t2[:, :], ALU.add))
                    dc.then(nc.vector.tensor_tensor(keepr[:, :], dr[:, :], dp[:, :], ALU.is_equal))
                    nc.vector.tensor_scalar(penr[:, :], keepr[:, :], 1.0, LOW, ALU.subtract, ALU.mult).then_inc(s_keep, 1)
                    dve.wait_ge(s_const, 16 * (len(consts) + len(wide) + 2))
                    dc.then(nc.vector.tensor_scalar(c[:, :], eps0[:, :], 2.0, None, ALU.add))
                    dc.then(nc.vector.tensor_tensor(c2[:, :], c[:, :], c[:, :], ALU.mult))
                    dc.then(nc.vector.tensor_scalar(c2[:, :], c2[:, :], 1.0 / F, None, ALU.mult))
                    dc.then(nc.vector.tensor_scalar(bias2c[:, :], bias2[:, :], 0.0, None, ALU.max))
                    dc.then(nc.vector.tensor_reduce(bm[:, :], bias2c[:, :], AX.X, ALU.add))
                    dc.then(nc.vector.tensor_scalar(bm[:, :], bm[:, :], 1.0 / F, None, ALU.mult))
                    dc.then(nc.vector.tensor_scalar(bias2c[:, :], bias2c[:, :], bm[:, :], None, ALU.subtract))
                    nc.vector.tensor_tensor(bias3[:, :], bias3[:, :], phb[:, :], ALU.add)
                    dc.then(nc.vector.tensor_tensor(pmt[:, :], phi[:, :], theta[:, :], ALU.subtract))
                    dc.last()

        with ExitStack() as scope:
            def sc(name, shape, dt=F32):
                return scope.enter_context(nc.sbuf_tensor(name, shape, dt))
            nx = [sc(f"nx{b}", [P, ROWS, F]) for b in range(2)]
            no = [sc(f"no{b}", [P, ROWS, F]) for b in range(2)]
            nd, nq = sc("nd", [P, ROWS, F]), sc("nq", [P, ROWS, F])
            nm, nv, ns, nr, nu = (sc(n, [P, ROWS]) for n in ("nm", "nv", "ns", "nr", "nu"))
            zeros = sc("zeros", [P, ZW])
            s_zeros, s_fill = sem("s_zeros"), sem("s_fill")
            pidx = [sc(f"pidx{b}", [P, PG * T], I32) for b in range(2)]
            pval = [sc(f"pval{b}", [P, PG * T]) for b in range(2)]
            s_nx, s_st, s_pos = sems("s_nx"), sems("s_st"), sems("s_pos")
            s_nchain, s_out, s_nvar, s_nstd, s_nd, s_nq, s_pstage, s_turn = (
                sem(n) for n in ("s_nchain", "s_out", "s_nvar", "s_nstd", "s_nd", "s_nq", "s_pstage", "s_turn"))
            xv = a["x"][0:P * ROWS * CHUNKS, :].rearrange("(p c r) f -> p c (r f)", p=P, c=CHUNKS)
            ov = out[0:P * ROWS * CHUNKS, :].rearrange("(p c r) f -> p c (r f)", p=P, c=CHUNKS)
            xpos_cells = xpos.rearrange("n (w o) -> (n w) o", o=1)
            with nc.Block() as block:
                @block.sync
                def _(sp):
                    def load(i, b):
                        wait(sp, s_out, i * 2 + b - 1)
                        sp.dma_start(nx[b][:, :, :].rearrange("p r f -> p (r f)"), xv[:, bass.ds(i * 2 + b, 1)].rearrange("p c w -> p (c w)")).then_inc(s_nx[b], 16)

                    def store(i, b):
                        wait(sp, s_out, i * 2 + b + 1)
                        sp.dma_start(ov[:, bass.ds(i * 2 + b, 1)].rearrange("p c w -> p (c w)"), no[b][:, :, :].rearrange("p r f -> p (r f)")).then_inc(s_st[b], 16)

                    for b in range(2):
                        load(0, b)
                    sp.wait_ge(s_zeros, 1)
                    sp.dma_start(other[EP:EP + 1, :], zeros[0:1, 0:F]).then_inc(s_fill, 16)
                    with sp.Fori(0, EP * F // P // ZW) as j:
                        sp.dma_start(other[0:EP, :].rearrange("(p r) f -> p (r f)", p=P)[:, bass.ds(j * ZW, ZW)], zeros[:, :]).then_inc(s_fill, 16)
                    with sp.Fori(1, CHUNKS // 2) as i:
                        for b in range(2):
                            store(i - 1, b)
                            load(i, b)
                    store(CHUNKS // 2 - 1, 0)
                    sp.dma_start(nx[0][0:RP, 0:RR, :], a["x"][N - REST:N, :].rearrange("(p r) f -> p r f", p=RP)).then_inc(s_nx[0], 16)
                    store(CHUNKS // 2 - 1, 1)
                    sp.wait_ge(s_out, CHUNKS + 1)
                    sp.dma_start(out[N - REST:N, :].rearrange("(p r) f -> p r f", p=RP), no[0][0:RP, 0:RR, :]).then_inc(s_st[0], 16)
                    sp.wait_ge(s_st[0], 16 * (CHUNKS // 2 + 1))
                    sp.wait_ge(s_st[1], 16 * (CHUNKS // 2))
                    sp.wait_ge(s_fill, 16 * (1 + EP * F // P // ZW))

                @block.scalar
                def _(act):
                    def root(n, p, r, src_t, scale):
                        act.wait_ge(s_nvar, n + 1)
                        nc.scalar.activation(ns[0:p, 0:r], src_t[0:p, 0:r], ACT.Sqrt, bias=lneps[0:p, :], scale=scale).then_inc(s_nstd, 1)

                    def square(n, p, r):
                        act.wait_ge(s_nd, n + 1)
                        nc.scalar.activation(nq[0:p, 0:r, :], nd[0:p, 0:r, :], ACT.Square).then_inc(s_nq, 1)

                    def work(n, p, r):
                        square(n * 2, p, r)
                        root(n * 4, p, r, nu, c2[0:p, :])
                        root(n * 4 + 1, p, r, nv, (1 + ALPHA) ** 2)
                        square(n * 2 + 1, p, r)
                        root(n * 4 + 2, p, r, nu, 1.0 / F)
                        root(n * 4 + 3, p, r, nv, 1.0 / F)

                    def stage(i, b):
                        w = PG * T
                        wait(act, s_pos[b], i * 16 * w)
                        nc.scalar.copy(pidx[b][:, :], posi[:, bass.ds((i * 2 + b) * w, w)]).then_inc(s_pstage, 1)
                        nc.scalar.copy(pval[b][:, :], ef[:, bass.ds((i * 2 + b) * w, w)]).then_inc(s_pstage, 1)

                    stage(0, 0)
                    stage(0, 1)
                    work(0, P, ROWS)
                    with act.Fori(1, CHUNKS // 2) as i:
                        stage(i, 0)
                        work(i * 2 - 1, P, ROWS)
                        stage(i, 1)
                        work(i * 2, P, ROWS)
                    work(CHUNKS - 1, P, ROWS)
                    work(CHUNKS, RP, RR)

                @block.gpsimd
                def _(pool):
                    bound = pool.to_reg(N * XW - 1)
                    with pool.Fori(0, CHUNKS // 2) as i:
                        for b in range(2):
                            pool.wait_ge(s_pstage, (i * 2 + b) * 2 + 2)
                            pool.sem_inc(s_turn, 1)
                            for t in range(PG * T):
                                nc.gpsimd.indirect_dma_start(
                                    out=xpos_cells, out_offset=bass.IndirectOffsetOnAxis(ap=pidx[b][:, t:t + 1], axis=0),
                                    in_=pval[b][:, t:t + 1], in_offset=None, bounds_check=bound, oob_is_err=False).then_inc(s_pos[b], 16)
                    for b in range(2):
                        pool.wait_ge(s_pos[b], CHUNKS // 2 * 16 * PG * T)

                @block.vector
                def _(dve):
                    dc = Chain(dve, s_nchain, 11)
                    nc.vector.memset(zeros[:, :], 0.0).then_inc(s_zeros, 1)

                    def chunk(n, i, b, p, r):
                        dc.turn(n)
                        x, d, q, o = nx[b][0:p, 0:r, :], nd[0:p, 0:r, :], nq[0:p, 0:r, :], no[b][0:p, 0:r, :]
                        m, v, s, rr, u = (t[0:p, 0:r] for t in (nm, nv, ns, nr, nu))
                        dve.wait_ge(s_nx[b], i * 16 + 16)
                        dc.then(nc.vector.tensor_reduce(m, x, AX.X, ALU.add))
                        nc.vector.scalar_tensor_tensor(out=d, in0=mid(m, r), scalar=-1.0 / F, in1=x, op0=ALU.mult, op1=ALU.add).then_inc(s_nd, 1)
                        dve.wait_ge(s_nq, n * 2 + 1)
                        nc.vector.tensor_reduce(u, q, AX.X, ALU.add).then_inc(s_nvar, 1)
                        dve.wait_ge(s_nvar, n * 4 + 1)
                        dve.wait_ge(s_nstd, n * 4 + 1)
                        dc.then(nc.vector.reciprocal(rr, s))
                        dc.then(nc.vector.scalar_tensor_tensor(out=u, in0=u, scalar=c2[0:p, :], in1=rr, op0=ALU.mult, op1=ALU.mult))
                        nc.vector.tensor_tensor(v, u, rr, ALU.mult).then_inc(s_nvar, 1)
                        dve.wait_ge(s_nvar, n * 4 + 2)
                        dc.then(nc.vector.tensor_scalar(rr, rr, c[0:p, :], None, ALU.mult))
                        dve.wait_ge(s_nstd, n * 4 + 2)
                        dc.then(nc.vector.reciprocal(u, s))
                        dc.then(nc.vector.scalar_tensor_tensor(out=rr, in0=u, scalar=1 + ALPHA, in1=rr, op0=ALU.mult, op1=ALU.mult))
                        dc.then(nc.vector.tensor_tensor(d, d, mid(rr, r), ALU.mult))
                        nc.vector.tensor_tensor(d, d, bias2c[0:p, :].unsqueeze(1).to_broadcast([p, r, F]), ALU.add).then_inc(s_nd, 1)
                        dve.wait_ge(s_nd, n * 2 + 2)
                        dve.wait_ge(s_nq, n * 2 + 2)
                        nc.vector.tensor_reduce(u, q, AX.X, ALU.add).then_inc(s_nvar, 1)
                        dve.wait_ge(s_nvar, n * 4 + 3)
                        dve.wait_ge(s_nstd, n * 4 + 3)
                        dc.then(nc.vector.reciprocal(rr, s))
                        dc.then(nc.vector.tensor_tensor(u, u, rr, ALU.mult))
                        nc.vector.tensor_tensor(v, u, rr, ALU.mult).then_inc(s_nvar, 1)
                        dve.wait_ge(s_nvar, n * 4 + 4)
                        dve.wait_ge(s_nstd, n * 4 + 4)
                        dc.then(nc.vector.reciprocal(u, s))
                        dc.then(nc.vector.tensor_tensor(rr, rr, u, ALU.mult))
                        wait(dve, s_st[b], i * 16)
                        nc.vector.tensor_tensor(o, d, mid(rr, r), ALU.mult).then_inc(s_out, 1)
                        dve.wait_ge(s_out, n + 1)
                        dc.last()

                    for b in range(2):
                        chunk(b, 0, b, P, ROWS)
                    with dve.Fori(1, CHUNKS // 2) as i:
                        for b in range(2):
                            chunk(i * 2 + b, i, b, P, ROWS)
                    chunk(CHUNKS, CHUNKS // 2, 0, RP, RR)

        pe_turn, pool_turn = sem("pe_turn"), sem("pool_turn")

        def slots(name, shape, dt=F32, n=U, scope=ctx):
            return [scope.enter_context(nc.sbuf_tensor(f"{name}{s}", shape, dt)) for s in range(n)]

        gb = slots("gb", [P, T, XW])
        ib = slots("ib", [P, 2 * T], I32)
        kb = slots("kb", [F, GE])
        scan = slots("scan", [F, GE], n=2)
        ey, ed, eq = (sb(n, [P, T, F]) for n in ("ey", "ed", "eq"))
        em, eu, er, es = (sb(n, [P, T]) for n in ("em", "eu", "er", "es"))
        psT = [ctx.enter_context(nc.psum_tensor(f"psT{b}", [F, GE], F32)) for b in range(2)]
        psR = [ctx.enter_context(nc.psum_tensor(f"psR{b}", [P, T, F], F32)) for b in range(2)]
        psH = [ctx.enter_context(nc.psum_tensor(f"psH{q}", [P, GE], F32)) for q in range(RC)]
        psM = ctx.enter_context(nc.psum_tensor("psM", [P, GE], F32))

        def slot(ap, t):
            return ap.rearrange("f (p t) -> f p t", t=T)[:, :, t]

        def keep_row(r, g):
            return rows_dram[r:r + 1, bass.ds(g * GE, GE)].to_broadcast([F, GE])

        def turns(eng, body, n=NT):
            for s in range(U):
                body(0, s)
            with eng.Fori(1, n) as i:
                for s in range(U):
                    body(i, s)

        def back(i, s, n):
            return (i, s - n) if s >= n else (i - 1, s - n + U)

        def flat(rows_sb):
            return rows_sb[:, :, :].rearrange("p t f -> p (t f)")

        def to_columns(dst_ps, rows_sb):
            for t in range(T):
                last = nc.tensor.transpose(slot(dst_ps, t), rows_sb[:, t, 0:F], ident[:, :])
            return last

        def to_rows(dst_ps, cols_sb):
            for t in range(T):
                last = nc.tensor.transpose(dst_ps[:, t, :], slot(cols_sb, t), ident[0:F, 0:F])
            return last

        def last_norm(dve, epi, s_var, s_std, g):
            epi.then(nc.vector.tensor_reduce(em[:, :], ey[:, :, :], AX.X, ALU.add))
            epi.then(nc.vector.scalar_tensor_tensor(out=ed[:, :, :], in0=mid(em[:, :], T), scalar=-1.0 / F, in1=ey[:, :, :], op0=ALU.mult, op1=ALU.add))
            epi.then(nc.vector.tensor_tensor(eq[:, :, :], ed[:, :, :], ed[:, :, :], ALU.mult))
            nc.vector.tensor_reduce(eu[:, :], eq[:, :, :], AX.X, ALU.add).then_inc(s_var, 1)
            dve.wait_ge(s_std, g + 1)
            epi.then(nc.vector.reciprocal(er[:, :], es[:, :]))

        def gather(s, table, width, col0=0, dst=None):
            dst = gb if dst is None else dst
            for t in range(T):
                yield nc.gpsimd.indirect_dma_start(
                    out=dst[s][:, t, 0:width], out_offset=None, in_=table,
                    in_offset=bass.IndirectOffsetOnAxis(ap=ib[s][:, col0 + t:col0 + t + 1], axis=0))

        with Scope(nc) as scope:
            def sp2(name, n=2):
                return slots(name, [P, T, F], n=n, scope=scope)
            xdb, efb = sp2("xdb", U), sp2("efb", U)
            msg, act0, x1s, x2s, x3s = (sp2(n) for n in ("msg0_", "act0_", "x1s", "x2s", "x3s"))
            ld, lq = (scope.enter_context(nc.sbuf_tensor(n, [P, T, F], F32)) for n in ("ld", "lq"))
            lm, lu, lv, lr, lw, ls = (scope.enter_context(nc.sbuf_tensor(n, [P, T], F32)) for n in ("lm", "lu", "lv", "lr", "lw", "ls"))
            s_g, s_ef, s_kb = ([sem(f"a_{n}{s}") for s in range(U)] for n in ("g", "ef", "kb"))
            s_s1, s_s2, s_s3, s_x1 = (sems(n) for n in ("a_s1", "a_s2", "a_s3", "a_x1"))
            (s_stage, s_add, s_relu, s_cols, s_scan, s_rows, s_lone, s_epi, s_src, s_posf, s_self, s_xd, s_sum, s_lvar, s_lstd,
             s_evar, s_estd, s_x1s) = (scope.sem(f"a_{n}") for n in (
                 "stage", "add", "relu", "cols", "scan", "rows", "lone", "epi", "src", "posf", "self", "xd", "sum",
                 "lvar", "lstd", "evar", "estd", "x1s"))
            with nc.Block() as block:
                @block.sync
                def _(sp):
                    def load(i, s):
                        g = i * U + s
                        wait(sp, s_add, g - U + 1)
                        sp.dma_start(flat(efb[s]), a["edge"][:, bass.ds(g * T * F, T * F)]).then_inc(s_ef[s], 16)
                        wait(sp, s_scan, g - U + 1)
                        sp.dma_start(kb[s][:, :], keep_row(0, g)).then_inc(s_kb[s], 16)

                    def store(i, s):
                        g, b = i * U + s, s % 2
                        sp.wait_ge(s_src, g + 1)
                        for buf, k, done in ((x1s, 1, s_s1), (x2s, 2, s_s2), (x3s, 3, s_s3)):
                            sp.dma_start(rows(layer[k], g, EP), flat(buf[b])).then_inc(done[b], 16)

                    def store_x1(i, s):
                        g = i * U + s
                        sp.wait_ge(s_xd, g + 1)
                        sp.dma_start(rows(layer[1], g), XD[:, bass.ds(g * T * F, T * F)]).then_inc(s_x1[s % 2], 16)

                    def body(i, s):
                        load(i, s)
                        if not (isinstance(i, int) and s < 1):
                            store(*back(i, s, 1))
                        if not (isinstance(i, int) and s < 3):
                            store_x1(*back(i, s, 3))

                    turns(sp, body)
                    store(NT - 1, U - 1)
                    for s in range(1, U):
                        store_x1(NT - 1, s)
                    for b in range(2):
                        for done in (s_s1, s_s2, s_s3, s_x1):
                            sp.wait_ge(done[b], 16 * NG // 2)

                @block.scalar
                def _(act):
                    def stage(i, s):
                        g = i * U + s
                        wait(act, s_g[s], i * 32 * T)
                        nc.scalar.copy(ib[s][:, 0:T], col(src, g)).then_inc(s_stage, 1)
                        nc.scalar.copy(ib[s][:, T:2 * T], col(dstc, g)).then_inc(s_stage, 1)

                    def root(s_in, n, s_done, to, of, scale):
                        act.wait_ge(s_in, n + 1)
                        nc.scalar.activation(to[:, :], of[:, :], ACT.Sqrt, bias=lneps[:, :], scale=scale).then_inc(s_done, 1)

                    def body(i, s):
                        g, b = i * U + s, s % 2
                        stage(i + (s + 2) // U, (s + 2) % U)
                        act.wait_ge(s_add, g + 1)
                        wait(act, s_cols, g - 1)
                        nc.scalar.activation(act0[b][:, :, :], msg[b][:, :, :], ACT.Relu).then_inc(s_relu, 1)
                        nc.scalar.copy(col(posf, g), gb[s][:, :, F]).then_inc(s_posf, 1)
                        root(s_lvar, g * 3, s_lstd, ls, lu, c2[:, :])
                        if not (isinstance(i, int) and s < 1):
                            root(s_evar, g - 1, s_estd, es, eu, 1.0 / F)
                        root(s_lvar, g * 3 + 1, s_lstd, ls, lv, (1 + ALPHA) ** 2)
                        root(s_lvar, g * 3 + 2, s_lstd, ls, lu, 1.0 / F)

                    stage(0, 0)
                    stage(0, 1)
                    turns(act, body)
                    root(s_evar, NG - 1, s_estd, es, eu, 1.0 / F)

                @block.gpsimd
                def _(pool):
                    def body(i, s):
                        g = i * U + s
                        wait(pool, s_posf, g - U + 1)
                        wait(pool, s_lvar, 3 * (g - U) + 1)
                        wait(pool, s_self, g - U + 1)
                        pool.wait_ge(s_stage, (g + 1) * 2)
                        pool.sem_inc(pool_turn, 1)
                        for ins in gather(s, xpos, XW):
                            ins.then_inc(s_g[s], 16)
                        for ins in gather(s, a["x"], F, T, xdb):
                            ins.then_inc(s_g[s], 16)

                    turns(pool, body)

                @block.tensor
                def _(pe):
                    def body(i, s):
                        g, b = i * U + s, s % 2
                        pe.wait_ge(s_relu, g + 1)
                        wait(pe, s_scan, g - 1)
                        pe.sem_inc(pe_turn, 1)
                        to_columns(psT[b], act0[b]).then_inc(s_cols, 1)
                        pe.wait_ge(s_scan, g + 1)
                        wait(pe, s_sum, g - 1)
                        pe.sem_inc(pe_turn, 1)
                        to_rows(psR[b], scan[b]).then_inc(s_rows, 1)

                    turns(pe, body)

                @block.vector
                def _(dve):
                    lone, epi = Chain(dve, s_lone, 12), Chain(dve, s_epi, 4)

                    def run_end(i, s):
                        g = i * U + s
                        epi.turn(g)
                        dve.wait_ge(s_rows, g + 1)
                        nc.vector.tensor_tensor(ey[:, :, :], psR[s % 2][:, :, :], xd(g), ALU.add).then_inc(s_sum, 1)
                        dve.wait_ge(s_sum, g + 1)
                        spread(epi, ey[:, :, :], ed[:, :, :], eq[:, :, :], em[:, :], T)
                        nc.vector.tensor_reduce(eu[:, :], eq[:, :, :], AX.X, ALU.add).then_inc(s_evar, 1)

                    def run_end_x1(i, s):
                        g = i * U + s
                        dve.wait_ge(s_estd, g + 1)
                        epi.then(nc.vector.reciprocal(er[:, :], es[:, :]))
                        nc.vector.tensor_tensor(xd(g), ed[:, :, :], mid(er[:, :], T), ALU.mult).then_inc(s_xd, 1)
                        epi.last()

                    def body(i, s):
                        g, b = i * U + s, s % 2
                        first = isinstance(i, int) and s < 1
                        lone.turn(g)
                        dve.wait_ge(s_g[s], (i + 1) * 32 * T)
                        dve.wait_ge(s_ef[s], (i + 1) * 16)
                        wait(dve, s_relu, g - 1)
                        nc.vector.tensor_tensor(msg[b][:, :, :], gb[s][:, :, 0:F], efb[s][:, :, :], ALU.add).then_inc(s_add, 1)
                        nc.vector.tensor_scalar(xd(g), xdb[s][:, :, :], c[:, :], None, ALU.mult).then_inc(s_self, 1)
                        spread(lone, gb[s][:, :, 0:F], ld[:, :, :], lq[:, :, :], lm[:, :], T)
                        nc.vector.tensor_reduce(lu[:, :], lq[:, :, :], AX.X, ALU.add).then_inc(s_lvar, 1)
                        if not first:
                            run_end(*back(i, s, 1))
                        dve.wait_ge(s_lvar, g * 3 + 1)
                        dve.wait_ge(s_lstd, g * 3 + 1)
                        lone.then(nc.vector.reciprocal(lr[:, :], ls[:, :]))
                        lone.then(nc.vector.scalar_tensor_tensor(out=lu[:, :], in0=lu[:, :], scalar=c2[:, :], in1=lr[:, :], op0=ALU.mult, op1=ALU.mult))
                        nc.vector.tensor_tensor(lv[:, :], lu[:, :], lr[:, :], ALU.mult).then_inc(s_lvar, 1)
                        dve.wait_ge(s_lvar, g * 3 + 2)
                        lone.then(nc.vector.tensor_scalar(lr[:, :], lr[:, :], c[:, :], None, ALU.mult))
                        for done in (s_s1, s_s2, s_s3):
                            wait(dve, done[b], 16 * (i * 2 + s // 2))
                        nc.vector.tensor_tensor(x1s[b][:, :, :], ld[:, :, :], mid(lr[:, :], T), ALU.mult).then_inc(s_x1s, 1)
                        if not first:
                            run_end_x1(*back(i, s, 1))
                        dve.wait_ge(s_lstd, g * 3 + 2)
                        dve.wait_ge(s_x1s, g + 1)
                        lone.then(nc.vector.reciprocal(lw[:, :], ls[:, :]))
                        lone.then(nc.vector.scalar_tensor_tensor(out=lr[:, :], in0=lw[:, :], scalar=1 + ALPHA, in1=lr[:, :], op0=ALU.mult, op1=ALU.mult))
                        lone.then(nc.vector.tensor_tensor(x2s[b][:, :, :], ld[:, :, :], mid(lr[:, :], T), ALU.mult))
                        lone.then(nc.vector.tensor_tensor(ld[:, :, :], x2s[b][:, :, :], bias2c[:, :].unsqueeze(1).to_broadcast([P, T, F]), ALU.add))
                        lone.then(nc.vector.tensor_tensor(lq[:, :, :], ld[:, :, :], ld[:, :, :], ALU.mult))
                        nc.vector.tensor_reduce(lu[:, :], lq[:, :, :], AX.X, ALU.add).then_inc(s_lvar, 1)
                        dve.wait_ge(s_cols, g + 1)
                        dve.wait_ge(s_kb[s], (i + 1) * 16)
                        wait(dve, s_rows, g - 1)
                        wait(dve, s_scan, g)
                        start = 0.0 if first else scan[1 - b][:, GE - 1:GE]
                        nc.vector.tensor_tensor_scan(scan[b][:, :], kb[s][:, :], psT[b][:, :], start, ALU.mult, ALU.add).then_inc(s_scan, 1)
                        dve.wait_ge(s_lvar, g * 3 + 3)
                        dve.wait_ge(s_lstd, g * 3 + 3)
                        lone.then(nc.vector.reciprocal(lr[:, :], ls[:, :]))
                        nc.vector.tensor_tensor(x3s[b][:, :, :], ld[:, :, :], mid(lr[:, :], T), ALU.mult).then_inc(s_src, 1)
                        dve.wait_ge(s_src, g + 1)
                        lone.last()

                    turns(dve, body)
                    run_end(NT - 1, U - 1)
                    run_end_x1(NT - 1, U - 1)

        step_e, held = dram("step_e", (EP + 1, XW)), dram("held", (EP, F))
        again = layer[1][0:EP + 1, :]
        rec = [dram(f"rec{k}", (EP + 1, T)) for k in range(2)]
        keep_list = [dram(f"keep_list{k}", (1, EP)) for k in range(2)]
        at_run = [dram(f"at_run{k}", (EP + 1, 1)) for k in range(2)]
        flag_row = [dram(f"flag_row{k}", (1, EP)) for k in range(2)]
        slot_row = [dram(f"slot_row{k}", (1, EP)) for k in range(2)]
        sp_turn = sem("sp_turn")
        count = [sb(f"count{k}", [1, 1], I32) for k in range(2)]
        zero49 = sb("zero49", [1, XW])
        q_e, w_s = sb("q_e", [P, NC]), sb("w_s", [P, NC])
        dst_f = sb("dst_f", [P, NC])
        layer1 = ctx.enter_context(ExitStack())
        SUM = layer1.enter_context(nc.sbuf_tensor("SUM", [P, NG * T * F], F32))
        W = NG * T

        with Scope(nc) as scope:
            s_idx, s_z, s_zd = (scope.sem(n) for n in ("s_idx", "s_z", "s_zd"))
            with nc.Block() as block:
                @block.sync
                def _(sp):
                    sp.wait_ge(s_z, 1)
                    sp.dma_start(step_e[EP:EP + 1, :], zero49[:, :]).then_inc(s_zd, 16)
                    for z in at_run:
                        sp.dma_start(z[EP:EP + 1, :], neg1[0:1, 0:1]).then_inc(s_zd, 16)
                    sp.wait_ge(s_zd, 16 * 3)

                @block.vector
                def _(dve):
                    dc = Chain(dve, s_idx, 6).turn(0)
                    own, end, has, far = ef[:, 0:W], posf[:, 0:W], t1[:, 0:W], t2[:, 0:W]
                    nc.vector.memset(neg1[:, :], -1.0)
                    dc.then(nc.vector.memset(zero49[:, :], 0.0))
                    nc.vector.memset(zero49[:, F:XW], -1.0).then_inc(s_z, 1)
                    dc.then(nc.vector.tensor_scalar(has, end, 0.0, None, ALU.is_ge))
                    dc.then(nc.vector.tensor_scalar(own, own, float(EP), None, ALU.add))
                    dc.then(nc.vector.tensor_tensor(far, end, own, ALU.subtract))
                    dc.then(nc.vector.tensor_tensor(far, far, has, ALU.mult))
                    nc.vector.tensor_tensor(idx2[:, 0:W], far, own, ALU.add)
                    nc.vector.memset(posf[:, W:NC], -1.0)
                    dc.then(nc.vector.memset(idx2[:, W:NC], 0))
                    dc.last()

        def sems4(name):
            return [sem(f"{name}{s}") for s in range(U)]

        def turns_of(eng, counted):
            return eng.value_load(counted[0:1, 0:1], min_val=0, max_val=NT - 2) + 2

        def compact(k, at, weight, dst_f, turns_in, region, q_out, idx_out, w_out):
            keep_in = rows_dram[0:1, :] if k == 0 else keep_list[0]
            with Scope(nc) as scope:
                names = iter(range(99))
                base = 4 * NC

                def tile(parts):
                    o = 3 * base + GE * next(names)
                    return region[0:parts, o:o + GE]

                recs, got, before = (region[:, j * base:(j + 1) * base] for j in range(3))
                fr, kr, one, C, D, B, H = (tile(NG) for _ in range(7))
                small = [scope.enter_context(nc.sbuf_tensor(f"sm{k}_{j}", [P, 1], F32)) for j in range(2)]
                line = [scope.enter_context(nc.sbuf_tensor(f"ln{k}_{j}", [1, NG], F32)) for j in range(4)]
                cnt_f = scope.enter_context(nc.sbuf_tensor(f"cnt{k}", [1, 1], F32))
                sidx = [scope.enter_context(nc.sbuf_tensor(f"sidx{k}_{s}", [P, T], I32)) for s in range(U)]
                sval = [scope.enter_context(nc.sbuf_tensor(f"sval{k}_{s}", [P, T * T], F32)) for s in range(U)]
                (s_dma, s_flag, s_back, s_cc, s_rank, s_pe, s_def, s_rec, s_sl) = (
                    scope.sem(f"k{k}_{n}") for n in ("dma", "flag", "back", "cc", "rank", "pe", "def", "rec", "sl"))
                s_kl = scope.sem(f"k{k}_kl")
                s_done = scope.sem(f"k{k}_done")
                s_sc = sems4(f"k{k}_sc")
                s_stage = scope.sem(f"k{k}_stage")
                pt = psM[0:1, 0:NG]
                pc = psH[0][0:NG, 0:1]

                def cols_of(row):
                    return row.rearrange("o (g p t) -> (o p) g t", g=NG, p=P)

                def lines_of(row):
                    return row.rearrange("o (g e) -> (o g) e", e=GE)

                def grid(ap):
                    return ap[:, 0:W].rearrange("p (g t) -> p g t", t=T)

                with nc.Block() as block:
                    @block.sync
                    def _(sp):
                        sp.wait_ge(s_flag, 1)
                        sp.dma_start(cols_of(flag_row[k]), grid(t1)).then_inc(s_dma, 16)
                        sp.dma_start(kr, lines_of(keep_in)).then_inc(s_back, 16)
                        sp.wait_ge(s_def, 1)
                        sp.dma_start(rec[k][1:EP + 1, :].rearrange("(p g) w -> p (g w)", p=P), got[:, 0:4 * W]).then_inc(s_rec, 16)
                        sp.dma_start(rec[k][0:1, :], neg1[0:1, 0:T]).then_inc(s_rec, 16)
                        sp.wait_ge(s_dma, 16)
                        sp.dma_start(fr, lines_of(flag_row[k])).then_inc(s_back, 16)
                        sp.wait_ge(s_rank, 1)
                        sp.dma_start(lines_of(slot_row[k]), C).then_inc(s_dma, 16)
                        sp.dma_start(lines_of(at_run[k][0:EP, :].rearrange("e o -> o e")), B).then_inc(s_dma, 16)
                        sp.wait_ge(s_dma, 48)
                        sp.dma_start(grid(t2), cols_of(slot_row[k])).then_inc(s_back, 16)
                        sp.dma_start(grid(q_out), cols_of(at_run[k][0:EP, :].rearrange("e o -> o e"))).then_inc(s_back, 16)
                        sp.wait_ge(s_done, 1)
                        sp.dma_start(got[:, 0:4 * W].rearrange("p (g tw) -> p g tw", g=NG), rec[k][1:EP + 1, :].rearrange("(g p t) w -> p g (t w)", p=P, t=T)).then_inc(s_kl, 16)
                        sp.dma_start(before[:, 0:4 * W].rearrange("p (g tw) -> p g tw", g=NG), rec[k][0:EP, :].rearrange("(g p t) w -> p g (t w)", p=P, t=T)).then_inc(s_kl, 16)
                        sp.wait_ge(s_kl, 33)
                        sp.dma_start(cols_of(keep_list[k]), grid(t1)).then_inc(s_dma, 16)
                        sp.wait_ge(s_dma, 64)
                        sp.wait_ge(s_rec, 32)

                    @block.tensor
                    def _(pe):
                        pe.wait_ge(s_pe, 1)
                        nc.tensor.transpose(pt, small[0][0:NG, :], ident[0:NG, 0:NG]).then_inc(s_cc, 1)
                        pe.wait_ge(s_pe, 2)
                        nc.tensor.transpose(pc, line[1][:, :], ident[0:1, 0:1]).then_inc(s_cc, 1)
                        pe.wait_ge(s_pe, 3)
                        nc.tensor.transpose(pt, small[1][0:NG, :], ident[0:NG, 0:NG]).then_inc(s_cc, 1)
                        pe.wait_ge(s_pe, 4)
                        nc.tensor.transpose(pc, line[3][:, :], ident[0:1, 0:1]).then_inc(s_cc, 1)

                    @block.vector
                    def _(dve):
                        dc = Chain(dve, s_sl, 23).turn(0)
                        dc.then(nc.vector.memset(t1[:, :], 0.0))
                        nc.vector.tensor_scalar(t1[:, :], at[:, :], 0.0, None, ALU.is_ge).then_inc(s_flag, 1)
                        dve.wait_ge(s_flag, 1)
                        rv, gv, bv = (z.rearrange("p (c w) -> p c w", w=T) for z in (recs, got, before))
                        nc.vector.tensor_copy(rv[:, :, 0], at[:, :])
                        nc.vector.tensor_copy(rv[:, :, 1], weight[:, :])
                        nc.vector.tensor_copy(rv[:, :, 2], dst_f)
                        nc.vector.memset(rv[:, :, 3], 0.0)
                        nc.vector.memset(gv[:, :, 0], float(EP))
                        nc.vector.memset(gv[:, :, 1], 0.0)
                        nc.vector.memset(gv[:, :, 2], float(N))
                        nc.vector.memset(gv[:, :, 3], 0.0).then_inc(s_def, 1)
                        dc.then(nc.vector.memset(one, 1.0))
                        dve.wait_ge(s_back, 32)
                        dc.then(nc.vector.tensor_tensor_scan(C, one, fr, 0.0, ALU.mult, ALU.add))
                        nc.vector.tensor_copy(small[0][0:NG, :], C[:, GE - 1:GE]).then_inc(s_pe, 1)
                        dve.wait_ge(s_cc, 1)
                        dc.then(nc.vector.tensor_copy(line[0][:, :], pt))
                        dc.then(nc.vector.tensor_tensor_scan(line[2][:, :], one[0:1, 0:NG], line[0][:, :], 0.0, ALU.mult, ALU.add))
                        nc.vector.tensor_tensor(line[1][:, :], line[2][:, :], line[0][:, :], ALU.subtract).then_inc(s_pe, 1)
                        dc.then(nc.vector.tensor_scalar(cnt_f[:, :], line[2][:, NG - 1:NG], float(GE * U - 1 - 2 * GE * U), 0.0, ALU.add, ALU.max))
                        dc.then(nc.vector.tensor_copy(count[k][:, :], cnt_f[:, :]))
                        dc.then(nc.vector.tensor_scalar(count[k][:, :], count[k][:, :], (GE * U).bit_length() - 1, None, ALU.logical_shift_right))
                        dve.wait_ge(s_cc, 2)
                        dc.then(nc.vector.tensor_copy(small[0][0:NG, :], pc))
                        dc.then(nc.vector.tensor_scalar(C, C, small[0][0:NG, :], None, ALU.add))
                        dc.then(nc.vector.tensor_tensor(D, C, fr, ALU.subtract))
                        dc.then(nc.vector.tensor_tensor(H, D, kr, ALU.mult))
                        dc.then(nc.vector.tensor_tensor(D, D, H, ALU.subtract))
                        dc.then(nc.vector.tensor_tensor_scan(B, one, D, 0.0, ALU.mult, ALU.max))
                        nc.vector.tensor_copy(small[1][0:NG, :], B[:, GE - 1:GE]).then_inc(s_pe, 1)
                        dve.wait_ge(s_cc, 3)
                        dc.then(nc.vector.tensor_copy(line[0][:, :], pt))
                        dc.then(nc.vector.tensor_tensor_scan(line[2][:, :], one[0:1, 0:NG], line[0][:, :], 0.0, ALU.mult, ALU.max))
                        nc.vector.memset(line[3][:, 0:1], 0.0)
                        nc.vector.tensor_copy(line[3][:, 1:NG], line[2][:, 0:NG - 1]).then_inc(s_pe, 1)
                        dve.wait_ge(s_cc, 4)
                        dc.then(nc.vector.tensor_copy(small[1][0:NG, :], pc))
                        dc.then(nc.vector.tensor_scalar(B, B, small[1][0:NG, :], None, ALU.max))
                        dc.then(nc.vector.tensor_tensor(H, C, B, ALU.is_gt))
                        dc.then(nc.vector.tensor_tensor(B, C, H, ALU.mult))
                        dc.then(nc.vector.tensor_scalar(B, B, 1.0, None, ALU.subtract))
                        dc.then(nc.vector.tensor_scalar(H, fr, -FAR, FAR, ALU.mult, ALU.add))
                        nc.vector.tensor_tensor(C, C, H, ALU.add).then_inc(s_rank, 1)
                        dve.wait_ge(s_back, 64)
                        nc.vector.tensor_copy(posi[:, 0:W], t2[:, 0:W])
                        dc.then(nc.vector.memset(q_out[:, W:NC], -1.0))
                        nc.vector.memset(posi[:, W:NC], 1 << 23).then_inc(s_rank, 1)
                        dve.wait_ge(s_kl, 32)
                        nc.vector.tensor_copy(idx_out[:, 0:W], gv[:, 0:W, 0])
                        nc.vector.memset(idx_out[:, W:NC], 0)
                        nc.vector.tensor_copy(w_out[:, 0:W], gv[:, 0:W, 1])
                        nc.vector.memset(w_out[:, W:NC], 0.0)
                        nc.vector.tensor_tensor(t1[:, 0:W], gv[:, 0:W, 2], bv[:, 0:W, 2], ALU.is_equal).then_inc(s_kl, 1)
                        dve.wait_ge(s_kl, 33)
                        dc.last()

                    @block.scalar
                    def _(act):
                        act.wait_ge(s_rank, 2)
                        n = NT if turns_in is None else turns_of(act, turns_in)

                        def stage(i, s):
                            g = i * U + s
                            wait(act, s_sc[s], i * 16 * T)
                            nc.scalar.copy(sidx[s][:, :], col(posi, g)).then_inc(s_stage, 1)
                            nc.scalar.copy(sval[s][:, :], recs[:, bass.ds(g * T * T, T * T)]).then_inc(s_stage, 1)

                        turns(act, stage, n)

                    @block.gpsimd
                    def _(pool):
                        bound = pool.to_reg(EP)
                        pool.wait_ge(s_rec, 32)
                        pool.wait_ge(s_rank, 2)
                        n = NT if turns_in is None else turns_of(pool, turns_in)

                        def put(i, s):
                            g = i * U + s
                            pool.wait_ge(s_stage, (g + 1) * 2)
                            pool.sem_inc(pool_turn, 1)
                            for t in range(T):
                                nc.gpsimd.indirect_dma_start(
                                    out=rec[k], out_offset=bass.IndirectOffsetOnAxis(ap=sidx[s][:, t:t + 1], axis=0),
                                    in_=sval[s][:, t * T:(t + 1) * T], in_offset=None, bounds_check=bound, oob_is_err=False).then_inc(s_sc[s], 16)

                        turns(pool, put, n)
                        for s in range(U):
                            pool.wait_ge(s_sc[s], n * 16 * T)
                        pool.sem_inc(s_done, 1)

        def steps(tag, turns_in, keep, w, idx, runs, acc, tail=None, q_in=None, q_table=None):
            with Scope(nc) as scope:
                rb = slots(f"rb_{tag}", [P, T, XW], n=2, scope=scope)
                msg = slots(f"msg_{tag}", [P, T, F], n=2, scope=scope)

                def se(name, n=None):
                    if n is None:
                        return scope.sem(f"step_{tag}_{name}")
                    return [scope.sem(f"step_{tag}_{name}{j}") for j in range(n)]
                s_g = sems4(f"step_{tag}_g")
                s_kb, s_rst, s_ast = se("kb", U), se("rst", 2), se("ast", 2)
                s_stage, s_msg, s_cols, s_scan, s_rows, s_rb, s_acc, s_two, s_tail = (
                    se(n) for n in ("stage", "msg", "cols", "scan", "rows", "rb", "acc", "two", "tail"))
                reads = 2 * T if q_table is not None else T

                def loaded(eng):
                    return NT if turns_in is None else turns_of(eng, turns_in)

                def acc_rows(g):
                    return acc[:, bass.ds(g * (T * F), T * F)]

                with nc.Block() as block:
                    @block.sync
                    def _(sp):
                        n = loaded(sp)
                        m = n * U

                        def one(k, source, target, mode):
                            width = XW if target is step_e else F

                            def load(i, s):
                                wait(sp, s_scan, k * m + i * U + s - U + 1)
                                sp.dma_start(kb[s][:, :], keep[:, bass.ds((i * U + s) * GE, GE)].to_broadcast([F, GE])).then_inc(s_kb[s], 16)

                            def store(i, s):
                                g, b = i * U + s, s % 2
                                if target is not None:
                                    sp.wait_ge(s_rb, k * m + g + 1)
                                    sp.dma_start(target[bass.ds(g * GE, GE), :].rearrange("(p t) f -> p t f", t=T), rb[b][:, :, 0:width]).then_inc(s_rst[b], 16)
                                if mode in ("first", "end"):
                                    sp.wait_ge(s_acc, k * m + g + 1)
                                    out_t = held if mode == "first" else again
                                    sp.dma_start(rows(out_t, g), acc_rows(g)).then_inc(s_ast[b], 16)

                            def body(i, s):
                                load(i, s)
                                if not (isinstance(i, int) and s < 2):
                                    store(*back(i, s, 2))

                            turns(sp, body, n)
                            store(n - 1, U - 2)
                            store(n - 1, U - 1)
                            if mode in ("first", "end"):
                                for b in range(2):
                                    sp.wait_ge(s_ast[b], n * 32)
                            if target is not None:
                                for b in range(2):
                                    sp.wait_ge(s_rst[b], (k + 1) * n * 32)
                            sp.sem_inc(sp_turn, 1)

                        runs(sp, one)

                    @block.scalar
                    def _(act):
                        n = loaded(act)
                        m = n * U

                        def one(k, source, target, mode):
                            def stage(i, s):
                                wait(act, s_g[s], (k * n + i) * 16 * reads)
                                nc.scalar.copy(ib[s][:, 0:T], col(idx, i * U + s)).then_inc(s_stage, 1)

                            def body(i, s):
                                g, b = i * U + s, s % 2
                                stage(i + (s + 2) // U, (s + 2) % U)
                                if tail is not None:
                                    act.wait_ge(s_g[s], (k * n + i + 1) * 16 * reads)
                                    nc.scalar.copy(col(tail, g), gb[s][:, :, F]).then_inc(s_tail, 1)
                                act.wait_ge(s_rows, k * m + g + 1)
                                if target is not None:
                                    wait(act, s_rst[b], (k * n + i) * 32 + s // 2 * 16)
                                wait(act, s_acc, k * m + g - 1)
                                if q_in is not None:
                                    nc.scalar.copy(rb[b][:, :, F], col(q_in, g))
                                nc.scalar.copy(rb[b][:, :, 0:F], psR[b][:, :, :]).then_inc(s_rb, 1)

                            wait(act, s_stage, k * (m + 2))
                            stage(0, 0)
                            stage(0, 1)
                            turns(act, body, n)

                        runs(act, one)

                    @block.gpsimd
                    def _(pool):
                        n = loaded(pool)
                        m = n * U

                        def one(k, source, target, mode):
                            def body(i, s):
                                g = i * U + s
                                wait(pool, s_msg, k * m + g - U + 1)
                                if tail is not None:
                                    wait(pool, s_tail, k * m + g - U + 1)
                                pool.wait_ge(s_stage, k * (m + 2) + g + 1)
                                pool.sem_inc(pool_turn, 1)
                                for ins in gather(s, source, XW if source is step_e else F):
                                    ins.then_inc(s_g[s], 16)
                                if q_table is not None:
                                    for t in range(T):
                                        nc.gpsimd.indirect_dma_start(
                                            out=gb[s][:, t, F:XW], out_offset=None, in_=q_table,
                                            in_offset=bass.IndirectOffsetOnAxis(ap=ib[s][:, t:t + 1], axis=0)).then_inc(s_g[s], 16)

                            for b in range(2):
                                wait(pool, s_rst[b], k * n * 32)
                            turns(pool, body, n)

                        runs(pool, one)

                    @block.tensor
                    def _(pe):
                        n = loaded(pe)
                        m = n * U

                        def one(k, source, target, mode):
                            def body(i, s):
                                b = s % 2
                                at_g = k * m + i * U + s
                                pe.wait_ge(s_msg, at_g + 1)
                                wait(pe, s_scan, at_g - 1)
                                pe.sem_inc(pe_turn, 1)
                                to_columns(psT[b], msg[b]).then_inc(s_cols, 1)
                                pe.wait_ge(s_scan, at_g + 1)
                                wait(pe, s_rb, at_g - 1)
                                pe.sem_inc(pe_turn, 1)
                                to_rows(psR[b], scan[b]).then_inc(s_rows, 1)

                            turns(pe, body, n)

                        runs(pe, one)

                    @block.vector
                    def _(dve):
                        n = loaded(dve)
                        m = n * U

                        def one(k, source, target, mode):
                            def epilogue(i, s):
                                g, b = i * U + s, s % 2
                                mine = acc_rows(g).rearrange("p (t f) -> p t f", f=F)
                                if mode == "first":
                                    dve.wait_ge(s_two, g + 1)
                                dve.wait_ge(s_rb, k * m + g + 1)
                                if mode == "set":
                                    nc.vector.tensor_scalar(mine, rb[b][:, :, 0:F], ALPHA, None, ALU.mult).then_inc(s_acc, 1)
                                else:
                                    nc.vector.scalar_tensor_tensor(out=mine, in0=rb[b][:, :, 0:F], scalar=1.0 if mode == "end" else ALPHA, in1=mine, op0=ALU.mult, op1=ALU.add).then_inc(s_acc, 1)

                            def body(i, s):
                                g, b = i * U + s, s % 2
                                at_g = k * m + g
                                first = isinstance(i, int) and s < 1
                                dve.wait_ge(s_g[s], (k * n + i + 1) * 16 * reads)
                                wait(dve, s_cols, at_g - 1)
                                nc.vector.tensor_tensor(msg[b][:, :, :], gb[s][:, :, 0:F], mid(col(w, g), T), ALU.mult).then_inc(s_msg, 1)
                                if mode == "first":
                                    nc.vector.tensor_scalar(xd(g), xd(g), 1 + ALPHA, None, ALU.mult).then_inc(s_two, 1)
                                if not first:
                                    epilogue(*back(i, s, 1))
                                dve.wait_ge(s_cols, at_g + 1)
                                dve.wait_ge(s_kb[s], (k * n + i + 1) * 16)
                                wait(dve, s_rows, at_g - 1)
                                wait(dve, s_scan, at_g)
                                start = 0.0 if first else scan[1 - b][:, GE - 1:GE]
                                nc.vector.tensor_tensor_scan(scan[b][:, :], kb[s][:, :], psT[b][:, :], start, ALU.mult, ALU.add).then_inc(s_scan, 1)

                            turns(dve, body, n)
                            epilogue(n - 1, U - 1)

                        runs(dve, one)

        def run_index(idx_out, q, k):
            with Scope(nc) as scope:
                s_q = scope.sem(f"s_q{k}")
                with nc.Block() as block:
                    @block.vector
                    def _(dve):
                        dc = Chain(dve, s_q, 2).turn(0)
                        dc.then(nc.vector.tensor_scalar(t1[:, :], q[:, :], 0.0, float(EP + 1), ALU.is_lt, ALU.mult))
                        dc.then(nc.vector.tensor_tensor(idx_out[:, :], t1[:, :], q[:, :], ALU.add))
                        dc.last()


        def single(source, target, mode):
            return lambda eng, one: one(0, source, target, mode)

        def middle(eng, one):
            one(0, other, again, "add")
            one(1, again, other, "add")
            with eng.Fori(1, (STEPS - 4) // 2) as j:
                one(j * 2, other, again, "add")
                one(j * 2 + 1, again, other, "add")
            one(STEPS - 4, other, None, "end")

        with nc.Block() as block:
            @block.vector
            def _(dve):
                nc.vector.tensor_copy(dst_f[:, :], dst[:, :])

        compact(0, posf, w9, dst_f[:, :], None, SUM, q_e, idxk, w_s)
        steps("e", None, rows_dram[0:1, :], w9, idx2, single(layer[1], step_e, "first"), XD, q_in=q_e)
        with Scope(nc) as scope:
            s_z = scope.sem("s_again")
            with nc.Block() as block:
                @block.sync
                def _(sp):
                    sp.dma_start(again[EP:EP + 1, :], zrow[:, :]).then_inc(s_z, 16)
                    sp.wait_ge(s_z, 16)

                @block.vector
                def _(dve):
                    nc.vector.memset(posf[:, :], -1.0)
        steps("s", count[0], keep_list[0], w_s, idxk, single(step_e, again, "set"), SUM, tail=posf)
        with Scope(nc) as scope:
            s_r = scope.sem("s_r")
            got = XD[:, 0:4 * W]
            with nc.Block() as block:
                @block.sync
                def _(sp):
                    sp.dma_start(got.rearrange("p (g tw) -> p g tw", g=NG), rec[0][1:EP + 1, :].rearrange("(g p t) w -> p g (t w)", p=P, t=T)).then_inc(s_r, 16)

                @block.vector
                def _(dve):
                    dve.wait_ge(s_r, 16)
                    nc.vector.tensor_copy(dst_f[:, 0:W], got.rearrange("p (c w) -> p c w", w=T)[:, :, 2])
        compact(1, posf, w_s, dst_f[:, :], count[0], XD, ef, nxt, w9)
        steps("t", count[1], keep_list[1], w9, nxt, single(again, other, "set"), XD, tail=dst_f, q_table=at_run[1])
        run_index(dstc, dst_f, 0)
        steps("u", count[1], keep_list[1], w9, dstc, middle, XD)
        run_index(src, ef, 1)
        run_index(dst, q_e, 2)

        with Scope(nc) as scope:
            s_g = sems4("m_g")
            s_st = [scope.sem(f"m_st{b}") for b in range(2)]
            s_stage, s_add = (scope.sem(f"m_{n}") for n in ("stage", "add"))

            def sums(g):
                return SUM[:, bass.ds(g * (T * F), T * F)]

            with nc.Block() as block:
                @block.sync
                def _(sp):
                    n = turns_of(sp, count[0])

                    def store(i, s):
                        g = i * U + s
                        sp.wait_ge(s_add, g + 1)
                        sp.dma_start(rows(other, g), sums(g)).then_inc(s_st[s % 2], 16)

                    turns(sp, store, n)
                    for b in range(2):
                        sp.wait_ge(s_st[b], n * 32)
                    sp.sem_inc(sp_turn, 1)

                @block.scalar
                def _(act):
                    n = turns_of(act, count[0])

                    def stage(i, s):
                        wait(act, s_g[s], i * 16 * T)
                        nc.scalar.copy(ib[s][:, 0:T], col(src, i * U + s)).then_inc(s_stage, 1)

                    turns(act, stage, n)

                @block.gpsimd
                def _(pool):
                    n = turns_of(pool, count[0])

                    def body(i, s):
                        g = i * U + s
                        wait(pool, s_add, g - U + 1)
                        pool.wait_ge(s_stage, g + 1)
                        pool.sem_inc(pool_turn, 1)
                        for ins in gather(s, again, F):
                            ins.then_inc(s_g[s], 16)

                    turns(pool, body, n)

                @block.vector
                def _(dve):
                    n = turns_of(dve, count[0])

                    def body(i, s):
                        g = i * U + s
                        mine = sums(g).rearrange("p (t f) -> p t f", f=F)
                        dve.wait_ge(s_g[s], (i + 1) * 16 * T)
                        nc.vector.tensor_tensor(mine, gb[s][:, :, 0:F], mine, ALU.add).then_inc(s_add, 1)

                    turns(dve, body, n)

        with Scope(nc) as scope:
            hb = slots("hb", [P, T, F], scope=scope)
            s_g, s_h = sems4("n_g"), [scope.sem(f"n_h{s}") for s in range(U)]
            s_st = [scope.sem(f"n_st{b}") for b in range(2)]
            s_stage, s_add, s_var, s_std, s_epi, s_xd = (
                scope.sem(f"n_{n}") for n in ("stage", "add", "var", "std", "epi", "xd"))
            with nc.Block() as block:
                @block.sync
                def _(sp):
                    def body(i, s):
                        g = i * U + s
                        wait(sp, s_add, g - U + 1)
                        sp.dma_start(flat(hb[s]), rows(held, g)).then_inc(s_h[s], 16)
                        if not (isinstance(i, int) and s < 3):
                            store(*back(i, s, 3))

                    def store(i, s):
                        g = i * U + s
                        sp.wait_ge(s_xd, g + 1)
                        sp.dma_start(rows(layer[2], g), XD[:, bass.ds(g * T * F, T * F)]).then_inc(s_st[s % 2], 16)

                    turns(sp, body)
                    for s in range(1, U):
                        store(NT - 1, s)
                    for b in range(2):
                        sp.wait_ge(s_st[b], NT * 32)

                @block.scalar
                def _(act):
                    def stage(i, s):
                        wait(act, s_g[s], i * 16 * T)
                        nc.scalar.copy(ib[s][:, 0:T], col(dst, i * U + s)).then_inc(s_stage, 1)

                    def body(i, s):
                        stage(i + (s + 2) // U, (s + 2) % U)
                        act.wait_ge(s_var, i * U + s + 1)
                        nc.scalar.activation(es[:, :], eu[:, :], ACT.Sqrt, bias=lneps[:, :], scale=1.0 / F).then_inc(s_std, 1)

                    stage(0, 0)
                    stage(0, 1)
                    turns(act, body)

                @block.gpsimd
                def _(pool):
                    def body(i, s):
                        g = i * U + s
                        wait(pool, s_add, g - U + 1)
                        pool.wait_ge(s_stage, g + 1)
                        pool.sem_inc(pool_turn, 1)
                        for ins in gather(s, other, F):
                            ins.then_inc(s_g[s], 16)

                    turns(pool, body)

                @block.vector
                def _(dve):
                    epi = Chain(dve, s_epi, 4)

                    def body(i, s):
                        g = i * U + s
                        epi.turn(g)
                        dve.wait_ge(s_g[s], (i + 1) * 16 * T)
                        dve.wait_ge(s_h[s], (i + 1) * 16)
                        nc.vector.tensor_tensor(ey[:, :, :], gb[s][:, :, 0:F], hb[s][:, :, :], ALU.add).then_inc(s_add, 1)
                        dve.wait_ge(s_add, g + 1)
                        last_norm(dve, epi, s_var, s_std, g)
                        nc.vector.tensor_tensor(xd(g), ed[:, :, :], mid(er[:, :], T), ALU.mult).then_inc(s_xd, 1)
                        epi.last()

                    turns(dve, body)
        layer1.close()

        with Scope(nc) as scope:
            xT = slots("xT", [RK, GE], scope=scope)
            hm = [slots(f"hm{b}", [P, GE], n=RC, scope=scope) for b in range(2)]
            mw = slots("mw", [F, GE], n=2, scope=scope)
            nb = slots("nb", [F, GE], scope=scope)
            s_g, s_kb, s_oh, s_nb = ([sem(f"c_{n}{s}") for s in range(U)] for n in ("g", "kb", "oh", "nb"))
            s_x3 = sems("c_x3")
            (s_gap, s_stage, s_cols, s_xT, s_h, s_h1, s_m, s_mw, s_scan, s_rows, s_sum, s_epi, s_xd, s_var, s_std) = (
                scope.sem(f"c_{n}") for n in ("gap", "stage", "cols", "xT", "h", "h1", "m", "mw", "scan", "rows",
                                              "sum", "epi", "xd", "var", "std"))
            with nc.Block() as block:
                @block.sync
                def _(sp):
                    sp.wait_ge(s_gap, 1)

                    def load(i, s):
                        g = i * U + s
                        wait(sp, s_h, RC * (g - U + 1))
                        sp.dma_start(xT[s][RS:RK, :], onehot[:, bass.ds(g * GE, GE)]).then_inc(s_oh[s], 16)
                        wait(sp, s_mw, g - U + 1)
                        sp.dma_start(nb[s][:, :], a["norm_row"][bass.ds(g * GE, GE)].partition_broadcast(F)).then_inc(s_nb[s], 16)
                        wait(sp, s_scan, g - U + 1)
                        sp.dma_start(kb[s][:, :], keep_row(0, g)).then_inc(s_kb[s], 16)

                    def store(i, s):
                        g = i * U + s
                        sp.wait_ge(s_xd, g + 1)
                        sp.dma_start(rows(layer[3], g), XD[:, bass.ds(g * T * F, T * F)]).then_inc(s_x3[s % 2], 16)

                    def body(i, s):
                        load(i, s)
                        if not isinstance(i, int):
                            store(i - 1, s)

                    turns(sp, body)
                    for s in range(U):
                        store(NT - 1, s)
                    for b in range(2):
                        sp.wait_ge(s_x3[b], 16 * NG // 2)

                @block.scalar
                def _(act):
                    def stage(i, s):
                        wait(act, s_g[s], i * 16 * T)
                        nc.scalar.copy(ib[s][:, 0:T], col(idx2, i * U + s)).then_inc(s_stage, 1)

                    def root(g):
                        act.wait_ge(s_var, g + 1)
                        nc.scalar.activation(es[:, :], eu[:, :], ACT.Sqrt, bias=lneps[:, :], scale=1.0 / F).then_inc(s_std, 1)

                    def body(i, s):
                        g, b = i * U + s, s % 2
                        stage(i + (s + 2) // U, (s + 2) % U)
                        act.wait_ge(s_cols, g + 1)
                        wait(act, s_h, RC * (g - U + 1))
                        nc.scalar.copy(xT[s][0:F, :], psT[b][:, :]).then_inc(s_xT, 1)
                        wait(act, s_m, g - 1)
                        for q in range(RC):
                            act.wait_ge(s_h, RC * g + q + 1)
                            nc.scalar.activation(hm[b][q][:, :], psH[q][:, :], ACT.Relu, bias=bias1[:, q:q + 1]).then_inc(s_h1, 1)
                        if not (isinstance(i, int) and s < 2):
                            root(g - 2)

                    act.wait_ge(s_gap, 1)
                    stage(0, 0)
                    stage(0, 1)
                    turns(act, body)
                    root(NG - 2)
                    root(NG - 1)

                @block.gpsimd
                def _(pool):
                    def body(i, s):
                        g = i * U + s
                        wait(pool, s_cols, g - U + 1)
                        pool.wait_ge(s_stage, g + 1)
                        pool.sem_inc(pool_turn, 1)
                        for ins in gather(s, layer[2], F):
                            ins.then_inc(s_g[s], 16)

                    turns(pool, body)

                @block.tensor
                def _(pe):
                    def second(i, s):
                        g = i * U + s
                        pe.wait_ge(s_h1, RC * (g + 1))
                        wait(pe, s_mw, g)
                        pe.sem_inc(pe_turn, 1)
                        for q in range(RC):
                            last = nc.tensor.matmul(psM[0:F, :], w2[:, q, :], hm[s % 2][q][:, :], start=q == 0, stop=q == RC - 1)
                        last.then_inc(s_m, 1)

                    def sums(i, s):
                        g = i * U + s
                        pe.wait_ge(s_scan, g + 1)
                        wait(pe, s_sum, g - 1)
                        pe.sem_inc(pe_turn, 1)
                        to_rows(psR[s % 2], scan[s % 2]).then_inc(s_rows, 1)

                    def body(i, s):
                        g = i * U + s
                        pe.wait_ge(s_g[s], (i + 1) * 16 * T)
                        wait(pe, s_xT, g - 1)
                        pe.sem_inc(pe_turn, 1)
                        to_columns(psT[s % 2], gb[s]).then_inc(s_cols, 1)
                        if not (isinstance(i, int) and s < 1):
                            second(*back(i, s, 1))
                        if not (isinstance(i, int) and s < 2):
                            sums(*back(i, s, 2))
                        pe.wait_ge(s_xT, g + 1)
                        pe.wait_ge(s_oh[s], (i + 1) * 16)
                        pe.sem_inc(pe_turn, 1)
                        for q in range(RC):
                            wait(pe, s_h1, RC * (g - 1) + q + 1)
                            nc.tensor.matmul(psH[q][:, :], w1[:, q * P:(q + 1) * P], xT[s][:, :], start=True, stop=True).then_inc(s_h, 1)

                    turns(pe, body)
                    second(NT - 1, U - 1)
                    sums(NT - 1, U - 2)
                    sums(NT - 1, U - 1)

                @block.vector
                def _(dve):
                    epi = Chain(dve, s_epi, 5)
                    for x in xT:
                        last = nc.vector.memset(x[32:RS, :], 0.0)
                    last.then_inc(s_gap, 1)

                    def epilogue(i, s):
                        g = i * U + s
                        epi.turn(g)
                        dve.wait_ge(s_rows, g + 1)
                        nc.vector.tensor_tensor(ey[:, :, :], psR[s % 2][:, :, :], bias2[:, :].unsqueeze(1).to_broadcast([P, T, F]), ALU.add).then_inc(s_sum, 1)
                        dve.wait_ge(s_sum, g + 1)
                        epi.then(nc.vector.scalar_tensor_tensor(out=ey[:, :, :], in0=ey[:, :, :], scalar=0.0, in1=xd(g), op0=ALU.max, op1=ALU.add))
                        last_norm(dve, epi, s_var, s_std, g)
                        nc.vector.tensor_tensor(xd(g), ed[:, :, :], mid(er[:, :], T), ALU.mult).then_inc(s_xd, 1)
                        epi.last()

                    def weigh(i, s):
                        g, b = i * U + s, s % 2
                        dve.wait_ge(s_m, g + 1)
                        dve.wait_ge(s_nb[s], (i + 1) * 16)
                        wait(dve, s_scan, g - 1)
                        nc.vector.tensor_tensor(mw[b][:, :], psM[0:F, :], nb[s][:, :], ALU.mult).then_inc(s_mw, 1)

                    def add_up(i, s):
                        g, b = i * U + s, s % 2
                        first = isinstance(i, int) and g == 0
                        dve.wait_ge(s_mw, g + 1)
                        dve.wait_ge(s_kb[s], (i + 1) * 16)
                        wait(dve, s_rows, g - 1)
                        wait(dve, s_scan, g)
                        start = 0.0 if first else scan[1 - b][:, GE - 1:GE]
                        nc.vector.tensor_tensor_scan(scan[b][:, :], kb[s][:, :], mw[b][:, :], start, ALU.mult, ALU.add).then_inc(s_scan, 1)

                    def body(i, s):
                        if not (isinstance(i, int) and s < 1):
                            weigh(*back(i, s, 1))
                            add_up(*back(i, s, 1))
                        if not (isinstance(i, int) and s < 2):
                            epilogue(*back(i, s, 2))

                    turns(dve, body)
                    weigh(NT - 1, U - 1)
                    add_up(NT - 1, U - 1)
                    epilogue(NT - 1, U - 2)
                    epilogue(NT - 1, U - 1)

        with Scope(nc) as scope:
            dT, xT = slots("dT", [F, GE], n=2, scope=scope), slots("xT3", [F, GE], n=2, scope=scope)
            xdb, xo = (slots(n, [P, T, F], scope=scope) for n in ("xdb3", "xo"))
            ob = slots("ob", [P, T], I32, scope=scope)
            psD = psH[0][0:F, :]
            s_g, s_kb, s_o = ([sem(f"d_{n}{s}") for s in range(U)] for n in ("g", "kb", "o"))
            (s_stage, s_own, s_cols, s_dcols, s_xT, s_dT, s_e, s_scan, s_rows, s_sum, s_epi, s_xo, s_var, s_std,
             s_obs) = (scope.sem(f"d_{n}") for n in ("stage", "own", "cols", "dcols", "xT", "dT", "e", "scan", "rows", "sum",
                                               "epi", "xo", "var", "std", "obs"))
            with nc.Block() as block:
                @block.sync
                def _(sp):
                    def load(i, s):
                        g = i * U + s
                        wait(sp, s_scan, g - U + 1)
                        sp.dma_start(kb[s][:, :], keep_row(1, g)).then_inc(s_kb[s], 16)

                    turns(sp, load)

                @block.scalar
                def _(act):
                    def stage(i, s):
                        wait(act, s_g[s], i * 16 * T)
                        nc.scalar.copy(ib[s][:, 0:T], col(idx2, i * U + s)).then_inc(s_stage, 1)

                    def root(g):
                        act.wait_ge(s_var, g + 1)
                        nc.scalar.activation(es[:, :], eu[:, :], ACT.Sqrt, bias=lneps[:, :], scale=1.0 / F).then_inc(s_std, 1)

                    def body(i, s):
                        g, b = i * U + s, s % 2
                        stage(i + (s + 2) // U, (s + 2) % U)
                        own(i, s)
                        act.wait_ge(s_cols, g + 1)
                        wait(act, s_e, g - 1)
                        nc.scalar.copy(xT[b][:, :], psT[b][:, :]).then_inc(s_xT, 1)
                        act.wait_ge(s_dcols, g + 1)
                        wait(act, s_rows, g - 1)
                        nc.scalar.copy(dT[b][:, :], psD).then_inc(s_dT, 1)
                        if not (isinstance(i, int) and s < 2):
                            number(*back(i, s, 2))
                            root(g - 2)

                    def own(i, s):
                        wait(act, s_dcols, i * U + s - U + 1)
                        wait(act, s_sum, i * U + s - U + 1)
                        nc.scalar.copy(xdb[s][:, :, :], xd(i * U + s)).then_inc(s_own, 1)

                    def number(i, s):
                        wait(act, s_o[s], i * 16 * T)
                        nc.scalar.copy(ob[s][:, :], col(outi, i * U + s)).then_inc(s_obs, 1)

                    stage(0, 0)
                    stage(0, 1)
                    turns(act, body)
                    for s in range(U - 2, U):
                        number(NT - 1, s)
                        root((NT - 1) * U + s)

                @block.gpsimd
                def _(pool):
                    bound = pool.to_reg(N - 1)

                    def fetch(i, s):
                        g = i * U + s
                        wait(pool, s_cols, g - U + 1)
                        pool.wait_ge(s_stage, g + 1)
                        pool.sem_inc(pool_turn, 1)
                        for ins in gather(s, layer[3], F):
                            ins.then_inc(s_g[s], 16)

                    def scatter(i, s):
                        g = i * U + s
                        pool.wait_ge(s_xo, g + 1)
                        pool.wait_ge(s_obs, g + 1)
                        pool.sem_inc(pool_turn, 1)
                        for t in range(T):
                            nc.gpsimd.indirect_dma_start(
                                out=out, out_offset=bass.IndirectOffsetOnAxis(ap=ob[s][:, t:t + 1], axis=0),
                                in_=xo[s][:, t, :], in_offset=None, bounds_check=bound, oob_is_err=False).then_inc(s_o[s], 16)

                    def body(i, s):
                        fetch(i, s)
                        if not isinstance(i, int):
                            scatter(i - 1, s)

                    turns(pool, body)
                    for s in range(U):
                        scatter(NT - 1, s)
                    for s in range(U):
                        pool.wait_ge(s_o[s], NT * 16 * T)

                @block.tensor
                def _(pe):
                    def total(i, s):
                        g, b = i * U + s, s % 2
                        pe.wait_ge(s_dT, g + 1)
                        pe.wait_ge(s_scan, g + 1)
                        wait(pe, s_sum, g - 1)
                        pe.sem_inc(pe_turn, 1)
                        for t in range(T):
                            nc.tensor.matmul(psR[b][:, t, :], slot(scan[b], t), ident[0:F, 0:F], start=True, stop=False)
                            last = nc.tensor.matmul(psR[b][:, t, :], slot(dT[b], t), theta[:, :], start=False, stop=True)
                        last.then_inc(s_rows, 1)

                    def body(i, s):
                        g, b = i * U + s, s % 2
                        pe.wait_ge(s_own, g + 1)
                        wait(pe, s_dT, g)
                        pe.sem_inc(pe_turn, 1)
                        to_columns(psD, xdb[s]).then_inc(s_dcols, 1)
                        pe.wait_ge(s_g[s], (i + 1) * 16 * T)
                        wait(pe, s_xT, g - 1)
                        pe.sem_inc(pe_turn, 1)
                        to_columns(psT[b], gb[s]).then_inc(s_cols, 1)
                        if not (isinstance(i, int) and s < 1):
                            total(*back(i, s, 1))
                        pe.wait_ge(s_xT, g + 1)
                        wait(pe, s_scan, g)
                        pe.sem_inc(pe_turn, 1)
                        nc.tensor.matmul(psM[0:F, :], pmt[:, :], xT[b][:, :], start=True, stop=True).then_inc(s_e, 1)

                    turns(pe, body)
                    total(NT - 1, U - 1)

                @block.vector
                def _(dve):
                    epi = Chain(dve, s_epi, 5)

                    def epilogue(i, s):
                        g = i * U + s
                        epi.turn(g)
                        dve.wait_ge(s_rows, g + 1)
                        epi.then(nc.vector.tensor_tensor(ey[:, :, :], psR[s % 2][:, :, :], bias3[:, :].unsqueeze(1).to_broadcast([P, T, F]), ALU.add))
                        nc.vector.tensor_tensor(ey[:, :, :], ey[:, :, :], xdb[s][:, :, :], ALU.add).then_inc(s_sum, 1)
                        dve.wait_ge(s_sum, g + 1)
                        last_norm(dve, epi, s_var, s_std, g)
                        wait(dve, s_o[s], i * 16 * T)
                        nc.vector.tensor_tensor(xo[s][:, :, :], ed[:, :, :], mid(er[:, :], T), ALU.mult).then_inc(s_xo, 1)
                        epi.last()

                    def body(i, s):
                        g, b = i * U + s, s % 2
                        first = isinstance(i, int) and s < 1
                        if not (isinstance(i, int) and s < 2):
                            epilogue(*back(i, s, 2))
                        dve.wait_ge(s_e, g + 1)
                        dve.wait_ge(s_kb[s], (i + 1) * 16)
                        wait(dve, s_rows, g - 1)
                        wait(dve, s_scan, g)
                        start = 0.0 if first else scan[1 - b][:, GE - 1:GE]
                        nc.vector.tensor_tensor_scan(scan[b][:, :], kb[s][:, :], psM[0:F, :], start, ALU.add, ALU.max).then_inc(s_scan, 1)

                    turns(dve, body)
                    epilogue(NT - 1, U - 2)
                    epilogue(NT - 1, U - 1)


def kernel(**inputs):
    import numpy as np
    import concourse.bacc as bacc
    from concourse.bass_utils import run_bass_kernel_spmd

    given = {k: np.ascontiguousarray(np.asarray(v)) for k, v in inputs.items()}

    def padded(v, n, fill):
        return np.concatenate([v, np.full((n - v.shape[0],) + v.shape[1:], fill, v.dtype)])

    def columns(v, fill):
        return np.ascontiguousarray(padded(v, NC * P, fill).reshape(NG + 2, P, T).transpose(1, 0, 2).reshape(P, NC))

    dst = given["dst"]
    arrays = {
        "x": given["x"],
        "src": columns(given["src"], 0),
        "dst": columns(dst, N),
        "nxt": columns(padded(dst[1:], E, N), N),
        "dst_row": np.concatenate([np.full(1, -1, dst.dtype), padded(dst, EP, N)]),
        "ew": columns(given["edge_weight"], 0),
        "edge": np.ascontiguousarray(padded(given["edge_attr_48"], EP, 0).reshape(NG, P, T * F).transpose(1, 0, 2).reshape(P, NG * T * F)),
        "type_row": padded(given["edge_type_8"], EP, 0),
        "norm_row": padded(given["edge_weight1"].reshape(E), EP, 0),
        "eps": given["L0_gnn_eps"],
        "w1": np.ascontiguousarray(given["L2_gnn_weight1"].transpose(1, 0, 2).reshape(F, R * F)),
        "w2": np.ascontiguousarray(given["L2_gnn_weight2"].reshape(RC, P, F).transpose(1, 0, 2)),
        "bias1": np.ascontiguousarray(np.tile(given["L2_gnn_bias1"], R).reshape(RC, P).T),
        "bias2": given["L2_gnn_bias2"],
        "thetaT": np.ascontiguousarray(given["L3_gnn_theta_w"].T),
        "phiT": np.ascontiguousarray(given["L3_gnn_phi_w"].T),
        "theta_b": given["L3_gnn_theta_b"],
        "phi_b": given["L3_gnn_phi_b"],
        "ident": np.eye(P, dtype=np.float32),
        "apart": np.where(np.arange(R * F)[None, :] // F == np.arange(R)[:, None], 0, -APART).astype(np.float32),
    }
    nc = bacc.Bacc("TRN2", target_bir_lowering=False, num_devices=1)
    aps = {k: nc.dram_tensor(f"in_{k}", v.shape, mybir.dt.from_np(v.dtype), kind="ExternalInput").ap() for k, v in arrays.items()}
    out = nc.dram_tensor("out", (N, F), F32, kind="ExternalOutput").ap()
    gnn(nc, aps, out)
    r = run_bass_kernel_spmd(nc, [{f"in_{k}": v for k, v in arrays.items()}], core_ids=[0])
    return r.results[0]["out"]
```
